# Optimizing a Trainium2 kernel written in Bass

```python
import numpy as np
import jax
import jax.numpy as jnp

def _softmax(x, axis=-1):
    return jax.nn.softmax(x, axis=axis)

def _gelu(x):
    return jax.nn.gelu(x, approximate=True)

def _silu(x):
    return jax.nn.silu(x)

def _sigmoid(x):
    return jax.nn.sigmoid(x)

def _layernorm(x, axis=-1, eps=1e-05):
    m = jnp.mean(x, axis=axis, keepdims=True)
    v = jnp.var(x, axis=axis, keepdims=True)
    return (x - m) / jnp.sqrt(v + eps)

def _scatter_add(tgt, idx, src, axis=0):
    return tgt.at[idx].add(src)

def _segment_sum(src, seg, n):
    return jax.ops.segment_sum(src, seg, n)
kernel_name = 'mk_seq_preln_d2_jaxref_r8_4b1d4a'

def setup_inputs(seed: int=0):
    np.random.seed(seed)
    _w = jnp.asarray

    def _L0_attn_setup():
        import jax, jax.numpy as jnp
        import numpy as np
        EMB_DIM = 128
        QUERY_DIM = 128
        CTX = 256
        BATCH = 8
        key = jax.random.key(seed)
        ks = jax.random.split(key, 7)
        s = 1.0 / np.sqrt(EMB_DIM)
        return {'x': jax.random.normal(ks[0], (BATCH, CTX, EMB_DIM), dtype=jnp.float32), 'Qw': jax.random.uniform(ks[1], (EMB_DIM, QUERY_DIM), jnp.float32, -s, s), 'Qb': jax.random.uniform(ks[2], (QUERY_DIM,), jnp.float32, -s, s), 'Kw': jax.random.uniform(ks[3], (EMB_DIM, QUERY_DIM), jnp.float32, -s, s), 'Kb': jax.random.uniform(ks[4], (QUERY_DIM,), jnp.float32, -s, s), 'Vw': jax.random.uniform(ks[5], (EMB_DIM, QUERY_DIM), jnp.float32, -s, s), 'Vb': jax.random.uniform(ks[6], (QUERY_DIM,), jnp.float32, -s, s)}
    _L0_attn_in = _L0_attn_setup()

    def _L0_ffn_setup():
        import jax, jax.numpy as jnp
        import numpy as np
        NUM_EXPERTS_TOTAL = 9
        TOP_K = 2
        key = jax.random.key(seed)
        k0, k1, k2, k3, k4 = jax.random.split(key, 5)
        B, S, H, I = (2, 256, 128, 352)
        E = NUM_EXPERTS_TOTAL
        x = jax.random.normal(k0, (B, S, H), dtype=jnp.float32)
        Wr = jax.random.normal(k1, (H, E), dtype=jnp.float32) * 0.02
        Wg = jax.random.normal(k2, (E, H, I), dtype=jnp.float32) * 0.02
        Wu = jax.random.normal(k3, (E, H, I), dtype=jnp.float32) * 0.02
        Wd = jax.random.normal(k4, (E, I, H), dtype=jnp.float32) * 0.02
        return {'x': x, 'Wr': Wr, 'Wg': Wg, 'Wu': Wu, 'Wd': Wd}
    _L0_ffn_in = _L0_ffn_setup()

    def _L1_attn_setup():
        import jax, jax.numpy as jnp
        import numpy as np
        import math
        N_HEAD = 16
        N_LATENTS = 64
        CHUNK = 128
        ROPE_THETA = 10000.0

        def _rope_cos_sin(T, D, theta):
            inv = 1.0 / theta ** (jnp.arange(0, D, 2, dtype=jnp.float32) / D)
            ang = jnp.arange(T, dtype=jnp.float32)[:, None] * inv[None, :]
            return (jnp.cos(ang), jnp.sin(ang))

        def _apply_rope(k, cos, sin):
            B, T, H, D = k.shape
            kr = k.reshape(B, T, H, D // 2, 2)
            a, b = (kr[..., 0], kr[..., 1])
            c = cos[None, :, None, :]
            s = sin[None, :, None, :]
            out = jnp.stack([a * c - b * s, a * s + b * c], axis=-1)
            return out.reshape(B, T, H, D).astype(k.dtype)
        key = jax.random.key(seed)
        ks = jax.random.split(key, 6)
        B, T, C = (8, 512, 128)
        H, L = (N_HEAD, N_LATENTS)
        D = C // H
        std_in = 1.0 / math.sqrt(C)
        return {'x': jax.random.normal(ks[0], (B, T, C), jnp.float32), 'latent_queries': jax.random.normal(ks[1], (1, L, H, D), jnp.float32) * (1.0 / math.sqrt(D)), 'W_k': jax.random.normal(ks[2], (C, C), jnp.float32) * std_in, 'W_v': jax.random.normal(ks[3], (C, C), jnp.float32) * std_in, 'W_g': jax.random.normal(ks[4], (H * L, C), jnp.float32) * std_in, 'W_p': jax.random.normal(ks[5], (C, C), jnp.float32) * std_in}
    _L1_attn_in = _L1_attn_setup()

    def _L1_ffn_setup():
        import jax, jax.numpy as jnp
        import numpy as np
        D_MODEL = 128
        D_HIDDEN = 512
        NUM_EXPERTS = 8
        B, T = (2, 256)
        key = jax.random.key(seed)
        ks = jax.random.split(key, 8)
        s = 0.02
        x = jax.random.normal(ks[0], (B, T, D_MODEL), dtype=jnp.float32)
        Wg = jax.random.normal(ks[1], (D_MODEL, NUM_EXPERTS), dtype=jnp.float32) * s
        bg = jnp.zeros((NUM_EXPERTS,), dtype=jnp.float32)
        W1 = jax.random.normal(ks[2], (NUM_EXPERTS, D_MODEL, D_HIDDEN), dtype=jnp.float32) * s
        b1 = jnp.zeros((NUM_EXPERTS, D_HIDDEN), dtype=jnp.float32)
        W2 = jax.random.normal(ks[3], (NUM_EXPERTS, D_HIDDEN, D_MODEL), dtype=jnp.float32) * s
        b2 = jnp.zeros((NUM_EXPERTS, D_MODEL), dtype=jnp.float32)
        return {'x': x, 'Wg': Wg, 'bg': bg, 'W1': W1, 'b1': b1, 'W2': W2, 'b2': b2}
    _L1_ffn_in = _L1_ffn_setup()
    _d = {'L0_attn_x': _L0_attn_in['x'], 'L0_attn_Qw': _L0_attn_in['Qw'], 'L0_attn_Qb': _L0_attn_in['Qb'], 'L0_attn_Kw': _L0_attn_in['Kw'], 'L0_attn_Kb': _L0_attn_in['Kb'], 'L0_attn_Vw': _L0_attn_in['Vw'], 'L0_attn_Vb': _L0_attn_in['Vb'], 'L0_ffn_Wr': _L0_ffn_in['Wr'], 'L0_ffn_Wg': _L0_ffn_in['Wg'], 'L0_ffn_Wu': _L0_ffn_in['Wu'], 'L0_ffn_Wd': _L0_ffn_in['Wd'], 'L1_attn_latent_queries': _L1_attn_in['latent_queries'], 'L1_attn_W_k': _L1_attn_in['W_k'], 'L1_attn_W_v': _L1_attn_in['W_v'], 'L1_attn_W_g': _L1_attn_in['W_g'], 'L1_attn_W_p': _L1_attn_in['W_p'], 'L1_ffn_Wg': _L1_ffn_in['Wg'], 'L1_ffn_bg': _L1_ffn_in['bg'], 'L1_ffn_W1': _L1_ffn_in['W1'], 'L1_ffn_b1': _L1_ffn_in['b1'], 'L1_ffn_W2': _L1_ffn_in['W2'], 'L1_ffn_b2': _L1_ffn_in['b2']}
    _x0 = _d['L0_attn_x']
    _d['L0_attn_x'] = jax.random.normal(jax.random.fold_in(jax.random.key(seed), 1), (8, 512, 128), dtype=_x0.dtype)
    del _x0
    return _d

def reference(L0_attn_x, L0_attn_Qw, L0_attn_Qb, L0_attn_Kw, L0_attn_Kb, L0_attn_Vw, L0_attn_Vb, L0_ffn_Wr, L0_ffn_Wg, L0_ffn_Wu, L0_ffn_Wd, L1_attn_latent_queries, L1_attn_W_k, L1_attn_W_v, L1_attn_W_g, L1_attn_W_p, L1_ffn_Wg, L1_ffn_bg, L1_ffn_W1, L1_ffn_b1, L1_ffn_W2, L1_ffn_b2):

    def _L0_attn_ref(x, Qw, Qb, Kw, Kb, Vw, Vb):
        import jax, jax.numpy as jnp
        import numpy as np
        EMB_DIM = 128
        QUERY_DIM = 128
        CTX = 256
        BATCH = 8
        B, C, E = x.shape
        q = x @ Qw + Qb
        k = x @ Kw + Kb
        v = x @ Vw + Vb
        scale = QUERY_DIM ** (-0.5)
        scores = jnp.einsum('bcd,bkd->bck', q, k) * scale
        causal = jnp.tril(jnp.ones((C, C), dtype=bool))
        scores = jnp.where(causal, scores, -jnp.inf)
        weights = jax.nn.softmax(scores, axis=-1)
        return jnp.einsum('bck,bkd->bcd', weights, v)

    def _L0_ffn_ref(x, Wr, Wg, Wu, Wd):
        import jax, jax.numpy as jnp
        import numpy as np
        NUM_EXPERTS_TOTAL = 9
        TOP_K = 2
        B, S, H = x.shape
        E = NUM_EXPERTS_TOTAL
        T = B * S
        logits = jnp.einsum('bsh,he->bse', x, Wr)
        probs = jax.nn.softmax(logits, axis=-1)
        topk_w, topk_idx = jax.lax.top_k(probs, TOP_K)
        topk_w = topk_w / jnp.sum(topk_w, axis=-1, keepdims=True)
        xf = x.reshape(T, H)
        wf = topk_w.reshape(T, TOP_K)
        idxf = topk_idx.reshape(T, TOP_K)
        cw = jnp.zeros((T, E), dtype=x.dtype).at[jnp.arange(T)[:, None], idxf].add(wf)
        gate = jax.nn.silu(jnp.einsum('th,ehi->tei', xf, Wg))
        hidden = gate * jnp.einsum('th,ehi->tei', xf, Wu)
        out = jnp.einsum('tei,eih,te->th', hidden, Wd, cw)
        return out.reshape(B, S, H)

    def _L1_attn_ref(x, latent_queries, W_k, W_v, W_g, W_p):
        import jax, jax.numpy as jnp
        import numpy as np
        import math
        N_HEAD = 16
        N_LATENTS = 64
        CHUNK = 128
        ROPE_THETA = 10000.0

        def _rope_cos_sin(T, D, theta):
            inv = 1.0 / theta ** (jnp.arange(0, D, 2, dtype=jnp.float32) / D)
            ang = jnp.arange(T, dtype=jnp.float32)[:, None] * inv[None, :]
            return (jnp.cos(ang), jnp.sin(ang))

        def _apply_rope(k, cos, sin):
            B, T, H, D = k.shape
            kr = k.reshape(B, T, H, D // 2, 2)
            a, b = (kr[..., 0], kr[..., 1])
            c = cos[None, :, None, :]
            s = sin[None, :, None, :]
            out = jnp.stack([a * c - b * s, a * s + b * c], axis=-1)
            return out.reshape(B, T, H, D).astype(k.dtype)
        B, T, C = x.shape
        H, L, cs = (N_HEAD, N_LATENTS, CHUNK)
        D = C // H
        scale = 1.0 / math.sqrt(D)
        k = (x @ W_k.T).reshape(B, T, H, D)
        v = (x @ W_v.T).reshape(B, T, H, D)
        cos, sin = _rope_cos_sin(T, D, ROPE_THETA)
        k = _apply_rope(k, cos, sin)
        gates = jax.nn.softmax((x @ W_g.T).reshape(B, T, H, L) * scale, axis=-1)
        q = jnp.transpose(latent_queries, (0, 2, 1, 3))
        nc = T // cs
        kc = jnp.transpose(k, (0, 2, 1, 3)).reshape(B, H, nc, cs, D)
        vc = jnp.transpose(v, (0, 2, 1, 3)).reshape(B, H, nc, cs, D)
        scores = jnp.einsum('zhld,bhncd->bhnlc', q, kc) * scale
        causal = jnp.arange(cs)[None, :] <= jnp.arange(L)[:, None]
        scores = jnp.where(causal[None, None, None], scores, -jnp.inf)
        probs = jax.nn.softmax(scores, axis=-1)
        attn = jnp.einsum('bhnlc,bhncd->bhld', probs, vc)
        weighted = jnp.einsum('bhld,bthl->bthd', attn, gates)
        out = weighted.reshape(B, T, C) @ W_p.T
        return out

    def _L1_ffn_ref(x, Wg, bg, W1, b1, W2, b2):
        import jax, jax.numpy as jnp
        import numpy as np
        D_MODEL = 128
        D_HIDDEN = 512
        NUM_EXPERTS = 8
        B, T = (2, 256)
        gate_logits = jnp.einsum('btd,de->bte', x, Wg) + bg
        gate_scores = jax.nn.softmax(gate_logits, axis=-1)
        top1_idx = jnp.argmax(gate_scores, axis=-1)
        top1_mask = jax.nn.one_hot(top1_idx, NUM_EXPERTS, dtype=x.dtype)
        top1_weight = jnp.sum(gate_scores * top1_mask, axis=-1, keepdims=True)
        h = jax.nn.silu(jnp.einsum('btd,edh->bteh', x, W1) + b1)
        o = jnp.einsum('bteh,ehd->bted', h, W2) + b2
        y = jnp.sum(o * top1_mask[..., None], axis=2) * top1_weight
        return y
    x = L0_attn_x
    x = x + _L0_attn_ref(_layernorm(x, axis=-1), L0_attn_Qw, L0_attn_Qb, L0_attn_Kw, L0_attn_Kb, L0_attn_Vw, L0_attn_Vb)
    x = x + _L0_ffn_ref(_layernorm(x, axis=-1), L0_ffn_Wr, L0_ffn_Wg, L0_ffn_Wu, L0_ffn_Wd)
    x = x + _L1_attn_ref(_layernorm(x, axis=-1), L1_attn_latent_queries, L1_attn_W_k, L1_attn_W_v, L1_attn_W_g, L1_attn_W_p)
    x = x + _L1_ffn_ref(_layernorm(x, axis=-1), L1_ffn_Wg, L1_ffn_bg, L1_ffn_W1, L1_ffn_b1, L1_ffn_W2, L1_ffn_b2)
    return x

_drawn_inputs = setup_inputs


def setup_inputs(seed=0):
    import zlib

    import numpy as np

    out = dict(_drawn_inputs(seed))
    spreads = {'L1_ffn_bg': (0.0, 0.564), 'L1_ffn_b1': (0.0, 0.8), 'L1_ffn_b2': (0.0, 0.488)}
    factors = {'L0_attn_Qb': 7.064,
     'L0_attn_Kb': 8.0,
     'L0_ffn_Wr': 8.0,
     'L0_ffn_Wg': 8.0,
     'L0_ffn_Wu': 8.0,
     'L0_ffn_Wd': 8.0,
     'L1_attn_latent_queries': 3.011,
     'L1_attn_W_k': 2.781,
     'L1_attn_W_g': 2.932,
     'L1_ffn_Wg': 3.186,
     'L1_ffn_W1': 6.856,
     'L1_ffn_W2': 6.198}
    for name, (base, spread) in spreads.items():
        noise = np.random.default_rng([zlib.crc32(name.encode()), seed]).standard_normal(out[name].shape)
        drawn = base * np.exp(spread * noise) if base else spread * noise
        out[name] = jnp.asarray(drawn.astype(out[name].dtype))
    for name, factor in factors.items():
        out[name] = (out[name] * factor).astype(out[name].dtype)
    return out
```

```python
from contextlib import ExitStack

import concourse.bass as bass
from concourse import mybir

F32 = mybir.dt.float32
BF16 = mybir.dt.bfloat16
I32 = mybir.dt.int32
U32 = mybir.dt.uint32
ALU = mybir.AluOpType
ACT = mybir.ActivationFunctionType
X = mybir.AxisListType.X

P = 128
B, T, C = 8, 512, 128
TILES = B * T // P
Q = T // P
GROUPS = 2
BG = B // GROUPS
TG = BG * Q
EPS = 1e-5
NEG = -1e30
RSQRT_GUESS = 1597463007.0
NEWTON = 3
LN_STEPS = 5 + 3 * NEWTON
SCALE0 = float(C) ** -0.5

E0, I0, K0 = 9, 352, 2
E1, I1, K1 = 8, 512, 1
HC0, HC1 = -(-I0 // P), I1 // P
CH = 4


def slot_tiles(experts, k):
    rows = k * TG * P
    most = (rows - experts) // P + experts
    return -(-most // CH) * CH


ST0, ST1 = slot_tiles(E0, K0), slot_tiles(E1, K1)
ST = max(ST0, ST1)

H, L = 16, 64
D = C // H
HP = H // 2
KC = 64
SCALE1 = float(D) ** -0.5
VW = 2 * D + 1
GW = 2 * D + 2

COLS, _at = {}, 0
for _name, _n in (("ident", P), ("cos", Q * KC), ("sin", Q * KC), ("headmask", H), ("iota_e", 16),
                  ("iota_j", ST), ("below", 81), ("ones", P), ("before", P), ("causal", P),
                  ("latmask", KC), ("pairones", 2)):
    COLS[_name] = (_at, _at + _n)
    _at += _n
NCONST = _at
LAST_STAGE = 4


def after(engine, semaphore, n):
    if not (isinstance(n, int) and n < 1):
        engine.wait_ge(semaphore, n)


def build(nc, a, out):
    ctx = ExitStack()
    with ctx:
        def sb(name, shape, dt=F32):
            return ctx.enter_context(nc.sbuf_tensor(name, shape, dt))

        def ps(name, shape, dt=F32):
            return ctx.enter_context(nc.psum_tensor(name, shape, dt))

        def sem(name):
            return ctx.enter_context(nc.semaphore(name))

        x = sb("x", [P, TILES, C])
        rows = sb("rows", [P, TILES, C])
        const = sb("const", [P, NCONST])

        def cst(name):
            return const[:, COLS[name][0]:COLS[name][1]]

        ident = cst("ident")
        cbf = sb("cbf", [P, 4 * P + KC], BF16)
        ident_bf, ones_bf, before_bf, causal_bf = (cbf[:, n * P:(n + 1) * P] for n in range(4))
        latmask_bf = cbf[:, 4 * P:4 * P + KC]
        qkvw = sb("qkvw", [P, 3, C])
        qkb = sb("qkb", [P, 2])
        vb = sb("vb", [P, C])
        work = sb("work", [P, 8 * T])
        xnT, qT, kT, v = (work[:, n * T:(n + 1) * T] for n in range(4))
        xn2 = sb("xn2", [P, Q, C])
        scratch = sb("scratch", [P, 1])
        xn = sb("xn", [P, Q, C])
        bn = sb("bn", [P, Q, 6])
        mv = sb("mv", [P, Q, 2])
        rstd = sb("rstd", [P, 4, Q])
        bn2 = sb("bn2", [P, Q, 6])
        mv2 = sb("mv2", [P, Q, 2])
        rstd2 = sb("rstd2", [P, 4, Q])
        prob = work[:, 4 * T:6 * T].rearrange("p (n t) -> p n t", n=2)
        probT = work[:, 6 * T:8 * T].rearrange("p (n t) -> p n t", n=2)
        mx = sb("mx", [P, Q])
        nmx = sb("nmx", [P, Q])
        rsum = sb("rsum", [P, Q])
        rinv = sb("rinv", [P, Q])
        x2T = sb("x2T", [P, T])
        wr = sb("wr", [P, E0])
        logits = sb("logits", [P, TILES, E0])
        wr1 = sb("wr1", [P, E1])
        br1 = sb("br1", [P, E1])
        logits1 = sb("logits1", [P, TILES, E1])
        wk1 = sb("wk1", [P, 2, C])
        wv1 = sb("wv1", [P, C])
        wg1 = sb("wg1", [P, H * L])
        wp1 = sb("wp1", [P, C])
        lat = sb("lat", [P, L])
        latbd = sb("latbd", [P, H, L])
        xT1 = work[:, 5 * 512:6 * 512]
        xkT = work[:, 7 * 512:7 * 512 + Q * KC]
        turned = work[:, 6 * 512:7 * 512].rearrange("p (n k) -> p n k", n=2)
        kT1 = sb("kT1", [P, Q * KC])
        vbd = sb("vbd", [P, 2, HP, 2, VW])
        ex = work[:, 0:3 * 512].rearrange("p (n t) -> p n t", n=3)
        exT = work[:, 3 * 512:5 * 512].rearrange("p (n t) -> p n t", n=2)
        umax = sb("umax", [P, 3, 8])
        chunk_inv = sb("chunk_inv", [P, 2, Q])
        chunk_out = sb("chunk_out", [P, 2, Q, 2 * D])
        attbd = sb("attbd", [P, HP, GW])
        gate_inv = sb("gate_inv", [P, HP, 2])
        mixed = sb("mixed", [P, HP, 2, D])
        mixedT = sb("mixedT", [P, P])

        below = cst("below").rearrange("p (e f) -> p e f", e=E0)
        rt_ge = sb("rt_ge", [P, TG, E0])
        rt_cand = sb("rt_cand", [P, TG, E0])
        rt_second = sb("rt_second", [P, TG, E0])
        rt_sel = sb("rt_sel", [P, K0, TG, E0])
        rt_selbf = sb("rt_selbf", [P, TG, E0], BF16)
        rt_pos = sb("rt_pos", [P, TG, E0])
        rt_prod = sb("rt_prod", [P, TG, E0])
        rt_max = sb("rt_max", [P, 3, TG])
        rt_gap = sb("rt_gap", [P, TG, E0])
        rt_den = sb("rt_den", [P, TG])
        rt_tiles = sb("rt_tiles", [P, E0], I32)
        rt_base = sb("rt_base", [P, E0])
        rt_end = sb("rt_end", [P, E0])
        rt_below = sb("rt_below", [P, E0, E0])
        rt_past = sb("rt_past", [P, ST, E0])
        rt_tile_e = sb("rt_tile_e", [P, ST])
        rt_posf = sb("rt_posf", [P, K0 * TG])
        rt_int = sb("rt_int", [P, 4, K0 * TG], I32)
        slot = [[sb(f"slot{n}{g}", [P, k, TG], U32) for g in range(GROUPS)] for n, k in ((0, K0), (1, K1))]
        weight = [[sb(f"weight{n}{g}", [P, k, TG]) for g in range(GROUPS)] for n, k in ((0, K0), (1, K1))]
        tile_e = [[sb(f"tile_e{n}{g}", [P, ST], I32) for g in range(GROUPS)] for n in (0, 1)]
        expert_w = sb("expert_w", [P, E0 * (2 * I0 + HC0 * C)])
        wgu = expert_w[:, 0:E0 * 2 * I0].rearrange("p (e n) -> p e n", e=E0)
        wd = expert_w[:, E0 * 2 * I0:].rearrange("p (e j c) -> p e j c", e=E0, j=HC0)
        w1 = expert_w[:, 0:E1 * I1].rearrange("p (e n) -> p e n", e=E1)
        w2 = expert_w[:, E1 * I1:2 * E1 * I1].rearrange("p (e j c) -> p e j c", e=E1, j=HC1)
        b1 = sb("b1", [P, E1, I1])
        b2 = sb("b2", [P, E1, C])
        zeros = sb("zeros", [P, CH * C])
        xs = sb("xs", [P, CH, C])
        xsT = sb("xsT", [P, CH * P])
        act_out = sb("act_out", [P, 2, 512])
        hid = sb("hid", [P, 2, 512])
        hidT = sb("hidT", [P, 2, 512])
        ysb = sb("ysb", [P, ST, C])
        fetched = sb("fetched", [P, TILES, C])
        back = [rows, fetched]

        xs_dram = [nc.dram_tensor(f"xs_dram{g}", (ST * P, C), F32, kind="Internal").ap() for g in range(GROUPS)]
        ys_dram = [nc.dram_tensor(f"ys_dram{g}", (ST * P, C), F32, kind="Internal").ap() for g in range(GROUPS)]
        xs_chunk = [t.rearrange("(c p t) h -> p c (t h)", p=P, t=CH) for t in xs_dram]
        ys_chunk = [t.rearrange("(c p t) h -> p c (t h)", p=P, t=CH) for t in ys_dram]

        bank = [ps(f"bank{n}", [P, 512]) for n in range(8)]
        bX, bQV, bK, bPT = bank[0], bank[1], bank[2], bank[5]
        bO = [bank[6], bank[7]]
        bS = [bank[3], bank[4]]
        bRank = bank[7]
        bU1, bT1, bO1 = [bank[1], bank[2], bank[3]], [bank[4], bank[5]], [bank[6], bank[7]]
        bG, bU, bHT, bY = [bank[1], bank[2]], [bank[3], bank[4]], bank[5], [bank[6], bank[7]]

        x_loaded = sem("x_loaded")
        const_loaded = sem("const_loaded")
        attw_loaded = sem("attw_loaded")
        const_cast = sem("const_cast")
        ln1_step = sem("ln1_step")
        xn_ready = sem("xn_ready")
        xnT_psum, xnT_ready = sem("xnT_psum"), sem("xnT_ready")
        q_psum, q_ready = sem("q_psum"), sem("q_ready")
        k_psum, k_ready = sem("k_psum"), sem("k_ready")
        v_psum, v_ready = sem("v_psum"), sem("v_ready")
        s_psum = sem("s_psum")
        max_step = sem("max_step")
        exp_done = sem("exp_done")
        pt_psum, pt_ready = sem("pt_psum"), sem("pt_ready")
        o_psum = sem("o_psum")
        rinv_done = sem("rinv_done")
        vb_added = sem("vb_added")
        attn_added = sem("attn_added")
        ln2_step = sem("ln2_step")
        rows_ready = sem("rows_ready")
        rows_kept = sem("rows_kept")
        x2T_psum, x2T_ready = sem("x2T_psum"), sem("x2T_ready")
        lg_psum, lg_ready = sem("lg_psum"), sem("lg_ready")
        out_stored = sem("out_stored")
        route_step = sem("route_step")
        chosen = sem("chosen")
        rank_psum = sem("rank_psum")
        gap_ready, gap_exp = sem("gap_ready"), sem("gap_exp")
        routed = sem("routed")
        zeros_ready, zero_filled = sem("zeros_ready"), sem("zero_filled")
        ffn0_loaded = sem("ffn0_loaded")
        scattered = [sem(f"scattered{g}") for g in range(GROUPS)]
        fetched_back = [sem(f"fetched_back{g}") for g in range(GROUPS)]
        xs_loaded, xs_psum, xsT_ready = sem("xs_loaded"), sem("xs_psum"), sem("xsT_ready")
        up_psum = sem("up_psum")
        silu_done, hid_ready = sem("silu_done"), sem("hid_ready")
        hidT_psum, hidT_ready = sem("hidT_psum"), sem("hidT_ready")
        y_psum, y_ready, y_stored = sem("y_psum"), sem("y_ready"), sem("y_stored")
        combined = sem("combined")
        att1_loaded, ffn1_loaded = sem("att1_loaded"), sem("ffn1_loaded")
        att1_zeroed, att1_preset, latbd_ready = sem("att1_zeroed"), sem("att1_preset"), sem("latbd_ready")
        key_psum, key_turned, kT1_ready = sem("key_psum"), sem("key_turned"), sem("kT1_ready")
        val_psum, val_ready = sem("val_psum"), sem("val_ready")
        unit_psum, unit_max, unit_sub, unit_exp = (sem("unit_" + n) for n in ("psum", "max", "sub", "exp"))
        exT_psum, exT_ready, unit_used = sem("exT_psum"), sem("exT_ready"), sem("unit_used")
        att_step = sem("att_step")
        gate_inverted, mixed_ready = sem("gate_inverted"), sem("mixed_ready")
        mixedT_psum, mixedT_ready = sem("mixedT_psum"), sem("mixedT_ready")
        proj_psum, proj_added = sem("proj_psum"), sem("proj_added")
        bias_added = sem("bias_added")
        xkT_ready = sem("xkT_ready")

        credited = [xnT_psum, lg_psum, x2T_psum, rows_kept, o_psum, pt_psum, exp_done,
                    pt_ready, attn_added, v_ready, k_ready, lg_ready, unit_used, exT_psum,
                    exT_ready, unit_sub, mixedT_psum, proj_psum, proj_added, mixed_ready]

        x_dram = a["L0_attn_x"].rearrange("b (i p) c -> p b i c", p=P)
        out_dram = out.rearrange("b (i p) c -> p b i c", p=P)
        xb = x[:, :, :].rearrange("p (b i) c -> p b i c", b=B)
        rowsb = rows[:, :, :].rearrange("p (b i) c -> p b i c", b=B)
        logitsb = logits[:, :, :].rearrange("p (b i) e -> p b i e", b=B)

        logits1b = logits1[:, :, :].rearrange("p (b i) e -> p b i e", b=B)

        def quad(b):
            return xb[:, bass.ds(b, 1), :, :].rearrange("p a i c -> p (a i) c")

        UNITS, SLOTS = 12, 16

        NT, K_OF = [ST0, ST1], [K0, K1]

        def tile0(n, g):
            return GROUPS * ST0 * n + NT[n] * g

        def chunk0(n, g):
            return tile0(n, g) // CH

        block = ctx.enter_context(nc.Block())

        @block.sync
        def _(sp):
            for s in credited:
                sp.sem_inc(s, 1)
            sp.dma_start(quad(0), x_dram[:, 0, :, :]).then_inc(x_loaded, 16)
            with sp.Fori(1, B) as b:
                sp.wait_ge(x_loaded, 16 * b)
                sp.dma_start(quad(b), x_dram[:, bass.ds(b, 1), :, :].rearrange("p a i c -> p (a i) c")).then_inc(x_loaded, 16)
            sp.wait_ge(zeros_ready, 1)
            for g in range(GROUPS):
                for c in range(ST // CH):
                    sp.dma_start(xs_chunk[g][:, c, :], zeros[:, :]).then_inc(zero_filled, 16)
            sp.dma_start(wgu[:, :, :], a["wgu"]).then_inc(ffn0_loaded, 16)
            sp.dma_start(wd[:, :, 0:2, :], a["wd_a"]).then_inc(ffn0_loaded, 16)
            sp.dma_start(wd[0:I0 - 2 * P, :, 2, :], a["wd_b"]).then_inc(ffn0_loaded, 16)

            for dst, name in ((wk1, "wk1"), (wv1, "wv1"), (wg1, "wg1"), (wp1, "wp1"), (lat, "lat"), (wr1, "L1_ffn_Wg")):
                sp.dma_start(dst[:], a[name]).then_inc(att1_loaded, 16)
            sp.dma_start(br1[:, :], a["L1_ffn_bg"].partition_broadcast(P)).then_inc(att1_loaded, 16)
            sp.dma_start(b1[:, :, :], a["L1_ffn_b1"].partition_broadcast(P)).then_inc(ffn1_loaded, 16)
            sp.dma_start(b2[:, :, :], a["L1_ffn_b2"].partition_broadcast(P)).then_inc(ffn1_loaded, 16)

            def load_rows(n, g):
                sp.wait_ge(scattered[g], 16 * (K0 * TG + (K1 * TG if n else 0)))
                c0 = chunk0(n, g)
                after(sp, xs_psum, c0)
                sp.dma_start(xs[:, :, :].rearrange("p t h -> p (t h)"), xs_chunk[g][:, 0, :]).then_inc(xs_loaded, 16)
                with sp.Fori(1, NT[n] // CH) as c:
                    after(sp, xs_psum, c + c0)
                    sp.dma_start(xs[:, :, :].rearrange("p t h -> p (t h)"),
                                 xs_chunk[g][:, bass.ds(c, 1), :].rearrange("p a h -> p (a h)")).then_inc(xs_loaded, 16)

            if LAST_STAGE >= 2:
                for g in range(GROUPS):
                    load_rows(0, g)
            if LAST_STAGE >= 4:
                sp.wait_ge(y_psum, GROUPS * ST0)
                sp.dma_start(w1, a["w1"]).then_inc(ffn1_loaded, 16)
                sp.dma_start(w2, a["w2"]).then_inc(ffn1_loaded, 16)
                for g in range(GROUPS):
                    load_rows(1, g)
                for g in range(GROUPS):
                    sp.wait_ge(combined, GROUPS + g + 1)
                    sp.dma_start(out_dram[:, BG * g:BG * (g + 1), :, :], xb[:, BG * g:BG * (g + 1), :, :]).then_inc(out_stored, 16)
                sp.wait_ge(out_stored, 16 * GROUPS)
            if LAST_STAGE == 3:
                sp.wait_ge(lg_ready, 1 + 2 * B)
                sp.dma_start(out_dram[:, :, :, :], xb).then_inc(out_stored, 16)
                sp.wait_ge(out_stored, 16)
            if LAST_STAGE == 2:
                sp.wait_ge(combined, GROUPS)
                sp.dma_start(out_dram[:, :, :, :], xb).then_inc(out_stored, 16)
                sp.wait_ge(out_stored, 16)
            if LAST_STAGE == 1:
                sp.wait_ge(attn_added, 1 + Q * B)
                sp.dma_start(out_dram[:, :, :, :], xb).then_inc(out_stored, 16)
                sp.wait_ge(out_stored, 16)

        @block.gpsimd
        def _(pool):
            nc.gpsimd.memset(zeros[:, :], 0.0).then_inc(zeros_ready, 1)

            def prepare0(g):
                pool.wait_ge(attw_loaded, 16 * 4)
                with pool.Fori(BG * g, BG * g + BG) as b:
                    pool.wait_ge(xn_ready, b + 1)
                    nc.gpsimd.tensor_tensor(quad(b), quad(b), vb[:, :].unsqueeze(1).to_broadcast([P, Q, C]),
                                            ALU.add).then_inc(vb_added, 1)
                    pool.wait_ge(rows_ready, b + 1)
                    nc.gpsimd.tensor_copy(rowsb[:, bass.ds(b, 1), :, :].rearrange("p a i c -> p (a i) c"),
                                          xn2[:, :, :]).then_inc(rows_kept, 1)

            def scatter(n, g):
                pool.wait_ge(routed, GROUPS * n + g + 1)
                pool.wait_ge(rows_kept, 1 + B * n + BG * (g + 1))
                if n == 0:
                    pool.wait_ge(zero_filled, 16 * GROUPS * (ST // CH))
                for t in range(TG):
                    for k in range(K_OF[n]):
                        nc.gpsimd.indirect_dma_start(
                            out=xs_dram[g][:, :],
                            out_offset=bass.IndirectOffsetOnAxis(ap=slot[n][g][:, k, t:t + 1], axis=0),
                            in_=rows[:, TG * g + t, :], in_offset=None).then_inc(scattered[g], 16)

            def fetch(n, g):
                pool.wait_ge(y_stored, 16 * (chunk0(n, g) + NT[n] // CH))
                if g == 0:
                    for h in range(GROUPS):
                        pool.wait_ge(scattered[h], 16 * (K0 * TG + (K1 * TG if n else 0)))
                for t in range(TG):
                    for k in range(K_OF[n]):
                        nc.gpsimd.indirect_dma_start(
                            out=back[g][:, k * TG + t, :], out_offset=None, in_=ys_dram[g][:, :],
                            in_offset=bass.IndirectOffsetOnAxis(ap=slot[n][g][:, k, t:t + 1], axis=0),
                        ).then_inc(fetched_back[g], 16)

            prepare0(0)
            if LAST_STAGE >= 2:
                scatter(0, 0)
            prepare0(1)
            if LAST_STAGE >= 2:
                scatter(0, 1)
                fetch(0, 0)
                fetch(0, 1)

            def prepare1(g):
                with pool.Fori(BG * g, BG * g + BG) as b:
                    pool.wait_ge(rows_ready, b + B + 1)
                    nc.gpsimd.tensor_copy(rowsb[:, bass.ds(b, 1), :, :].rearrange("p a i c -> p (a i) c"),
                                          xn2[:, :, :]).then_inc(rows_kept, 1)

            if LAST_STAGE >= 3:
                prepare1(0)
                if LAST_STAGE >= 4:
                    scatter(1, 0)
                prepare1(1)
            if LAST_STAGE >= 4:
                scatter(1, 1)
                fetch(1, 0)
                fetch(1, 1)

        @block.scalar
        def _(act):
            act.dma_start(const[:, :], a["const"]).then_inc(const_loaded, 16)
            act.dma_start(qkvw[:, :, :], a["qkvw"]).then_inc(attw_loaded, 16)
            act.dma_start(qkb[:, :], a["qkb"]).then_inc(attw_loaded, 16)
            act.dma_start(vb[:, :], a["L0_attn_Vb"].partition_broadcast(P)).then_inc(attw_loaded, 16)
            act.dma_start(wr[:, :], a["L0_ffn_Wr"]).then_inc(attw_loaded, 16)

            def evac_xnT(b):
                act.wait_ge(xnT_psum, 1 + b + 1)
                nc.scalar.activation(xnT[:, :], bX[:, :], ACT.Copy).then_inc(xnT_ready, 1)

            def evac_qkv(b):
                act.wait_ge(q_psum, b + 1)
                nc.scalar.activation(qT[:, :], bQV[:, :], ACT.Identity, bias=qkb[:, 0:1]).then_inc(q_ready, 1)
                act.wait_ge(k_psum, b + 1)
                nc.scalar.activation(kT[:, :], bK[:, :], ACT.Identity, bias=qkb[:, 1:2]).then_inc(k_ready, 1)
                act.wait_ge(v_psum, b + 1)
                nc.scalar.activation(v[:, :], bQV[:, :], ACT.Copy).then_inc(v_ready, 1)

            def exps(b):
                for i in range(Q):
                    act.wait_ge(max_step, 2 * (Q * b + i + 1))
                    after(act, pt_psum, 1 + Q * b + max(i - 1, 0))
                    nc.scalar.activation(prob[:, i % 2, 0:(i + 1) * P], bS[i % 2][:, 0:(i + 1) * P], ACT.Exp,
                                         bias=nmx[:, i:i + 1], scale=SCALE0,
                                         accum_out=rsum[:, i:i + 1]).then_inc(exp_done, 1)

            def evac_x2T(b):
                act.wait_ge(x2T_psum, 1 + b + 1)
                after(act, lg_psum, 1 + b)
                nc.scalar.activation(x2T[:, :], bX[:, :], ACT.Copy).then_inc(x2T_ready, 1)

            def attention0_first(g):
                act.wait_ge(attw_loaded, 16 * 4)
                evac_xnT(BG * g)
                evac_qkv(BG * g)

            def attention0_rest(g):
                b0 = BG * g
                with act.Fori(0, BG - 1) as bl:
                    exps(b0 + bl)
                    evac_xnT(b0 + bl + 1)
                    evac_qkv(b0 + bl + 1)
                    evac_x2T(b0 + bl)
                exps(b0 + BG - 1)
                evac_x2T(b0 + BG - 1)

            def route_exp(n, g):
                act.wait_ge(gap_ready, GROUPS * n + g + 1)
                gap = rt_gap[:, :, 0:1] if n == 0 else rt_gap[:, :, 0:E1]
                nc.scalar.activation(gap, gap, ACT.Exp).then_inc(gap_exp, 1)

            def evac_xs(c):
                act.wait_ge(xs_psum, c + 1)
                after(act, up_psum, CH * c)
                nc.scalar.activation(xsT[:, :], bX[:, :], ACT.Copy).then_inc(xsT_ready, 1)

            def silu0(m, t):
                act.wait_ge(up_psum, m + 1)
                after(act, hid_ready, m - 1)
                nc.scalar.activation(act_out[:, t % 2, 0:I0], bG[t % 2][:, 0:I0], ACT.Silu).then_inc(silu_done, 1)

            def evac_y(m, ml, t):
                act.wait_ge(y_psum, m + 1)
                nc.scalar.activation(ysb[:, bass.ds(ml, 1), :].rearrange("p a c -> p (a c)"), bY[t % 2][:, 0:C],
                                     ACT.Copy).then_inc(y_ready, 1)

            def store_y(n, g, c):
                act.wait_ge(y_ready, CH * (c + 1) + tile0(n, g))
                act.dma_start(ys_chunk[g][:, bass.ds(c, 1), :].rearrange("p a h -> p (a h)"),
                              ysb[:, bass.ds(c * CH, CH), :].rearrange("p t h -> p (t h)")).then_inc(y_stored, 16)

            def experts0(g):
                m0, c0, nch = tile0(0, g), chunk0(0, g), NT[0] // CH

                def chunk(c, first=False, last=False):
                    for t in range(CH):
                        m = c * CH + t
                        silu0(m + m0, t)
                        if t == 3 and not last:
                            evac_xs(c + c0 + 1)
                        if not (first and t < 2):
                            evac_y(m + m0 - 2, m - 2, t)
                        if t == 1 and not first:
                            store_y(0, g, c - 1)

                evac_xs(c0)
                after(act, y_stored, 16 * c0)
                chunk(0, first=True)
                with act.Fori(1, nch - 1) as c:
                    chunk(c)
                chunk(nch - 1, last=True)
                for t in (2, 3):
                    m = (nch - 1) * CH + t
                    evac_y(m + m0, m, t)
                store_y(0, g, nch - 1)

            def exp_unit(b, u):
                n = UNITS * b + u
                act.wait_ge(unit_sub, 1 + n + 1)
                nc.scalar.activation(ex[:, u % 3, :], ex[:, u % 3, :], ACT.Exp, scale=SCALE1).then_inc(unit_exp, 1)

            def evac_exT(b, u):
                n = UNITS * b + u
                act.wait_ge(exT_psum, 1 + n + 1)
                after(act, unit_used, 1 + (n - 1 if u >= 2 else UNITS * b))
                nc.scalar.activation(exT[:, u % 2, :], bT1[u % 2][:, :], ACT.Copy).then_inc(exT_ready, 1)

            def evac_mixedT(b, t):
                act.wait_ge(mixedT_psum, 1 + Q * b + t + 1)
                after(act, proj_psum, 1 + Q * b + t)
                nc.scalar.activation(mixedT[:, :], bO1[1][:, 0:P], ACT.Copy).then_inc(mixedT_ready, 1)

            def evac_xT1(b):
                act.wait_ge(xnT_psum, 1 + B + b + 1)
                after(act, unit_psum, UNITS * b)
                nc.scalar.activation(xkT.rearrange("p (n c) -> p n c", n=Q),
                                     bX[:, :].rearrange("p (n c) -> p n c", n=Q)[:, :, 0:KC], ACT.Copy).then_inc(xkT_ready, 1)
                nc.scalar.activation(xT1, bX[:, :], ACT.Copy).then_inc(xnT_ready, 1)

            def evac_values(b):
                act.wait_ge(val_psum, b + 1)
                after(act, unit_used, 1 + UNITS * b)
                for n in range(2):
                    r = slice(n * KC, (n + 1) * KC)
                    nc.scalar.activation(vbd[r, :, :, n, 0:2 * D],
                                         bX[r, 0:2 * C].rearrange("p (u h d) -> p u h d", u=2, h=HP),
                                         ACT.Copy).then_inc(val_ready, 1)

            def attention1_sequence(b, ahead):
                for s in range(SLOTS):
                    if s < UNITS:
                        exp_unit(b, s)
                    if 0 <= s - 2 < UNITS:
                        evac_exT(b, s - 2)
                    if s % 2 and s >= 9:
                        evac_mixedT(b, (s - 9) // 2)
                    if s == 11 and ahead:
                        evac_xT1(b + 1)
                    if s == 15 and ahead:
                        evac_values(b + 1)
                evac_x2T(B + b)

            def attention1(g):
                b0 = BG * g
                evac_xT1(b0)
                evac_values(b0)
                with act.Fori(b0, b0 + BG - 1) as b:
                    attention1_sequence(b, True)
                attention1_sequence(b0 + BG - 1, False)

            def silu1(m, t):
                act.wait_ge(bias_added, m - tile0(1, 0) + 1)
                act.wait_ge(hidT_psum, m - 1)
                nc.scalar.activation(hid[:, t % 2, :], act_out[:, t % 2, :], ACT.Silu).then_inc(hid_ready, 1)

            def evac_hidT1(m, t):
                act.wait_ge(hidT_psum, m + 1)
                act.wait_ge(y_psum, m - 1)
                nc.scalar.activation(hidT[:, t % 2, :], bHT[:, :], ACT.Copy).then_inc(hidT_ready, 1)

            def experts1(g):
                m0, c0, nch = tile0(1, g), chunk0(1, g), NT[1] // CH

                def chunk(c, first=False, last=False):
                    for t in range(CH):
                        m = c * CH + t
                        silu1(m + m0, t)
                        if not (first and t < 1):
                            evac_hidT1(m + m0 - 1, t - 1)
                        if t == 3 and not last:
                            evac_xs(c + c0 + 1)
                        if t == 2 and not first:
                            store_y(1, g, c - 1)

                evac_xs(c0)
                chunk(0, first=True)
                with act.Fori(1, nch - 1) as c:
                    chunk(c)
                chunk(nch - 1, last=True)
                evac_hidT1(nch * CH - 1 + m0, 3)
                store_y(1, g, nch - 1)

            for g in range(GROUPS):
                attention0_first(g)
                if g == 1 and LAST_STAGE >= 2:
                    route_exp(0, 0)
                attention0_rest(g)
            if LAST_STAGE >= 2:
                route_exp(0, 1)
                for g in range(GROUPS):
                    experts0(g)
            if LAST_STAGE >= 3:
                for g in range(GROUPS):
                    attention1(g)
                    if LAST_STAGE >= 4:
                        route_exp(1, g)
            if LAST_STAGE >= 4:
                for g in range(GROUPS):
                    experts1(g)

        @block.vector
        def _(dve):
            dve.wait_ge(const_loaded, 16)
            for n, name in enumerate(("ident", "ones", "before", "causal")):
                nc.vector.tensor_copy(cbf[:, n * P:(n + 1) * P], cst(name)).then_inc(const_cast, 1)
            nc.vector.tensor_copy(latmask_bf, cst("latmask")).then_inc(const_cast, 1)

            def take_wait():
                nc.vector.memset(scratch[:, :], 0.0)

            def layernorm(src, dst, b, step, ready, bn, mv, rs):
                var, half, y, t = (rs[:, n, :] for n in range(4))
                done = [LN_STEPS * b]

                def then(ins):
                    done[0] = done[0] + 1
                    ins.then_inc(step, 1)
                    dve.wait_ge(step, done[0])

                take_wait()
                for i in range(Q):
                    ins = nc.vector.bn_stats(bn[:, i, :], src[:, i, :])
                then(ins)
                take_wait()
                for i in range(Q):
                    ins = nc.vector.bn_aggr(mv[:, i, :], bn[:, i, :])
                then(ins)
                then(nc.vector.tensor_scalar(var, mv[:, :, 1], EPS, None, ALU.add))
                then(nc.vector.tensor_scalar(half.bitcast(I32), var.bitcast(I32), 1, None, ALU.logical_shift_right))
                then(nc.vector.tensor_scalar(y.bitcast(I32), half.bitcast(I32), -1.0, RSQRT_GUESS, ALU.mult, ALU.add))
                for _ in range(NEWTON):
                    then(nc.vector.tensor_tensor(t, y, y, ALU.mult))
                    then(nc.vector.scalar_tensor_tensor(out=t, in0=t, scalar=-0.5, in1=var, op0=ALU.mult, op1=ALU.mult))
                    then(nc.vector.scalar_tensor_tensor(out=y, in0=t, scalar=1.5, in1=y, op0=ALU.add, op1=ALU.mult))
                for i in range(Q):
                    ins = nc.vector.tensor_scalar(dst[:, i, :], src[:, i, :], mv[:, i, 0:1], rs[:, 2, i:i + 1],
                                                  ALU.subtract, ALU.mult)
                ins.then_inc(ready, 1)

            def ln1(b):
                dve.wait_ge(x_loaded, 16 * b + 16)
                after(dve, xnT_psum, 1 + b)
                layernorm(quad(b), xn[:, :, :], b, ln1_step, xn_ready, bn, mv, rstd)

            def rowmax(b, i):
                dve.wait_ge(s_psum, Q * b + i + 1)
                nc.vector.tensor_reduce(mx[:, i:i + 1], bS[i % 2][:, 0:(i + 1) * P], X, ALU.max).then_inc(max_step, 1)
                dve.wait_ge(max_step, 2 * (Q * b + i) + 1)
                nc.vector.tensor_scalar(nmx[:, i:i + 1], mx[:, i:i + 1], -SCALE0, None, ALU.mult).then_inc(max_step, 1)

            def copy_pt(b, i):
                dve.wait_ge(pt_psum, 1 + Q * b + i + 1)
                after(dve, o_psum, 1 + Q * b + max(i - 1, 0))
                nc.vector.tensor_copy(probT[:, i % 2, 0:(i + 1) * P], bPT[:, 0:(i + 1) * P]).then_inc(pt_ready, 1)

            def add_attn(b, i):
                dve.wait_ge(exp_done, 1 + Q * b + i + 1)
                nc.vector.reciprocal(rinv[:, i:i + 1], rsum[:, i:i + 1]).then_inc(rinv_done, 1)
                dve.wait_ge(rinv_done, Q * b + i + 1)
                dve.wait_ge(o_psum, 1 + Q * b + i + 1)
                dve.wait_ge(vb_added, b + 1)
                xt = xb[:, bass.ds(b, 1), i, :].rearrange("p a c -> p (a c)")
                nc.vector.scalar_tensor_tensor(out=xt, in0=bO[i % 2][:, 0:C], scalar=rinv[:, i:i + 1],
                                               in1=xt, op0=ALU.mult, op1=ALU.add).then_inc(attn_added, 1)

            def ln2(b):
                dve.wait_ge(attn_added, 1 + Q * b + Q)
                after(dve, x2T_psum, 1 + b)
                after(dve, rows_kept, 1 + b)
                layernorm(quad(b), xn2[:, :, :], b, ln2_step, rows_ready, bn2, mv2, rstd2)

            def evac_logits1(b):
                dve.wait_ge(lg_psum, 1 + B + b + 1)
                nc.vector.tensor_tensor(logits1b[:, bass.ds(b, 1), :, :].rearrange("p a i e -> p (a i) e"),
                                        bX[:, 0:Q * E1].rearrange("p (i e) -> p i e", i=Q),
                                        br1[:, :].unsqueeze(1).to_broadcast([P, Q, E1]), ALU.add).then_inc(lg_ready, 1)

            def evac_logits(b):
                dve.wait_ge(lg_psum, 1 + b + 1)
                nc.vector.tensor_copy(logitsb[:, bass.ds(b, 1), :, :].rearrange("p a i e -> p (a i) e"),
                                      bX[:, 0:Q * E0].rearrange("p (i e) -> p i e", i=Q)).then_inc(lg_ready, 1)

            def sequence0(b, ahead):
                rowmax(b, 0)
                rowmax(b, 1)
                copy_pt(b, 0)
                rowmax(b, 2)
                copy_pt(b, 1)
                add_attn(b, 0)
                rowmax(b, 3)
                if ahead:
                    ln1(b + 1)
                copy_pt(b, 2)
                add_attn(b, 1)
                copy_pt(b, 3)
                add_attn(b, 2)
                add_attn(b, 3)
                ln2(b)
                evac_logits(b)

            steps = [0]

            def then(ins):
                steps[0] += 1
                ins.then_inc(route_step, 1)
                dve.wait_ge(route_step, steps[0])

            def first_max(src, sel, top, E):
                ge, cand = rt_ge[:, :, 0:E], rt_cand[:, :, 0:E]
                iota = cst("iota_e")[:, 0:E].unsqueeze(1).to_broadcast([P, TG, E])
                then(nc.vector.tensor_reduce(top, src, X, ALU.max))
                then(nc.vector.tensor_tensor(ge, src, top.unsqueeze(2).to_broadcast([P, TG, E]), ALU.is_ge))
                then(nc.vector.scalar_tensor_tensor(out=cand, in0=ge, scalar=-16.0, in1=iota, op0=ALU.mult, op1=ALU.add))
                then(nc.vector.tensor_reduce(rt_max[:, 2, :], cand, X, ALU.min))
                then(nc.vector.tensor_tensor(sel, cand, rt_max[:, 2, :].unsqueeze(2).to_broadcast([P, TG, E]),
                                             ALU.is_equal))

            def choose(n, g):
                E = (E0, E1)[n]
                lg = (logits if n == 0 else logits1)[:, TG * g:TG * (g + 1), :]
                dve.wait_ge(lg_ready, 1 + B * n + BG * (g + 1))
                sel = rt_sel[:, :, :, 0:E]
                first_max(lg, sel[:, 0], rt_max[:, 0, :], E)
                if n == 0:
                    second = rt_second[:, :, :]
                    then(nc.vector.scalar_tensor_tensor(out=second, in0=sel[:, 0], scalar=NEG, in1=lg,
                                                        op0=ALU.mult, op1=ALU.add))
                    first_max(second, sel[:, 1], rt_max[:, 1, :], E)
                    nc.vector.tensor_tensor(rt_gap[:, :, 0], rt_max[:, 1, :], rt_max[:, 0, :],
                                            ALU.subtract).then_inc(gap_ready, 1)
                    nc.vector.tensor_tensor(rt_selbf[:, :, 0:E], sel[:, 0], sel[:, 1], ALU.add).then_inc(chosen, 1)
                else:
                    nc.vector.tensor_tensor(rt_gap[:, :, 0:E], lg, rt_max[:, 0, :].unsqueeze(2).to_broadcast([P, TG, E]),
                                            ALU.subtract).then_inc(gap_ready, 1)
                    nc.vector.tensor_copy(rt_selbf[:, :, 0:E], sel[:, 0]).then_inc(chosen, 1)

            def place(n, g):
                E, K, N = (E0, E1)[n], K_OF[n], NT[n]
                sel = rt_sel[:, :, :, 0:E]
                tiles, base, end = rt_tiles[:, 0:E], rt_base[:, 0:E], rt_end[:, 0:E]
                dve.wait_ge(rank_psum, GROUPS * n + g + 1)
                rank = bRank[:, 0:TG * E].rearrange("p (t e) -> p t e", e=E)
                then(nc.vector.tensor_scalar(tiles, bRank[:, TG * E:(TG + 1) * E], P - 1.0, None, ALU.add))
                then(nc.vector.tensor_scalar(tiles, tiles, 7, None, ALU.logical_shift_right))
                then(nc.vector.tensor_tensor(rt_below[:, 0:E, 0:E], below[:, 0:E, 0:E],
                                             tiles.unsqueeze(1).to_broadcast([P, E, E]), ALU.mult))
                then(nc.vector.tensor_reduce(base, rt_below[:, 0:E, 0:E], X, ALU.add))
                nc.vector.tensor_tensor(end, base, tiles, ALU.add)
                then(nc.vector.scalar_tensor_tensor(out=rt_pos[:, :, 0:E], in0=base.unsqueeze(1).to_broadcast([P, TG, E]),
                                                    scalar=float(P), in1=rank, op0=ALU.mult, op1=ALU.add))
                pos, hi, mid, lo = (rt_int[:, m, 0:K * TG] for m in range(4))
                for k in range(K):
                    then(nc.vector.tensor_tensor(rt_prod[:, :, 0:E], sel[:, k], rt_pos[:, :, 0:E], ALU.mult))
                    then(nc.vector.tensor_reduce(rt_posf[:, k * TG:(k + 1) * TG], rt_prod[:, :, 0:E], X, ALU.add))
                then(nc.vector.tensor_copy(pos, rt_posf[:, 0:K * TG]))
                nc.vector.tensor_scalar(hi, pos, ~(CH * P - 1) & 0x7FFFFFFF, None, ALU.bitwise_and)
                nc.vector.tensor_scalar(mid, pos, P - 1, 2, ALU.bitwise_and, ALU.logical_shift_left)
                then(nc.vector.tensor_scalar(lo, pos, 7, CH - 1, ALU.logical_shift_right, ALU.bitwise_and))
                then(nc.vector.tensor_tensor(hi, hi, mid, ALU.bitwise_or))
                then(nc.vector.tensor_tensor(slot[n][g][:, :, :].rearrange("p k t -> p (k t)").bitcast(I32), hi, lo,
                                             ALU.bitwise_or))
                past = rt_past[:, 0:N, 0:E]
                then(nc.vector.tensor_tensor(past, cst("iota_j")[:, 0:N].unsqueeze(2).to_broadcast([P, N, E]),
                                             end.unsqueeze(1).to_broadcast([P, N, E]), ALU.is_ge))
                then(nc.vector.tensor_reduce(rt_tile_e[:, 0:N], past, X, ALU.add))
                nc.vector.tensor_scalar(tile_e[n][g][:, 0:N], rt_tile_e[:, 0:N], E - 1.0, None, ALU.min).then_inc(routed, 1)

            def weigh(n, g):
                w = weight[n][g]
                dve.wait_ge(gap_exp, GROUPS * n + g + 1)
                if n == 0:
                    then(nc.vector.tensor_scalar(rt_den[:, :], rt_gap[:, :, 0], 1.0, None, ALU.add))
                    then(nc.vector.reciprocal(w[:, 0, :], rt_den[:, :]))
                    then(nc.vector.tensor_tensor(w[:, 1, :], rt_gap[:, :, 0], w[:, 0, :], ALU.mult))
                else:
                    then(nc.vector.tensor_reduce(rt_den[:, :], rt_gap[:, :, 0:E1], X, ALU.add))
                    then(nc.vector.reciprocal(w[:, 0, :], rt_den[:, :]))

            def gate0(m, t):
                dve.wait_ge(silu_done, m + 1)
                after(dve, hidT_psum, m - 1)
                nc.vector.tensor_tensor(hid[:, t % 2, 0:I0], act_out[:, t % 2, 0:I0], bU[t % 2][:, 0:I0],
                                        ALU.mult).then_inc(hid_ready, 1)

            def evac_hidT0(m, t):
                dve.wait_ge(hidT_psum, m + 1)
                after(dve, y_psum, m - 1)
                nc.vector.tensor_copy(hidT[:, t % 2, 0:HC0 * P], bHT[:, 0:HC0 * P]).then_inc(hidT_ready, 1)

            def experts0(g):
                m0, nch = tile0(0, g), NT[0] // CH

                def chunk(c, first=False):
                    for t in range(CH):
                        m = c * CH + t + m0
                        gate0(m, t)
                        if not (first and t < 1):
                            evac_hidT0(m - 1, t - 1)

                chunk(0, first=True)
                with dve.Fori(1, nch) as c:
                    chunk(c)
                evac_hidT0(nch * CH - 1 + m0, 3)

            def combine(n, g):
                dve.wait_ge(fetched_back[g], 16 * (K0 * TG + (K1 * TG if n else 0)))
                for k in range(K_OF[n]):
                    for t in range(TG):
                        xt = x[:, TG * g + t, :]
                        ins = nc.vector.scalar_tensor_tensor(out=xt, in0=back[g][:, k * TG + t, :],
                                                             scalar=weight[n][g][:, k, t:t + 1], in1=xt,
                                                             op0=ALU.mult, op1=ALU.add)
                    if k < K_OF[n] - 1:
                        then(ins)
                ins.then_inc(combined, 1)
                dve.wait_ge(combined, GROUPS * n + g + 1)

            def ln3(b):
                after(dve, xnT_psum, 1 + B + b)
                layernorm(quad(b), xn[:, :, :], B + b, ln1_step, xn_ready, bn, mv, rstd)

            def ln4(b):
                dve.wait_ge(proj_added, 1 + Q * b + Q)
                dve.wait_ge(x2T_psum, 1 + B + b)
                dve.wait_ge(rows_kept, 1 + B + b)
                layernorm(quad(b), xn2[:, :, :], B + b, ln2_step, rows_ready, bn2, mv2, rstd2)

            def turn_keys(b):
                dve.wait_ge(key_psum, b + 1)
                after(dve, unit_psum, UNITS * b)
                nc.vector.tensor_tensor(turned[:, :, :].rearrange("p a k -> p (a k)"), bX[:, :],
                                        const[:, COLS["cos"][0]:COLS["sin"][1]], ALU.mult).then_inc(key_turned, 1)
                dve.wait_ge(key_turned, b + 1)
                nc.vector.tensor_tensor(kT1[:, :], turned[:, 0, :], turned[:, 1, :], ALU.add).then_inc(kT1_ready, 1)

            def shift_unit(b, u):
                n = UNITS * b + u
                dve.wait_ge(unit_psum, n + 1)
                unit = bU1[u % 3][:, :].rearrange("p (s k) -> p s k", s=8)
                nc.vector.tensor_reduce(umax[:, u % 3, :], unit, X, ALU.max).then_inc(unit_max, 1)
                dve.wait_ge(unit_max, n + 1)
                after(dve, exT_psum, 1 + (n - 2 if u >= 3 else UNITS * b))
                nc.vector.tensor_tensor(ex[:, u % 3, :].rearrange("p (s k) -> p s k", s=8), unit,
                                        umax[:, u % 3, :].unsqueeze(2).to_broadcast([P, 8, KC]),
                                        ALU.subtract).then_inc(unit_sub, 1)

            def sum_chunks(b, u):
                step = 3 * (Q * b + u)
                dve.wait_ge(unit_used, 1 + UNITS * b + u + 1)
                got = bO1[u % 2][:, 0:2 * Q * VW].rearrange("p (h n v) -> p h n v", h=2, n=Q)
                nc.vector.reciprocal(chunk_inv[:, :, :], got[:, :, :, 2 * D]).then_inc(att_step, 1)
                dve.wait_ge(att_step, step + 1)
                nc.vector.tensor_tensor(chunk_out[:, :, :, :], got[:, :, :, 0:2 * D],
                                        chunk_inv[:, :, :].unsqueeze(3).to_broadcast([P, 2, Q, 2 * D]),
                                        ALU.mult).then_inc(att_step, 1)
                dve.wait_ge(att_step, step + 2)
                after(dve, unit_used, 1 + UNITS * b)
                for n in range(2):
                    r = slice(n * L, (n + 1) * L)
                    ins = nc.vector.tensor_reduce(attbd[r, 2 * u:2 * u + 2, n * D:(n + 1) * D],
                                                  chunk_out[r, :, :, n * D:(n + 1) * D].rearrange("p h n d -> p h d n"),
                                                  X, ALU.add)
                ins.then_inc(att_step, 1)

            def normalise_gates(b, t):
                dve.wait_ge(unit_used, 1 + UNITS * b + 4 + 2 * t + 2)
                got = bO1[0][:, 0:HP * GW].rearrange("p (h v) -> p h v", h=HP)
                nc.vector.reciprocal(gate_inv[:, :, :], got[:, :, 2 * D:GW]).then_inc(gate_inverted, 1)
                dve.wait_ge(gate_inverted, Q * b + t + 1)
                after(dve, mixedT_psum, 1 + Q * b + t)
                nc.vector.tensor_tensor(mixed[:, :, :, :], got[:, :, 0:2 * D].rearrange("p h (k d) -> p h k d", k=2),
                                        gate_inv[:, :, :].unsqueeze(3).to_broadcast([P, HP, 2, D]),
                                        ALU.mult).then_inc(mixed_ready, 1)

            def add_projected(b, t):
                dve.wait_ge(proj_psum, 1 + Q * b + t + 1)
                xt = xb[:, bass.ds(b, 1), t, :].rearrange("p a c -> p (a c)")
                nc.vector.tensor_tensor(xt, xt, bO1[1][:, 0:C], ALU.add).then_inc(proj_added, 1)

            def attention1_sequence(b, ahead):
                for s in range(SLOTS):
                    if s < UNITS:
                        shift_unit(b, s)
                    if 0 <= s - 3 < 4:
                        sum_chunks(b, s - 3)
                    if s == 7 and ahead:
                        ln3(b + 1)
                    if s % 2 == 0 and s >= 8:
                        normalise_gates(b, (s - 8) // 2)
                    if s % 2 and s >= 9:
                        add_projected(b, (s - 9) // 2)
                    if s == 13 and ahead:
                        turn_keys(b + 1)
                ln4(b)
                evac_logits1(b)

            def attention1(g):
                b0 = BG * g
                ln3(b0)
                turn_keys(b0)
                with dve.Fori(b0, b0 + BG - 1) as b:
                    attention1_sequence(b, True)
                attention1_sequence(b0 + BG - 1, False)

            def tile_expert(g, m):
                return dve.value_load(tile_e[1][g][0:1, bass.ds(m, 1)], min_val=0, max_val=E1 - 1)

            def bias1(g, m, mg, t):
                e = tile_expert(g, m)
                dve.wait_ge(up_psum, mg + 1)
                dve.wait_ge(hid_ready, mg - 1)
                nc.vector.tensor_tensor(act_out[:, t % 2, :], bG[t % 2][:, :],
                                        b1[:, bass.ds(e, 1), :].rearrange("p a n -> p (a n)"), ALU.add).then_inc(bias_added, 1)

            def evac_y1(g, m, mg, t):
                e = tile_expert(g, m)
                dve.wait_ge(y_psum, mg + 1)
                nc.vector.tensor_tensor(ysb[:, bass.ds(m, 1), :].rearrange("p a c -> p (a c)"), bY[t % 2][:, 0:C],
                                        b2[:, bass.ds(e, 1), :].rearrange("p a n -> p (a n)"), ALU.add).then_inc(y_ready, 1)

            def experts1(g):
                m0, nch = tile0(1, g), NT[1] // CH
                dve.wait_ge(y_stored, 16 * chunk0(1, g))
                dve.wait_ge(ffn1_loaded, 16 * 4)

                def chunk(c, first=False):
                    for t in range(CH):
                        m = c * CH + t
                        bias1(g, m, m + m0, t)
                        if not (first and t < 2):
                            evac_y1(g, m - 2, m + m0 - 2, t)

                chunk(0, first=True)
                with dve.Fori(1, nch) as c:
                    chunk(c)
                for m in (nch * CH - 2, nch * CH - 1):
                    evac_y1(g, m, m + m0, m % 2)

            if LAST_STAGE >= 3:
                nc.vector.memset(vbd[:], 0.0).then_inc(att1_zeroed, 1)
                nc.vector.memset(attbd[:], 0.0).then_inc(att1_zeroed, 1)
                dve.wait_ge(att1_zeroed, 2)
                for n in range(2):
                    nc.vector.memset(vbd[n * KC:(n + 1) * KC, :, :, n, 2 * D:VW], 1.0).then_inc(att1_preset, 1)
                    nc.vector.memset(attbd[n * L:(n + 1) * L, :, 2 * D + n:2 * D + n + 1], 1.0).then_inc(att1_preset, 1)

            def preset_latents():
                dve.wait_ge(att1_loaded, 16 * 7)
                nc.vector.tensor_tensor(latbd[:, :, :], lat[:, :].unsqueeze(1).to_broadcast([P, H, L]),
                                        cst("headmask").unsqueeze(2).to_broadcast([P, H, L]), ALU.mult).then_inc(latbd_ready, 1)

            for g in range(GROUPS):
                b0 = BG * g
                ln1(b0)
                if g == 1 and LAST_STAGE >= 2:
                    choose(0, 0)
                    place(0, 0)
                    weigh(0, 0)
                with dve.Fori(b0, b0 + BG - 1) as b:
                    sequence0(b, True)
                sequence0(b0 + BG - 1, False)
            if LAST_STAGE >= 2:
                choose(0, 1)
                place(0, 1)
                weigh(0, 1)
                for g in range(GROUPS):
                    experts0(g)
                for g in range(GROUPS):
                    if LAST_STAGE >= 3 and g == 0:
                        preset_latents()
                    combine(0, g)
                    if LAST_STAGE >= 3:
                        attention1(g)
                        if LAST_STAGE >= 4:
                            choose(1, g)
                            place(1, g)
                            weigh(1, g)
            if LAST_STAGE >= 4:
                for g in range(GROUPS):
                    experts1(g)
                for g in range(GROUPS):
                    combine(1, g)

        @block.tensor
        def _(pe):
            pe.wait_ge(const_cast, 5)
            pe.wait_ge(attw_loaded, 16 * 4)

            def t1(b, earlier):
                pe.wait_ge(xn_ready, b + 1)
                after(pe, lg_ready, 1 + earlier)
                for i in range(Q):
                    ins = nc.tensor.transpose(bX[:, i * P:(i + 1) * P], xn[:, i, :], ident)
                ins.then_inc(xnT_psum, 1)

            def qkv(b):
                pe.wait_ge(xnT_ready, b + 1)
                after(pe, v_ready, 1 + b)
                nc.tensor.matmul(bQV[:, :], qkvw[:, 0, :], xnT[:, :], start=True, stop=True).then_inc(q_psum, 1)
                after(pe, k_ready, 1 + b)
                nc.tensor.matmul(bK[:, :], qkvw[:, 1, :], xnT[:, :], start=True, stop=True).then_inc(k_psum, 1)
                pe.wait_ge(q_ready, b + 1)
                for i in range(Q):
                    ins = nc.tensor.matmul(bQV[:, i * P:(i + 1) * P],
                                           xnT[:, i * P:(i + 1) * P],
                                           qkvw[:, 2, :], start=True, stop=True)
                ins.then_inc(v_psum, 1)

            def scores(b, i):
                if i == 0:
                    pe.wait_ge(k_ready, 1 + b + 1)
                after(pe, exp_done, 1 + Q * b + max(i - 1, 0))
                nc.tensor.matmul(bS[i % 2][:, i * P:(i + 1) * P], ident_bf, causal_bf, start=True, stop=False,
                                 skip_group_check=True)
                nc.tensor.matmul(bS[i % 2][:, 0:(i + 1) * P],
                                 qT[:, i * P:(i + 1) * P],
                                 kT[:, 0:(i + 1) * P],
                                 start=False, stop=True, skip_group_check=True).then_inc(s_psum, 1)

            def pt(b, i):
                pe.wait_ge(exp_done, 1 + Q * b + i + 1)
                after(pe, pt_ready, 1 + Q * b + i)
                for j in range(i + 1):
                    ins = nc.tensor.transpose(bPT[:, j * P:(j + 1) * P], prob[:, i % 2, j * P:(j + 1) * P], ident)
                ins.then_inc(pt_psum, 1)

            def pv(b, i):
                pe.wait_ge(pt_ready, 1 + Q * b + i + 1)
                if i == 0:
                    pe.wait_ge(v_ready, 1 + b + 1)
                after(pe, attn_added, 1 + Q * b + max(i - 1, 0))
                for j in range(i + 1):
                    ins = nc.tensor.matmul(bO[i % 2][:, 0:C], probT[:, i % 2, j * P:(j + 1) * P],
                                           v[:, j * C:(j + 1) * C],
                                           start=(j == 0), stop=(j == i))
                ins.then_inc(o_psum, 1)

            def route_logits(b, ahead, router, E):
                pe.wait_ge(rows_ready, b + 1)
                pe.wait_ge(xnT_ready, b + 1 + ahead)
                for i in range(Q):
                    ins = nc.tensor.transpose(bX[:, i * P:(i + 1) * P],
                                              xn2[:, i, :], ident)
                ins.then_inc(x2T_psum, 1)
                pe.wait_ge(x2T_ready, b + 1)
                for i in range(Q):
                    ins = nc.tensor.matmul(bX[:, i * E:(i + 1) * E], x2T[:, i * P:(i + 1) * P], router[:, :],
                                           start=True, stop=True)
                ins.then_inc(lg_psum, 1)

            def sequence0(b, ahead):
                scores(b, 0)
                scores(b, 1)
                pt(b, 0)
                scores(b, 2)
                pt(b, 1)
                pv(b, 0)
                scores(b, 3)
                pt(b, 2)
                pv(b, 1)
                if ahead:
                    t1(b + 1, b)
                pt(b, 3)
                pv(b, 2)
                pv(b, 3)
                if ahead:
                    qkv(b + 1)
                route_logits(b, ahead, wr, E0)

            def rank(n, g):
                E = (E0, E1)[n]
                pe.wait_ge(chosen, GROUPS * n + g + 1)
                nc.tensor.matmul(bRank[:, 0:TG * E], before_bf, rt_selbf[:, :, 0:E], start=True, stop=False,
                                 skip_group_check=True)
                for t in range(TG):
                    ins = nc.tensor.matmul(bRank[:, (t + 1) * E:(TG + 1) * E], ones_bf,
                                           rt_selbf[:, t, 0:E].unsqueeze(1).to_broadcast([P, TG - t, E]),
                                           start=False, stop=(t == TG - 1), skip_group_check=True)
                ins.then_inc(rank_psum, 1)

            def xs_transpose(c):
                pe.wait_ge(xs_loaded, 16 * c + 16)
                after(pe, xsT_ready, c)
                for t in range(CH):
                    ins = nc.tensor.transpose(bX[:, t * P:(t + 1) * P], xs[:, t, :], ident)
                ins.then_inc(xs_psum, 1)

            def expert_of(n, g, m):
                return pe.value_load(tile_e[n][g][0:1, bass.ds(m, 1)], min_val=0, max_val=(E0, E1)[n] - 1)

            def up0(g, m, mg, t, chunk):
                e = expert_of(0, g, m)
                if t == 0:
                    pe.wait_ge(xsT_ready, chunk + 1)
                after(pe, hid_ready, mg - 1)
                for bk, half in ((bG, 0), (bU, 1)):
                    ins = nc.tensor.matmul(bk[t % 2][:, 0:I0], xsT[:, t * P:(t + 1) * P],
                                           wgu[:, bass.ds(e, 1), half * I0:(half + 1) * I0].rearrange("p a n -> p (a n)"),
                                           start=True, stop=True)
                ins.then_inc(up_psum, 1)

            def turn0(mg, t):
                pe.wait_ge(hid_ready, mg + 1)
                after(pe, hidT_ready, mg)
                for j in range(HC0):
                    w = min(P, I0 - j * P)
                    ins = nc.tensor.transpose(bHT[0:w, j * P:(j + 1) * P], hid[:, t % 2, j * P:j * P + w], ident)
                ins.then_inc(hidT_psum, 1)

            def down0(g, m, mg, t):
                e = expert_of(0, g, m)
                pe.wait_ge(hidT_ready, mg + 1)
                after(pe, y_ready, mg - 1)
                for j in range(HC0):
                    w = min(P, I0 - j * P)
                    ins = nc.tensor.matmul(bY[t % 2][:, 0:C], hidT[0:w, t % 2, j * P:(j + 1) * P],
                                           wd[0:w, bass.ds(e, 1), j, :].rearrange("p a n -> p (a n)"),
                                           start=(j == 0), stop=(j == HC0 - 1))
                ins.then_inc(y_psum, 1)

            def experts0(g):
                m0, c0, nch = tile0(0, g), chunk0(0, g), NT[0] // CH
                pe.wait_ge(ffn0_loaded, 16 * 3)
                pe.wait_ge(routed, g + 1)

                def chunk(c, first=False, last=False):
                    for t in range(CH):
                        m = c * CH + t
                        up0(g, m, m + m0, t, c + c0)
                        if t == 3 and not last:
                            xs_transpose(c + c0 + 1)
                        if not (first and t < 1):
                            turn0(m + m0 - 1, t - 1)
                        if not (first and t < 2):
                            down0(g, m - 2, m + m0 - 2, t)

                xs_transpose(c0)
                chunk(0, first=True)
                with pe.Fori(1, nch - 1) as c:
                    chunk(c)
                chunk(nch - 1, last=True)
                end = nch * CH
                turn0(end - 1 + m0, 3)
                down0(g, end - 2, end - 2 + m0, 2)
                down0(g, end - 1, end - 1 + m0, 3)

            def keys(b):
                pe.wait_ge(xnT_ready, B + b + 1)
                pe.wait_ge(xkT_ready, b + 1)
                for n in range(2):
                    ins = nc.tensor.matmul(bX[:, n * Q * KC:(n + 1) * Q * KC], wk1[:, n, :], xkT, start=True, stop=True)
                ins.then_inc(key_psum, 1)

            def values(b):
                pe.wait_ge(key_turned, b + 1)
                for n in range(2):
                    ins = nc.tensor.matmul(bX[:, n * C:(n + 1) * C], xkT[:, n * P:(n + 1) * P], wv1[:, :], start=True, stop=True)
                ins.then_inc(val_psum, 1)

            def produce(b, u):
                n = UNITS * b + u
                bk = bU1[u % 3]
                after(pe, unit_sub, 1 + (n - 2 if u >= 3 else UNITS * b))
                if u < 4:
                    pe.wait_ge(kT1_ready, b + 1)
                    nc.tensor.matmul(bk[:, :].rearrange("p (s k) -> p s k", s=8), ident_bf,
                                     latmask_bf.unsqueeze(1).to_broadcast([P, 8, KC]), start=True, stop=False,
                                     skip_group_check=True)
                    for h in range(2):
                        ins = nc.tensor.matmul(bk[:, h * Q * KC:(h + 1) * Q * KC],
                                               latbd[:, 4 * u + 2 * h:4 * u + 2 * h + 2, :].rearrange("p h l -> p (h l)"),
                                               kT1[:, :], start=False, stop=True, skip_group_check=True)
                else:
                    t, half = (u - 4) // 2, u % 2
                    ins = nc.tensor.matmul(bk[:, :], xT1[:, t * P:(t + 1) * P], wg1[:, half * 512:(half + 1) * 512],
                                           start=True, stop=True)
                ins.then_inc(unit_psum, 1)

            def turn_unit(b, u):
                n = UNITS * b + u
                pe.wait_ge(unit_exp, n + 1)
                after(pe, exT_ready, 1 + (n - 1 if u >= 2 else UNITS * b))
                for j in range(4):
                    ins = nc.tensor.transpose(bT1[u % 2][:, j * P:(j + 1) * P], ex[:, u % 3, j * P:(j + 1) * P], ident)
                ins.then_inc(exT_psum, 1)

            def use_unit(b, u):
                n = UNITS * b + u
                pe.wait_ge(exT_ready, 1 + n + 1)
                if u < 4:
                    if u >= 2:
                        pe.wait_ge(att_step, 3 * (Q * b + u - 2) + 2)
                    elif u == 0:
                        after(pe, mixed_ready, 1 + Q * b)
                    else:
                        after(pe, proj_added, 1 + Q * b)
                    if u == 0:
                        pe.wait_ge(val_ready, 2 * b + 2)
                    for j in range(4):
                        ins = nc.tensor.matmul(bO1[u % 2][:, j * 2 * VW:(j + 1) * 2 * VW], exT[:, u % 2, j * P:(j + 1) * P],
                                               vbd[:, j % 2, 2 * u + j // 2, :, :].rearrange("p n v -> p (n v)"),
                                               start=True, stop=True)
                else:
                    t = (u - 4) // 2
                    if t == 0:
                        pe.wait_ge(att_step, 3 * (Q * b + Q))
                    else:
                        pe.wait_ge(mixed_ready, 1 + Q * b + t)
                    for j in range(4):
                        h = 4 * (u % 2) + j
                        ins = nc.tensor.matmul(bO1[0][:, h * GW:(h + 1) * GW], exT[:, u % 2, j * P:(j + 1) * P],
                                               attbd[:, h, :], start=True, stop=True)
                ins.then_inc(unit_used, 1)

            def turn_mixed(b, t):
                pe.wait_ge(mixed_ready, 1 + Q * b + t + 1)
                if t == 0:
                    pe.wait_ge(att_step, 3 * (Q * b + Q))
                else:
                    pe.wait_ge(proj_added, 1 + Q * b + t)
                nc.tensor.transpose(bO1[1][:, 0:P], mixed[:, :, :, :].rearrange("p h k d -> p (h k d)"),
                                    ident).then_inc(mixedT_psum, 1)

            def project(b, t):
                pe.wait_ge(mixedT_ready, Q * b + t + 1)
                nc.tensor.matmul(bO1[1][:, 0:C], mixedT[:, :], wp1[:, :], start=True, stop=True).then_inc(proj_psum, 1)

            def attention1_sequence(b, ahead):
                for s in range(SLOTS):
                    if s < UNITS:
                        produce(b, s)
                    if s % 2 and s >= 9:
                        turn_mixed(b, (s - 9) // 2)
                    if s == 10 and ahead:
                        t1(B + b + 1, B + b)
                    if 0 <= s - 2 < UNITS:
                        turn_unit(b, s - 2)
                    if 0 <= s - 3 < UNITS:
                        use_unit(b, s - 3)
                    if s == 12 and ahead:
                        keys(b + 1)
                    if s == 14 and ahead:
                        values(b + 1)
                    if s % 2 and s >= 9:
                        project(b, (s - 9) // 2)
                if ahead:
                    pe.wait_ge(val_ready, 2 * b + 4)
                route_logits(B + b, ahead, wr1, E1)

            def attention1(g):
                b0 = BG * g
                t1(B + b0, B + b0)
                keys(b0)
                values(b0)
                with pe.Fori(b0, b0 + BG - 1) as b:
                    attention1_sequence(b, True)
                attention1_sequence(b0 + BG - 1, False)

            def up1(g, m, mg, t, chunk):
                e = expert_of(1, g, m)
                if t == 0:
                    pe.wait_ge(xsT_ready, chunk + 1)
                after(pe, bias_added, mg - tile0(1, 0) - 1)
                nc.tensor.matmul(bG[t % 2][:, :], xsT[:, t * P:(t + 1) * P],
                                 w1[:, bass.ds(e, 1), :].rearrange("p a n -> p (a n)"),
                                 start=True, stop=True).then_inc(up_psum, 1)

            def turn1(mg, t):
                pe.wait_ge(hid_ready, mg + 1)
                pe.wait_ge(hidT_ready, mg)
                for j in range(HC1):
                    ins = nc.tensor.transpose(bHT[:, j * P:(j + 1) * P], hid[:, t % 2, j * P:(j + 1) * P], ident)
                ins.then_inc(hidT_psum, 1)

            def down1(g, m, mg, t):
                e = expert_of(1, g, m)
                pe.wait_ge(hidT_ready, mg + 1)
                pe.wait_ge(y_ready, mg - 1)
                for j in range(HC1):
                    ins = nc.tensor.matmul(bY[t % 2][:, 0:C], hidT[:, t % 2, j * P:(j + 1) * P],
                                           w2[:, bass.ds(e, 1), j, :].rearrange("p a n -> p (a n)"),
                                           start=(j == 0), stop=(j == HC1 - 1))
                ins.then_inc(y_psum, 1)

            def experts1(g):
                m0, c0, nch = tile0(1, g), chunk0(1, g), NT[1] // CH
                pe.wait_ge(ffn1_loaded, 16 * 4)
                pe.wait_ge(routed, GROUPS + g + 1)

                def chunk(c, first=False, last=False):
                    for t in range(CH):
                        m = c * CH + t
                        up1(g, m, m + m0, t, c + c0)
                        if t == 3 and not last:
                            xs_transpose(c + c0 + 1)
                        if not (first and t < 1):
                            turn1(m + m0 - 1, t - 1)
                        if not (first and t < 2):
                            down1(g, m - 2, m + m0 - 2, t)

                xs_transpose(c0)
                chunk(0, first=True)
                with pe.Fori(1, nch - 1) as c:
                    chunk(c)
                chunk(nch - 1, last=True)
                end = nch * CH
                turn1(end - 1 + m0, 3)
                down1(g, end - 2, end - 2 + m0, 2)
                down1(g, end - 1, end - 1 + m0, 3)

            for g in range(GROUPS):
                b0 = BG * g
                t1(b0, b0)
                qkv(b0)
                if g == 1 and LAST_STAGE >= 2:
                    rank(0, 0)
                with pe.Fori(0, BG - 1) as bl:
                    sequence0(b0 + bl, True)
                sequence0(b0 + BG - 1, False)
            if LAST_STAGE >= 2:
                rank(0, 1)
                for g in range(GROUPS):
                    experts0(g)
            if LAST_STAGE >= 3:
                pe.wait_ge(att1_loaded, 16 * 7)
                pe.wait_ge(latbd_ready, 1)
                pe.wait_ge(att1_preset, 4)
                for g in range(GROUPS):
                    attention1(g)
                    if LAST_STAGE >= 4:
                        rank(1, g)
            if LAST_STAGE >= 4:
                for g in range(GROUPS):
                    experts1(g)


def _consts():
    import numpy as np
    c = np.zeros((P, NCONST), np.float32)
    p = np.arange(P)

    def put(name, value):
        c[:, COLS[name][0]:COLS[name][1]] = value

    put("ident", np.eye(P))
    inv = (1.0 / 10000.0 ** (np.arange(0, D, 2, dtype=np.float32) / D)).astype(np.float32)
    pos = (np.arange(Q)[:, None] * P + np.arange(KC)[None, :]).reshape(-1).astype(np.float32)
    ang = (pos[None, :] * inv[(p % D) // 2][:, None]).astype(np.float32)
    put("cos", np.cos(ang))
    put("sin", np.sin(ang) * np.where(p % 2 == 0, -1.0, 1.0)[:, None])
    put("headmask", (p[:, None] // D) == np.arange(H)[None, :])
    put("iota_e", np.arange(16)[None, :])
    put("iota_j", np.arange(ST)[None, :])
    e = np.arange(E0)
    put("below", (e[None, :] < e[:, None]).reshape(1, -1))
    put("ones", 1.0)
    put("before", p[:, None] < p[None, :])
    put("causal", np.where(p[None, :] <= p[:, None], 0.0, NEG))
    put("latmask", np.where(np.arange(KC)[None, :] <= (p % L)[:, None], 0.0, NEG))
    put("pairones", (p[:, None] // L) == np.arange(2)[None, :])
    return c


def kernel(**inputs):
    import numpy as np
    import concourse.bacc as bacc
    from concourse.bass_utils import run_bass_kernel_spmd

    i = {n: np.asarray(v) for n, v in inputs.items()}
    swap = np.arange(C) ^ 1
    arrays = {
        "const": _consts(),
        "L0_attn_x": i["L0_attn_x"],
        "qkvw": np.stack([i["L0_attn_Qw"], i["L0_attn_Kw"], i["L0_attn_Vw"]], axis=1),
        "qkb": np.stack([i["L0_attn_Qb"], i["L0_attn_Kb"]], axis=1),
        "L0_attn_Vb": i["L0_attn_Vb"],
        "L0_ffn_Wr": i["L0_ffn_Wr"],
        "wk1": np.stack([i["L1_attn_W_k"].T, i["L1_attn_W_k"].T[:, swap]], axis=1),
        "wv1": i["L1_attn_W_v"].T,
        "wg1": i["L1_attn_W_g"].T,
        "wp1": i["L1_attn_W_p"].T,
        "lat": i["L1_attn_latent_queries"][0].transpose(1, 2, 0).reshape(C, L),
        "L1_ffn_Wg": i["L1_ffn_Wg"],
        "L1_ffn_bg": i["L1_ffn_bg"],
        "w1": i["L1_ffn_W1"].transpose(1, 0, 2),
        "w2": i["L1_ffn_W2"].reshape(E1, HC1, P, C).transpose(2, 0, 1, 3),
        "L1_ffn_b1": i["L1_ffn_b1"],
        "L1_ffn_b2": i["L1_ffn_b2"],
        "wgu": np.concatenate([i["L0_ffn_Wg"], i["L0_ffn_Wu"]], axis=2).transpose(1, 0, 2),
        "wd_a": i["L0_ffn_Wd"][:, :2 * P].reshape(E0, 2, P, C).transpose(2, 0, 1, 3),
        "wd_b": i["L0_ffn_Wd"][:, 2 * P:].transpose(1, 0, 2),
    }
    arrays = {n: np.ascontiguousarray(v) for n, v in arrays.items()}
    nc = bacc.Bacc("TRN2", target_bir_lowering=False, num_devices=1)
    a = {n: nc.dram_tensor("in_" + n, v.shape, mybir.dt.from_np(v.dtype), kind="ExternalInput").ap()
         for n, v in arrays.items()}
    out = nc.dram_tensor("out", (B, T, C), F32, kind="ExternalOutput").ap()
    build(nc, a, out)
    got = run_bass_kernel_spmd(nc, [{"in_" + n: v for n, v in arrays.items()}], core_ids=[0])
    return got.results[0]["out"]
```

```python
from contextlib import ExitStack

import concourse.bass as bass
from concourse import mybir

F32 = mybir.dt.float32
BF16 = mybir.dt.bfloat16
I32 = mybir.dt.int32
U32 = mybir.dt.uint32
ALU = mybir.AluOpType
ACT = mybir.ActivationFunctionType
X = mybir.AxisListType.X

P = 128
B, T, C = 8, 512, 128
TILES = B * T // P
Q = T // P
GROUPS = 2
BG = B // GROUPS
TG = BG * Q
EPS = 1e-5
NEG = -1e30
SCALE0 = float(C) ** -0.5

E0, I0, K0 = 9, 352, 2
E1, I1, K1 = 8, 512, 1
HC0, HC1 = -(-I0 // P), I1 // P
CH = 4


def slot_tiles(experts, k):
    rows = k * TG * P
    most = (rows - experts) // P + experts
    return -(-most // CH) * CH


ST0, ST1 = slot_tiles(E0, K0), slot_tiles(E1, K1)
ST = max(ST0, ST1)

H, L = 16, 64
D = C // H
HP = H // 2
KC = 64
SCALE1 = float(D) ** -0.5
VW = 2 * D + 1
GW = 2 * D + 2

COLS, _at = {}, 0
for _name, _n in (("ident", P), ("cos", Q * KC), ("sin", Q * KC), ("headmask", H), ("iota_e", 16),
                  ("iota_j", ST), ("below", 81), ("ones", P), ("before", P), ("causal", P),
                  ("latmask", KC), ("pairones", 2)):
    COLS[_name] = (_at, _at + _n)
    _at += _n
NCONST = _at


NEWTON = 3
LN_STEPS = 3 * NEWTON + 3


def after(engine, semaphore, n):
    if not (isinstance(n, int) and n < 1):
        engine.wait_ge(semaphore, n)


def build(nc, a, out):
    ctx = ExitStack()
    with ctx:
        def sb(name, shape, dt=F32):
            return ctx.enter_context(nc.sbuf_tensor(name, shape, dt))

        def ps(name, shape, dt=F32):
            return ctx.enter_context(nc.psum_tensor(name, shape, dt))

        def sem(name):
            return ctx.enter_context(nc.semaphore(name))

        x = sb("x", [P, TILES, C])
        rows = sb("rows", [P, TILES, C])
        const = sb("const", [P, NCONST])

        def cst(name):
            return const[:, COLS[name][0]:COLS[name][1]]

        ident = cst("ident")
        cbf = sb("cbf", [P, 4 * P + KC], BF16)
        ident_bf, ones_bf, before_bf, causal_bf = (cbf[:, n * P:(n + 1) * P] for n in range(4))
        latmask_bf = cbf[:, 4 * P:4 * P + KC]
        qkvw = sb("qkvw", [P, 3, C])
        qkb = sb("qkb", [P, 2])
        vb = sb("vb", [P, C])
        work = sb("work", [P, 8 * T])
        xnT, qT, kT, v = (work[:, n * T:(n + 1) * T] for n in range(4))
        xn2 = sb("xn2", [P, Q, C])
        scratch = sb("scratch", [P, 1])
        xn = sb("xn", [P, Q, C])
        bn = sb("bn", [P, 2 * Q, 6])
        mv = sb("mv", [P, 2 * Q, 2])
        var, root, square, shift = (sb(n, [P, 2 * Q]) for n in ("var", "root", "square", "shift"))
        prob = work[:, 4 * T:6 * T].rearrange("p (n t) -> p n t", n=2)
        probT = work[:, 6 * T:8 * T].rearrange("p (n t) -> p n t", n=2)
        mx = sb("mx", [P, Q])
        nmx = sb("nmx", [P, Q])
        rsum = sb("rsum", [P, Q])
        rinv = sb("rinv", [P, Q])
        x2T = sb("x2T", [P, T])
        wr = sb("wr", [P, E0])
        logits = sb("logits", [P, TILES, E0])
        wr1 = sb("wr1", [P, E1])
        br1 = sb("br1", [P, E1])
        logits1 = sb("logits1", [P, TILES, E1])
        wk1 = sb("wk1", [P, 2, C])
        wv1 = sb("wv1", [P, C])
        wg1 = sb("wg1", [P, H * L])
        wp1 = sb("wp1", [P, C])
        lat = sb("lat", [P, L])
        latbd = sb("latbd", [P, H, L])
        xT1 = work[:, 5 * 512:6 * 512]
        xTn = sb("xTn", [P, T])
        xkT = work[:, 7 * 512:7 * 512 + Q * KC]
        turned = work[:, 6 * 512:7 * 512].rearrange("p (n k) -> p n k", n=2)
        kT1 = sb("kT1", [P, Q * KC])
        vbd = sb("vbd", [P, 2, HP, 2, VW])
        ex = work[:, 0:3 * 512].rearrange("p (n t) -> p n t", n=3)
        exT = work[:, 3 * 512:5 * 512].rearrange("p (n t) -> p n t", n=2)
        umax = sb("umax", [P, 3, 8])
        chunk_inv = sb("chunk_inv", [P, 2, Q])
        chunk_out = sb("chunk_out", [P, 2, Q, 2 * D])
        attbd = sb("attbd", [P, HP, GW])
        gate_inv = sb("gate_inv", [P, HP, 2])
        mixed = sb("mixed", [P, HP, 2, D])
        mixedT = sb("mixedT", [P, P])

        below = cst("below").rearrange("p (e f) -> p e f", e=E0)
        rt_ge = sb("rt_ge", [P, TG, E0])
        rt_cand = sb("rt_cand", [P, TG, E0])
        rt_second = sb("rt_second", [P, TG, E0])
        rt_sel = sb("rt_sel", [P, K0, TG, E0])
        rt_selbf = sb("rt_selbf", [P, TG, E0], BF16)
        rt_pos = sb("rt_pos", [P, TG, E0])
        rt_prod = sb("rt_prod", [P, TG, E0])
        rt_max = sb("rt_max", [P, 3, TG])
        rt_gap = sb("rt_gap", [P, TG, E0])
        rt_den = sb("rt_den", [P, TG])
        rt_tiles = sb("rt_tiles", [P, E0], I32)
        rt_base = sb("rt_base", [P, E0])
        rt_end = sb("rt_end", [P, E0])
        rt_below = sb("rt_below", [P, E0, E0])
        rt_past = sb("rt_past", [P, ST, E0])
        rt_tile_e = sb("rt_tile_e", [P, ST])
        rt_posf = sb("rt_posf", [P, K0 * TG])
        rt_int = sb("rt_int", [P, 4, K0 * TG], I32)
        slot = [[sb(f"slot{n}{g}", [P, k, TG], U32) for g in range(GROUPS)] for n, k in ((0, K0), (1, K1))]
        weight = [[sb(f"weight{n}{g}", [P, k, TG]) for g in range(GROUPS)] for n, k in ((0, K0), (1, K1))]
        tile_e = [[sb(f"tile_e{n}{g}", [P, ST], I32) for g in range(GROUPS)] for n in (0, 1)]
        expert_w = sb("expert_w", [P, E0 * (2 * I0 + HC0 * C)])
        wgu = expert_w[:, 0:E0 * 2 * I0].rearrange("p (e n) -> p e n", e=E0)
        wd = expert_w[:, E0 * 2 * I0:].rearrange("p (e j c) -> p e j c", e=E0, j=HC0)
        w1 = expert_w[:, 0:E1 * I1].rearrange("p (e n) -> p e n", e=E1)
        w2 = expert_w[:, E1 * I1:2 * E1 * I1].rearrange("p (e j c) -> p e j c", e=E1, j=HC1)
        b1 = sb("b1", [P, E1, I1])
        b2 = sb("b2", [P, E1, C])
        zeros = sb("zeros", [P, CH * C])
        xs = sb("xs", [P, CH, C])
        xsT = sb("xsT", [P, CH * P])
        act_out = sb("act_out", [P, 2, 512])
        hid = sb("hid", [P, 2, 512])
        hidT = sb("hidT", [P, 2, 512])
        ysb = sb("ysb", [P, ST, C])
        fetched = sb("fetched", [P, TILES, C])
        back = [rows, fetched]

        xs_dram = [nc.dram_tensor(f"xs_dram{g}", (ST * P, C), F32, kind="Internal").ap() for g in range(GROUPS)]
        ys_dram = [nc.dram_tensor(f"ys_dram{g}", (ST * P, C), F32, kind="Internal").ap() for g in range(GROUPS)]
        xs_chunk = [t.rearrange("(c p t) h -> p c (t h)", p=P, t=CH) for t in xs_dram]
        ys_chunk = [t.rearrange("(c p t) h -> p c (t h)", p=P, t=CH) for t in ys_dram]

        bank = [ps(f"bank{n}", [P, 512]) for n in range(8)]
        bX, bQV, bK, bPT = bank[0], bank[1], bank[2], bank[5]
        bO = [bank[6], bank[7]]
        bS = [bank[3], bank[4]]
        bRank = bank[7]
        bU1, bT1, bO1 = [bank[1], bank[2], bank[3]], [bank[4], bank[5]], [bank[6], bank[7]]
        bG, bU, bHT, bY = [bank[1], bank[2]], [bank[3], bank[4]], bank[5], [bank[6], bank[7]]

        x_loaded = sem("x_loaded")
        const_loaded = sem("const_loaded")
        attw_loaded = sem("attw_loaded")
        const_cast = sem("const_cast")
        ln_stats, ln_step = sem("ln_stats"), sem("ln_step")
        xn_ready = sem("xn_ready")
        xnT_psum, xnT_ready = sem("xnT_psum"), sem("xnT_ready")
        q_psum, q_ready = sem("q_psum"), sem("q_ready")
        k_psum, k_ready = sem("k_psum"), sem("k_ready")
        v_psum, v_ready = sem("v_psum"), sem("v_ready")
        s_psum = sem("s_psum")
        max_step = sem("max_step")
        exp_done = sem("exp_done")
        pt_psum, pt_ready = sem("pt_psum"), sem("pt_ready")
        o_psum = sem("o_psum")
        rinv_done = sem("rinv_done")
        attn_added = sem("attn_added")
        rows_ready = sem("rows_ready")
        rows_kept = sem("rows_kept")
        x2T_psum, x2T_ready = sem("x2T_psum"), sem("x2T_ready")
        lg_psum, lg_ready = sem("lg_psum"), sem("lg_ready")
        out_stored = sem("out_stored")
        route_step = sem("route_step")
        chosen = sem("chosen")
        rank_psum = sem("rank_psum")
        gap_ready, gap_exp = sem("gap_ready"), sem("gap_exp")
        routed = sem("routed")
        zeros_ready, zero_filled = sem("zeros_ready"), sem("zero_filled")
        ffn0_loaded = sem("ffn0_loaded")
        scattered = [sem(f"scattered{g}") for g in range(GROUPS)]
        fetched_back = [sem(f"fetched_back{g}") for g in range(GROUPS)]
        xs_loaded, xs_psum, xsT_ready = sem("xs_loaded"), sem("xs_psum"), sem("xsT_ready")
        up_psum = sem("up_psum")
        silu_done, hid_ready = sem("silu_done"), sem("hid_ready")
        hidT_psum, hidT_ready = sem("hidT_psum"), sem("hidT_ready")
        y_psum, y_ready, y_stored = sem("y_psum"), sem("y_ready"), sem("y_stored")
        combined = sem("combined")
        att1_loaded, ffn1_loaded = sem("att1_loaded"), sem("ffn1_loaded")
        att1_zeroed, att1_preset, latbd_ready = sem("att1_zeroed"), sem("att1_preset"), sem("latbd_ready")
        key_psum, key_turned, kT1_ready = sem("key_psum"), sem("key_turned"), sem("kT1_ready")
        val_psum, val_ready = sem("val_psum"), sem("val_ready")
        unit_psum, unit_max, unit_sub, unit_exp = (sem("unit_" + n) for n in ("psum", "max", "sub", "exp"))
        exT_psum, exT_ready, unit_used = sem("exT_psum"), sem("exT_ready"), sem("unit_used")
        att_step = sem("att_step")
        gate_inverted, mixed_ready = sem("gate_inverted"), sem("mixed_ready")
        mixedT_psum, mixedT_ready = sem("mixedT_psum"), sem("mixedT_ready")
        proj_psum, proj_added = sem("proj_psum"), sem("proj_added")
        bias_added = sem("bias_added")
        xkT_ready = sem("xkT_ready")
        xT1_ready = sem("xT1_ready")

        credited = [xnT_psum, lg_psum, x2T_psum, rows_kept, o_psum, pt_psum, exp_done,
                    pt_ready, attn_added, v_ready, k_ready, lg_ready, unit_used, exT_psum,
                    exT_ready, unit_sub, mixedT_psum, proj_psum, proj_added, mixed_ready]

        x_dram = a["L0_attn_x"].rearrange("b (i p) c -> p b i c", p=P)
        out_dram = out.rearrange("b (i p) c -> p b i c", p=P)
        xb = x[:, :, :].rearrange("p (b i) c -> p b i c", b=B)
        rowsb = rows[:, :, :].rearrange("p (b i) c -> p b i c", b=B)
        logitsb = logits[:, :, :].rearrange("p (b i) e -> p b i e", b=B)

        logits1b = logits1[:, :, :].rearrange("p (b i) e -> p b i e", b=B)

        def quad(b):
            return xb[:, bass.ds(b, 1), :, :].rearrange("p a i c -> p (a i) c")

        UNITS = 12

        def unit(b, u):
            return (b, u) if u >= 0 else (b - 1, u + UNITS)

        NT, K_OF = [ST0, ST1], [K0, K1]

        def tile0(n, g):
            return GROUPS * ST0 * n + NT[n] * g

        def chunk0(n, g):
            return tile0(n, g) // CH

        def experts_of(engine, n, g, c, first):
            lead = 0 if first else 2
            table = tile_e[n][g][0:1, bass.ds(c * CH - lead, CH + lead)]
            _, values = nc.values_load_multi_w_load_instructions(
                table, engines=[engine], min_val=0, max_val=(E0, E1)[n] - 1,
                skip_runtime_bounds_check_because="routing clamps the table to the experts")
            return {t - lead: v for t, v in enumerate(values)}

        def LnCall(n, last, ahead):
            return n, 0 if ahead else Q, 2 * Q if last else Q

        LN1 = B + 2

        block = ctx.enter_context(nc.Block())

        @block.sync
        def _(sp):
            for s in credited:
                sp.sem_inc(s, 1)
            sp.dma_start(quad(0), x_dram[:, 0, :, :]).then_inc(x_loaded, 16)
            with sp.Fori(1, B) as b:
                sp.wait_ge(x_loaded, 16 * b)
                sp.dma_start(quad(b), x_dram[:, bass.ds(b, 1), :, :].rearrange("p a i c -> p (a i) c")).then_inc(x_loaded, 16)
            sp.wait_ge(zeros_ready, 1)
            for g in range(GROUPS):
                for c in range(ST // CH):
                    sp.dma_start(xs_chunk[g][:, c, :], zeros[:, :]).then_inc(zero_filled, 16)
            sp.dma_start(wgu[:, :, :], a["wgu"]).then_inc(ffn0_loaded, 16)
            sp.dma_start(wd[:, :, 0:2, :], a["wd_a"]).then_inc(ffn0_loaded, 16)
            sp.dma_start(wd[0:I0 - 2 * P, :, 2, :], a["wd_b"]).then_inc(ffn0_loaded, 16)
            for dst, name in ((wk1, "wk1"), (wv1, "wv1"), (wg1, "wg1"), (wp1, "wp1"), (lat, "lat"), (wr1, "L1_ffn_Wg")):
                sp.dma_start(dst[:], a[name]).then_inc(att1_loaded, 16)
            sp.dma_start(br1[:, :], a["L1_ffn_bg"].partition_broadcast(P)).then_inc(att1_loaded, 16)
            sp.dma_start(b1[:, :, :], a["L1_ffn_b1"].partition_broadcast(P)).then_inc(ffn1_loaded, 16)
            sp.dma_start(b2[:, :, :], a["L1_ffn_b2"].partition_broadcast(P)).then_inc(ffn1_loaded, 16)

            def keep_rows(n, b):
                sp.wait_ge(rows_ready, b + B * n + 1)
                sp.dma_start(rowsb[:, bass.ds(b, 1), :, :].rearrange("p a i c -> p (a i) c"),
                             xn2[:, :, :]).then_inc(rows_kept, 16)

            def pass_on(b):
                sp.wait_ge(unit_psum, UNITS * b)
                sp.dma_start(xT1, xTn[:, :]).then_inc(xT1_ready, 16)

            def load_rows(n, g):
                sp.wait_ge(scattered[g], 16 * (K0 * TG + (K1 * TG if n else 0)))
                c0 = chunk0(n, g)
                after(sp, xs_psum, c0)
                sp.dma_start(xs[:, :, :].rearrange("p t h -> p (t h)"), xs_chunk[g][:, 0, :]).then_inc(xs_loaded, 16)
                with sp.Fori(1, NT[n] // CH) as c:
                    sp.wait_ge(xs_psum, c + c0)
                    sp.dma_start(xs[:, :, :].rearrange("p t h -> p (t h)"),
                                 xs_chunk[g][:, bass.ds(c, 1), :].rearrange("p a h -> p (a h)")).then_inc(xs_loaded, 16)

            with sp.Fori(0, B) as b:
                keep_rows(0, b)
            for g in range(GROUPS):
                load_rows(0, g)
            sp.wait_ge(y_psum, GROUPS * ST0)
            sp.dma_start(w1, a["w1"]).then_inc(ffn1_loaded, 16)
            sp.dma_start(w2, a["w2"]).then_inc(ffn1_loaded, 16)
            sp.wait_ge(xnT_ready, B + 1)
            sp.dma_start(xT1, xTn[:, :]).then_inc(xT1_ready, 16)
            sp.wait_ge(combined, 1)
            with sp.Fori(0, B - 1) as b:
                pass_on(b + 1)
                keep_rows(1, b)
            keep_rows(1, B - 1)
            for g in range(GROUPS):
                load_rows(1, g)
            for g in range(GROUPS):
                sp.wait_ge(combined, GROUPS + g + 1)
                sp.dma_start(out_dram[:, BG * g:BG * (g + 1), :, :], xb[:, BG * g:BG * (g + 1), :, :]).then_inc(out_stored, 16)
            sp.wait_ge(out_stored, 16 * GROUPS)

        @block.gpsimd
        def _(pool):
            nc.gpsimd.memset(zeros[:, :], 0.0).then_inc(zeros_ready, 1)

            def scatter(n, g):
                pool.wait_ge(routed, GROUPS * n + g + 1)
                pool.wait_ge(rows_kept, 1 + 16 * (B * n + BG * (g + 1)))
                if n == 0:
                    pool.wait_ge(zero_filled, 16 * GROUPS * (ST // CH))
                for t in range(TG):
                    for k in range(K_OF[n]):
                        nc.gpsimd.indirect_dma_start(
                            out=xs_dram[g][:, :],
                            out_offset=bass.IndirectOffsetOnAxis(ap=slot[n][g][:, k, t:t + 1], axis=0),
                            in_=rows[:, TG * g + t, :], in_offset=None).then_inc(scattered[g], 16)

            def fetch(n, g):
                pool.wait_ge(y_stored, 16 * (chunk0(n, g) + NT[n] // CH))
                if g == 0:
                    for h in range(GROUPS):
                        pool.wait_ge(scattered[h], 16 * (K0 * TG + (K1 * TG if n else 0)))
                for t in range(TG):
                    for k in range(K_OF[n]):
                        nc.gpsimd.indirect_dma_start(
                            out=back[g][:, k * TG + t, :], out_offset=None, in_=ys_dram[g][:, :],
                            in_offset=bass.IndirectOffsetOnAxis(ap=slot[n][g][:, k, t:t + 1], axis=0),
                        ).then_inc(fetched_back[g], 16)

            for g in range(GROUPS):
                scatter(0, g)
            for g in range(GROUPS):
                fetch(0, g)
            for g in range(GROUPS):
                scatter(1, g)
            for g in range(GROUPS):
                fetch(1, g)

        @block.scalar
        def _(act):
            act.dma_start(const[:, :], a["const"]).then_inc(const_loaded, 16)
            act.dma_start(qkvw[:, :, :], a["qkvw"]).then_inc(attw_loaded, 16)
            act.dma_start(qkb[:, :], a["qkb"]).then_inc(attw_loaded, 16)
            act.dma_start(vb[:, :], a["L0_attn_Vb"].partition_broadcast(P)).then_inc(attw_loaded, 16)
            act.dma_start(wr[:, :], a["L0_ffn_Wr"]).then_inc(attw_loaded, 16)

            def normalise(n, b, dst, first):
                act.wait_ge(ln_step, LN_STEPS * (n + 1))
                for i in range(Q):
                    xt = xb[:, bass.ds(b, 1), i, :].rearrange("p a c -> p (a c)")
                    j = first + i
                    ins = nc.scalar.activation(dst[:, i, :], xt, ACT.Identity, bias=shift[:, j:j + 1],
                                               scale=root[:, j:j + 1])
                return ins

            def normalise_next(n, b, m):
                after(act, xnT_psum, 1 + m)
                normalise(n, b, xn, 0).then_inc(xn_ready, 1)

            def normalise_last(n, b, m):
                after(act, x2T_psum, 1 + m)
                after(act, rows_kept, 1 + 16 * m)
                normalise(n, b, xn2, Q).then_inc(rows_ready, 1)

            def evac_xnT(b):
                act.wait_ge(xnT_psum, 1 + b + 1)
                nc.scalar.activation(xnT[:, :], bX[:, :], ACT.Copy).then_inc(xnT_ready, 1)

            def evac_q(b):
                act.wait_ge(q_psum, b + 1)
                nc.scalar.activation(qT[:, :], bQV[:, :], ACT.Identity, bias=qkb[:, 0:1]).then_inc(q_ready, 1)

            def evac_k(b):
                act.wait_ge(k_psum, b + 1)
                nc.scalar.activation(kT[:, :], bK[:, :], ACT.Identity, bias=qkb[:, 1:2]).then_inc(k_ready, 1)

            def exp_scores(b, i):
                act.wait_ge(max_step, 2 * (Q * b + i + 1))
                after(act, pt_psum, 1 + Q * b + i - 1)
                nc.scalar.activation(prob[:, i % 2, 0:(i + 1) * P], bS[i % 2][:, 0:(i + 1) * P], ACT.Exp,
                                     bias=nmx[:, i:i + 1], scale=SCALE0,
                                     accum_out=rsum[:, i:i + 1]).then_inc(exp_done, 1)

            def evac_x2T(b):
                act.wait_ge(x2T_psum, 1 + b + 1)
                after(act, lg_psum, 1 + b)
                nc.scalar.activation(x2T[:, :], bX[:, :], ACT.Copy).then_inc(x2T_ready, 1)

            def sequence0(b, last=True, ahead=True):
                exp_scores(b, 0)
                exp_scores(b, 1)
                exp_scores(b, 2)
                if ahead:
                    normalise_next(b + 1, b + 1, b + 1)
                exp_scores(b, 3)
                if ahead:
                    evac_xnT(b + 1)
                if last:
                    normalise_last(b + 1, b - 1, b - 1)
                if ahead:
                    evac_q(b + 1)
                if last:
                    evac_x2T(b - 1)
                if ahead:
                    evac_k(b + 1)

            def attention0():
                act.wait_ge(attw_loaded, 16 * 4)
                normalise_next(0, 0, 0)
                evac_xnT(0)
                evac_q(0)
                evac_k(0)
                sequence0(0, last=False)
                with act.Fori(1, BG) as b:
                    sequence0(b)
                sequence0(BG)
                route_exp(0, 0)
                with act.Fori(BG + 1, B - 1) as b:
                    sequence0(b)
                sequence0(B - 1, ahead=False)
                normalise_last(B + 1, B - 1, B - 1)
                evac_x2T(B - 1)
                route_exp(0, 1)

            def route_exp(n, g):
                act.wait_ge(gap_ready, GROUPS * n + g + 1)
                gap = rt_gap[:, :, 0:1] if n == 0 else rt_gap[:, :, 0:E1]
                nc.scalar.activation(gap, gap, ACT.Exp).then_inc(gap_exp, 1)

            def evac_xs(c):
                act.wait_ge(xs_psum, c + 1)
                after(act, up_psum, CH * c)
                nc.scalar.activation(xsT[:, :], bX[:, :], ACT.Copy).then_inc(xsT_ready, 1)

            def silu0(m, t):
                act.wait_ge(up_psum, m + 1)
                after(act, hid_ready, m - 1)
                nc.scalar.activation(act_out[:, t % 2, 0:I0], bG[t % 2][:, 0:I0], ACT.Silu).then_inc(silu_done, 1)

            def evac_y(m, ml, t):
                act.wait_ge(y_psum, m + 1)
                nc.scalar.activation(ysb[:, bass.ds(ml, 1), :].rearrange("p a c -> p (a c)"), bY[t % 2][:, 0:C],
                                     ACT.Copy).then_inc(y_ready, 1)

            def store_y(n, g, c):
                act.wait_ge(y_ready, CH * (c + 1) + tile0(n, g))
                act.dma_start(ys_chunk[g][:, bass.ds(c, 1), :].rearrange("p a h -> p (a h)"),
                              ysb[:, bass.ds(c * CH, CH), :].rearrange("p t h -> p (t h)")).then_inc(y_stored, 16)

            def experts0(g):
                m0, c0, nch = tile0(0, g), chunk0(0, g), NT[0] // CH

                def chunk(c, first=False, last=False):
                    for t in range(CH):
                        m = c * CH + t
                        silu0(m + m0, t)
                        if t == 3 and not last:
                            evac_xs(c + c0 + 1)
                        if not (first and t < 2):
                            evac_y(m + m0 - 2, m - 2, t)
                        if t == 1 and not first:
                            store_y(0, g, c - 1)

                evac_xs(c0)
                after(act, y_stored, 16 * c0)
                chunk(0, first=True)
                with act.Fori(1, nch - 1) as c:
                    chunk(c)
                chunk(nch - 1, last=True)
                for t in (2, 3):
                    m = (nch - 1) * CH + t
                    evac_y(m + m0, m, t)
                store_y(0, g, nch - 1)

            def exp_unit(b, u):
                n = UNITS * b + u
                act.wait_ge(unit_sub, 1 + n + 1)
                nc.scalar.activation(ex[:, u % 3, :], ex[:, u % 3, :], ACT.Exp, scale=SCALE1).then_inc(unit_exp, 1)

            def evac_exT(b, u):
                n = UNITS * b + u
                act.wait_ge(exT_psum, 1 + n + 1)
                after(act, unit_used, 1 + n - 1)
                nc.scalar.activation(exT[:, u % 2, :], bT1[u % 2][:, :], ACT.Copy).then_inc(exT_ready, 1)

            def evac_mixedT(b, t):
                act.wait_ge(mixedT_psum, 1 + Q * b + t + 1)
                after(act, proj_psum, 1 + Q * b + t)
                nc.scalar.activation(mixedT[:, :], bO1[1][:, 0:P], ACT.Copy).then_inc(mixedT_ready, 1)

            def evac_xTn(b):
                act.wait_ge(xnT_psum, 1 + B + b + 1)
                nc.scalar.activation(xkT.rearrange("p (n c) -> p n c", n=Q),
                                     bX[:, :].rearrange("p (n c) -> p n c", n=Q)[:, :, 0:KC], ACT.Copy).then_inc(xkT_ready, 1)
                after(act, xT1_ready, 16 * b)
                nc.scalar.activation(xTn[:, :], bX[:, :], ACT.Copy).then_inc(xnT_ready, 1)

            def evac_values(b):
                act.wait_ge(val_psum, b + 1)
                for n in range(2):
                    r = slice(n * KC, (n + 1) * KC)
                    nc.scalar.activation(vbd[r, :, :, n, 0:2 * D],
                                         bX[r, 0:2 * C].rearrange("p (u h d) -> p u h d", u=2, h=HP),
                                         ACT.Copy).then_inc(val_ready, 1)

            def attention1_sequence(b, last=True, ahead=True):
                for s in range(UNITS):
                    if s in (1, 3) and last:
                        evac_mixedT(b - 1, 2 + s // 2)
                    if s in (9, 11):
                        evac_mixedT(b, s // 2 - 4)
                    if last or s >= 2:
                        evac_exT(*unit(b, s - 2))
                    if s == 8 and last:
                        evac_x2T(B + b - 1)
                    exp_unit(b, s)
                    if s == 6 and last:
                        normalise_last(LN1 + b + 1, b - 1, B + b - 1)
                    if s == 7 and ahead:
                        normalise_next(LN1 + b + 1, b + 1, B + b + 1)
                    if s == 9 and ahead:
                        evac_xTn(b + 1)
                    if s == 11 and ahead:
                        evac_values(b + 1)

            def attention1():
                normalise_next(LN1, 0, B)
                evac_xTn(0)
                evac_values(0)
                attention1_sequence(0, last=False)
                with act.Fori(1, BG) as b:
                    attention1_sequence(b)
                attention1_sequence(BG)
                route_exp(1, 0)
                with act.Fori(BG + 1, B - 1) as b:
                    attention1_sequence(b)
                attention1_sequence(B - 1, ahead=False)
                for s in range(4):
                    if s % 2:
                        evac_mixedT(B - 1, 2 + s // 2)
                    if s < 2:
                        evac_exT(B - 1, UNITS - 2 + s)
                normalise_last(LN1 + B + 1, B - 1, 2 * B - 1)
                evac_x2T(2 * B - 1)
                route_exp(1, 1)

            def silu1(m, t):
                act.wait_ge(bias_added, m - tile0(1, 0) + 1)
                act.wait_ge(hidT_psum, m - 1)
                nc.scalar.activation(hid[:, t % 2, :], act_out[:, t % 2, :], ACT.Silu).then_inc(hid_ready, 1)

            def evac_hidT1(m, t):
                act.wait_ge(hidT_psum, m + 1)
                act.wait_ge(y_psum, m - 1)
                nc.scalar.activation(hidT[:, t % 2, :], bHT[:, :], ACT.Copy).then_inc(hidT_ready, 1)

            def experts1(g):
                m0, c0, nch = tile0(1, g), chunk0(1, g), NT[1] // CH

                def chunk(c, first=False, last=False):
                    for t in range(CH):
                        m = c * CH + t
                        silu1(m + m0, t)
                        if not (first and t < 1):
                            evac_hidT1(m + m0 - 1, t - 1)
                        if t == 3 and not last:
                            evac_xs(c + c0 + 1)
                        if t == 2 and not first:
                            store_y(1, g, c - 1)

                evac_xs(c0)
                chunk(0, first=True)
                with act.Fori(1, nch - 1) as c:
                    chunk(c)
                chunk(nch - 1, last=True)
                evac_hidT1(nch * CH - 1 + m0, 3)
                store_y(1, g, nch - 1)

            attention0()
            for g in range(GROUPS):
                experts0(g)
            attention1()
            for g in range(GROUPS):
                experts1(g)

        @block.vector
        def _(dve):
            dve.wait_ge(const_loaded, 16)
            for n, name in enumerate(("ident", "ones", "before", "causal")):
                nc.vector.tensor_copy(cbf[:, n * P:(n + 1) * P], cst(name)).then_inc(const_cast, 1)
            nc.vector.tensor_copy(latmask_bf, cst("latmask")).then_inc(const_cast, 1)

            def take_wait():
                nc.vector.memset(scratch[:, :], 0.0)

            def statistics(call, src_next, src_last):
                n, lo, hi = call
                take_wait()
                for j in range(lo, hi):
                    src = quad(src_next) if j < Q else quad(src_last)
                    ins = nc.vector.bn_stats(bn[:, j, :], src[:, j % Q, :])
                ins.then_inc(ln_stats, 1)

            def aggregate(call):
                n, lo, hi = call
                dve.wait_ge(ln_stats, 2 * n + 1)
                take_wait()
                for j in range(lo, hi):
                    ins = nc.vector.bn_aggr(mv[:, j, :], bn[:, j, :])
                ins.then_inc(ln_stats, 1)

            def guess_root(call):
                n, lo, hi = call
                dve.wait_ge(ln_stats, 2 * n + 2)
                nc.vector.tensor_scalar(var[:, lo:hi], mv[:, lo:hi, 1], EPS, None, ALU.add).then_inc(ln_step, 1)
                dve.wait_ge(ln_step, LN_STEPS * n + 1)
                nc.vector.tensor_scalar(root[:, lo:hi].bitcast(I32), var[:, lo:hi].bitcast(I32), -0.5,
                                        float(0x5F3759DF), ALU.mult, ALU.add).then_inc(ln_step, 1)

            def refine(call, step):
                n, lo, hi = call
                done = LN_STEPS * n + 2 + 3 * step
                r, q = root[:, lo:hi], square[:, lo:hi]
                dve.wait_ge(ln_step, done)
                nc.vector.tensor_tensor(q, r, r, ALU.mult).then_inc(ln_step, 1)
                dve.wait_ge(ln_step, done + 1)
                nc.vector.scalar_tensor_tensor(out=q, in0=q, scalar=-0.5, in1=var[:, lo:hi], op0=ALU.mult,
                                               op1=ALU.mult).then_inc(ln_step, 1)
                dve.wait_ge(ln_step, done + 2)
                nc.vector.scalar_tensor_tensor(out=r, in0=q, scalar=1.5, in1=r, op0=ALU.add,
                                               op1=ALU.mult).then_inc(ln_step, 1)

            def shift_mean(call):
                n, lo, hi = call
                dve.wait_ge(ln_step, LN_STEPS * (n + 1) - 1)
                nc.vector.scalar_tensor_tensor(out=shift[:, lo:hi], in0=mv[:, lo:hi, 0], scalar=-1.0,
                                               in1=root[:, lo:hi], op0=ALU.mult, op1=ALU.mult).then_inc(ln_step, 1)

            def normalisers(call):
                aggregate(call)
                guess_root(call)
                for step in range(NEWTON):
                    refine(call, step)
                shift_mean(call)

            def rowmax(b, i):
                dve.wait_ge(s_psum, Q * b + i + 1)
                nc.vector.tensor_reduce(mx[:, i:i + 1], bS[i % 2][:, 0:(i + 1) * P], X, ALU.max).then_inc(max_step, 1)
                dve.wait_ge(max_step, 2 * (Q * b + i) + 1)
                nc.vector.tensor_scalar(nmx[:, i:i + 1], mx[:, i:i + 1], -SCALE0, None, ALU.mult).then_inc(max_step, 1)

            def copy_pt(b, i):
                dve.wait_ge(pt_psum, 1 + Q * b + i + 1)
                after(dve, o_psum, 1 + Q * b + i - 1)
                nc.vector.tensor_copy(probT[:, i % 2, 0:(i + 1) * P], bPT[:, 0:(i + 1) * P]).then_inc(pt_ready, 1)

            def add_attn(b, i):
                dve.wait_ge(exp_done, 1 + Q * b + i + 1)
                nc.vector.reciprocal(rinv[:, i:i + 1], rsum[:, i:i + 1]).then_inc(rinv_done, 1)
                dve.wait_ge(rinv_done, Q * b + i + 1)
                dve.wait_ge(o_psum, 1 + Q * b + i + 1)
                xt = xb[:, bass.ds(b, 1), i, :].rearrange("p a c -> p (a c)")
                nc.vector.scalar_tensor_tensor(out=xt, in0=bO[i % 2][:, 0:C], scalar=rinv[:, i:i + 1],
                                               in1=xt, op0=ALU.mult, op1=ALU.add).then_inc(attn_added, 1)

            def evac_v(b):
                dve.wait_ge(v_psum, b + 1)
                nc.vector.tensor_tensor(v[:, :].rearrange("p (i c) -> p i c", i=Q),
                                        bQV[:, :].rearrange("p (i c) -> p i c", i=Q),
                                        vb[:, :].unsqueeze(1).to_broadcast([P, Q, C]), ALU.add).then_inc(v_ready, 1)

            def evac_logits0(b):
                dve.wait_ge(lg_psum, 1 + b + 1)
                nc.vector.tensor_copy(logitsb[:, bass.ds(b, 1), :, :].rearrange("p a i e -> p (a i) e"),
                                      bX[:, 0:Q * E0].rearrange("p (i e) -> p i e", i=Q)).then_inc(lg_ready, 1)

            def evac_logits1(b):
                dve.wait_ge(lg_psum, 1 + B + b + 1)
                nc.vector.tensor_tensor(logits1b[:, bass.ds(b, 1), :, :].rearrange("p a i e -> p (a i) e"),
                                        bX[:, 0:Q * E1].rearrange("p (i e) -> p i e", i=Q),
                                        br1[:, :].unsqueeze(1).to_broadcast([P, Q, E1]), ALU.add).then_inc(lg_ready, 1)

            def sequence0(b, last=True, ahead=True):
                rowmax(b, 0)
                rowmax(b, 1)
                if last or ahead:
                    call = LnCall(b + 1, last, ahead)
                    if ahead:
                        dve.wait_ge(x_loaded, 16 * b + 32)
                    if last:
                        dve.wait_ge(attn_added, 1 + Q * b)
                    statistics(call, b + 1, b - 1)
                copy_pt(b, 0)
                if last or ahead:
                    aggregate(call)
                    guess_root(call)
                rowmax(b, 2)
                if last or ahead:
                    refine(call, 0)
                copy_pt(b, 1)
                if last or ahead:
                    refine(call, 1)
                    refine(call, 2)
                    shift_mean(call)
                rowmax(b, 3)
                add_attn(b, 0)
                copy_pt(b, 2)
                add_attn(b, 1)
                copy_pt(b, 3)
                add_attn(b, 2)
                add_attn(b, 3)
                if ahead:
                    evac_v(b + 1)
                if last:
                    evac_logits0(b - 1)

            def attention0():
                call = LnCall(0, False, True)
                dve.wait_ge(x_loaded, 16)
                statistics(call, 0, 0)
                normalisers(call)
                dve.wait_ge(attw_loaded, 16 * 4)
                evac_v(0)
                sequence0(0, last=False)
                with dve.Fori(1, BG) as b:
                    sequence0(b)
                sequence0(BG)
                choose(0, 0)
                place(0, 0)
                weigh(0, 0)
                with dve.Fori(BG + 1, B - 1) as b:
                    sequence0(b)
                sequence0(B - 1, ahead=False)
                call = LnCall(B + 1, True, False)
                dve.wait_ge(attn_added, 1 + Q * B)
                statistics(call, 0, B - 1)
                normalisers(call)
                evac_logits0(B - 1)
                choose(0, 1)
                place(0, 1)
                weigh(0, 1)

            steps = [0]

            def then(ins):
                steps[0] += 1
                ins.then_inc(route_step, 1)
                dve.wait_ge(route_step, steps[0])

            def first_max(src, sel, top, E):
                ge, cand = rt_ge[:, :, 0:E], rt_cand[:, :, 0:E]
                iota = cst("iota_e")[:, 0:E].unsqueeze(1).to_broadcast([P, TG, E])
                then(nc.vector.tensor_reduce(top, src, X, ALU.max))
                then(nc.vector.tensor_tensor(ge, src, top.unsqueeze(2).to_broadcast([P, TG, E]), ALU.is_ge))
                then(nc.vector.scalar_tensor_tensor(out=cand, in0=ge, scalar=-16.0, in1=iota, op0=ALU.mult, op1=ALU.add))
                then(nc.vector.tensor_reduce(rt_max[:, 2, :], cand, X, ALU.min))
                then(nc.vector.tensor_tensor(sel, cand, rt_max[:, 2, :].unsqueeze(2).to_broadcast([P, TG, E]),
                                             ALU.is_equal))

            def choose(n, g):
                E = (E0, E1)[n]
                lg = (logits if n == 0 else logits1)[:, TG * g:TG * (g + 1), :]
                dve.wait_ge(lg_ready, 1 + B * n + BG * (g + 1))
                sel = rt_sel[:, :, :, 0:E]
                first_max(lg, sel[:, 0], rt_max[:, 0, :], E)
                if n == 0:
                    second = rt_second[:, :, :]
                    then(nc.vector.scalar_tensor_tensor(out=second, in0=sel[:, 0], scalar=NEG, in1=lg,
                                                        op0=ALU.mult, op1=ALU.add))
                    first_max(second, sel[:, 1], rt_max[:, 1, :], E)
                    nc.vector.tensor_tensor(rt_gap[:, :, 0], rt_max[:, 1, :], rt_max[:, 0, :],
                                            ALU.subtract).then_inc(gap_ready, 1)
                    nc.vector.tensor_tensor(rt_selbf[:, :, 0:E], sel[:, 0], sel[:, 1], ALU.add).then_inc(chosen, 1)
                else:
                    nc.vector.tensor_tensor(rt_gap[:, :, 0:E], lg, rt_max[:, 0, :].unsqueeze(2).to_broadcast([P, TG, E]),
                                            ALU.subtract).then_inc(gap_ready, 1)
                    nc.vector.tensor_copy(rt_selbf[:, :, 0:E], sel[:, 0]).then_inc(chosen, 1)

            def place(n, g):
                E, K, N = (E0, E1)[n], K_OF[n], NT[n]
                sel = rt_sel[:, :, :, 0:E]
                tiles, base, end = rt_tiles[:, 0:E], rt_base[:, 0:E], rt_end[:, 0:E]
                dve.wait_ge(rank_psum, GROUPS * n + g + 1)
                rank = bRank[:, 0:TG * E].rearrange("p (t e) -> p t e", e=E)
                then(nc.vector.tensor_scalar(tiles, bRank[:, TG * E:(TG + 1) * E], P - 1.0, None, ALU.add))
                then(nc.vector.tensor_scalar(tiles, tiles, 7, None, ALU.logical_shift_right))
                then(nc.vector.tensor_tensor(rt_below[:, 0:E, 0:E], below[:, 0:E, 0:E],
                                             tiles.unsqueeze(1).to_broadcast([P, E, E]), ALU.mult))
                then(nc.vector.tensor_reduce(base, rt_below[:, 0:E, 0:E], X, ALU.add))
                nc.vector.tensor_tensor(end, base, tiles, ALU.add)
                then(nc.vector.scalar_tensor_tensor(out=rt_pos[:, :, 0:E], in0=base.unsqueeze(1).to_broadcast([P, TG, E]),
                                                    scalar=float(P), in1=rank, op0=ALU.mult, op1=ALU.add))
                pos, hi, mid, lo = (rt_int[:, m, 0:K * TG] for m in range(4))
                for k in range(K):
                    then(nc.vector.tensor_tensor(rt_prod[:, :, 0:E], sel[:, k], rt_pos[:, :, 0:E], ALU.mult))
                    then(nc.vector.tensor_reduce(rt_posf[:, k * TG:(k + 1) * TG], rt_prod[:, :, 0:E], X, ALU.add))
                then(nc.vector.tensor_copy(pos, rt_posf[:, 0:K * TG]))
                nc.vector.tensor_scalar(hi, pos, ~(CH * P - 1) & 0x7FFFFFFF, None, ALU.bitwise_and)
                nc.vector.tensor_scalar(mid, pos, P - 1, 2, ALU.bitwise_and, ALU.logical_shift_left)
                then(nc.vector.tensor_scalar(lo, pos, 7, CH - 1, ALU.logical_shift_right, ALU.bitwise_and))
                then(nc.vector.tensor_tensor(hi, hi, mid, ALU.bitwise_or))
                then(nc.vector.tensor_tensor(slot[n][g][:, :, :].rearrange("p k t -> p (k t)").bitcast(I32), hi, lo,
                                             ALU.bitwise_or))
                past = rt_past[:, 0:N, 0:E]
                then(nc.vector.tensor_tensor(past, cst("iota_j")[:, 0:N].unsqueeze(2).to_broadcast([P, N, E]),
                                             end.unsqueeze(1).to_broadcast([P, N, E]), ALU.is_ge))
                then(nc.vector.tensor_reduce(rt_tile_e[:, 0:N], past, X, ALU.add))
                nc.vector.tensor_scalar(tile_e[n][g][:, 0:N], rt_tile_e[:, 0:N], E - 1.0, None, ALU.min).then_inc(routed, 1)

            def weigh(n, g):
                w = weight[n][g]
                dve.wait_ge(gap_exp, GROUPS * n + g + 1)
                if n == 0:
                    then(nc.vector.tensor_scalar(rt_den[:, :], rt_gap[:, :, 0], 1.0, None, ALU.add))
                    then(nc.vector.reciprocal(w[:, 0, :], rt_den[:, :]))
                    then(nc.vector.tensor_tensor(w[:, 1, :], rt_gap[:, :, 0], w[:, 0, :], ALU.mult))
                else:
                    then(nc.vector.tensor_reduce(rt_den[:, :], rt_gap[:, :, 0:E1], X, ALU.add))
                    then(nc.vector.reciprocal(w[:, 0, :], rt_den[:, :]))

            def gate0(m, t):
                dve.wait_ge(silu_done, m + 1)
                after(dve, hidT_psum, m - 1)
                nc.vector.tensor_tensor(hid[:, t % 2, 0:I0], act_out[:, t % 2, 0:I0], bU[t % 2][:, 0:I0],
                                        ALU.mult).then_inc(hid_ready, 1)

            def evac_hidT0(m, t):
                dve.wait_ge(hidT_psum, m + 1)
                after(dve, y_psum, m - 1)
                nc.vector.tensor_copy(hidT[:, t % 2, 0:HC0 * P], bHT[:, 0:HC0 * P]).then_inc(hidT_ready, 1)

            def experts0(g):
                m0, nch = tile0(0, g), NT[0] // CH

                def chunk(c, first=False):
                    for t in range(CH):
                        m = c * CH + t + m0
                        gate0(m, t)
                        if not (first and t < 1):
                            evac_hidT0(m - 1, t - 1)

                chunk(0, first=True)
                with dve.Fori(1, nch) as c:
                    chunk(c)
                evac_hidT0(nch * CH - 1 + m0, 3)

            def combine(n, g):
                dve.wait_ge(fetched_back[g], 16 * (K0 * TG + (K1 * TG if n else 0)))
                for k in range(K_OF[n]):
                    for t in range(TG):
                        xt = x[:, TG * g + t, :]
                        ins = nc.vector.scalar_tensor_tensor(out=xt, in0=back[g][:, k * TG + t, :],
                                                             scalar=weight[n][g][:, k, t:t + 1], in1=xt,
                                                             op0=ALU.mult, op1=ALU.add)
                    if k < K_OF[n] - 1:
                        then(ins)
                ins.then_inc(combined, 1)
                dve.wait_ge(combined, GROUPS * n + g + 1)

            def turn_keys(b):
                dve.wait_ge(key_psum, b + 1)
                nc.vector.tensor_tensor(turned[:, :, :].rearrange("p a k -> p (a k)"), bX[:, :],
                                        const[:, COLS["cos"][0]:COLS["sin"][1]], ALU.mult).then_inc(key_turned, 1)
                dve.wait_ge(key_turned, b + 1)
                nc.vector.tensor_tensor(kT1[:, :], turned[:, 0, :], turned[:, 1, :], ALU.add).then_inc(kT1_ready, 1)

            def shift_unit(b, u):
                n = UNITS * b + u
                dve.wait_ge(unit_psum, n + 1)
                unit = bU1[u % 3][:, :].rearrange("p (s k) -> p s k", s=8)
                nc.vector.tensor_reduce(umax[:, u % 3, :], unit, X, ALU.max).then_inc(unit_max, 1)
                dve.wait_ge(unit_max, n + 1)
                after(dve, exT_psum, 1 + n - 2)
                nc.vector.tensor_tensor(ex[:, u % 3, :].rearrange("p (s k) -> p s k", s=8), unit,
                                        umax[:, u % 3, :].unsqueeze(2).to_broadcast([P, 8, KC]),
                                        ALU.subtract).then_inc(unit_sub, 1)

            def sum_chunks(b, u):
                step = 3 * (Q * b + u)
                dve.wait_ge(unit_used, 1 + UNITS * b + u + 1)
                got = bO1[u % 2][:, 0:2 * Q * VW].rearrange("p (h n v) -> p h n v", h=2, n=Q)
                nc.vector.reciprocal(chunk_inv[:, :, :], got[:, :, :, 2 * D]).then_inc(att_step, 1)
                dve.wait_ge(att_step, step + 1)
                nc.vector.tensor_tensor(chunk_out[:, :, :, :], got[:, :, :, 0:2 * D],
                                        chunk_inv[:, :, :].unsqueeze(3).to_broadcast([P, 2, Q, 2 * D]),
                                        ALU.mult).then_inc(att_step, 1)
                dve.wait_ge(att_step, step + 2)
                after(dve, unit_used, 1 + UNITS * b)
                for n in range(2):
                    r = slice(n * L, (n + 1) * L)
                    ins = nc.vector.tensor_reduce(attbd[r, 2 * u:2 * u + 2, n * D:(n + 1) * D],
                                                  chunk_out[r, :, :, n * D:(n + 1) * D].rearrange("p h n d -> p h d n"),
                                                  X, ALU.add)
                ins.then_inc(att_step, 1)

            def normalise_gates(b, t):
                dve.wait_ge(unit_used, 1 + UNITS * b + 4 + 2 * t + 2)
                got = bO1[0][:, 0:HP * GW].rearrange("p (h v) -> p h v", h=HP)
                nc.vector.reciprocal(gate_inv[:, :, :], got[:, :, 2 * D:GW]).then_inc(gate_inverted, 1)
                dve.wait_ge(gate_inverted, Q * b + t + 1)
                after(dve, mixedT_psum, 1 + Q * b + t)
                nc.vector.tensor_tensor(mixed[:, :, :, :], got[:, :, 0:2 * D].rearrange("p h (k d) -> p h k d", k=2),
                                        gate_inv[:, :, :].unsqueeze(3).to_broadcast([P, HP, 2, D]),
                                        ALU.mult).then_inc(mixed_ready, 1)

            def add_projected(b, t):
                dve.wait_ge(proj_psum, 1 + Q * b + t + 1)
                xt = xb[:, bass.ds(b, 1), t, :].rearrange("p a c -> p (a c)")
                nc.vector.tensor_tensor(xt, xt, bO1[1][:, 0:C], ALU.add).then_inc(proj_added, 1)

            def attention1_sequence(b, last=True, ahead=True):
                call = LnCall(LN1 + b + 1, last, ahead)
                for s in range(UNITS):
                    if s == 9 and last:
                        evac_logits1(b - 1)
                    if s == 11 and ahead:
                        turn_keys(b + 1)
                    shift_unit(b, s)
                    if 0 <= s - 3 < 4:
                        sum_chunks(b, s - 3)
                    if s in (0, 2) and last:
                        normalise_gates(b - 1, 2 + s // 2)
                    if s in (8, 10):
                        normalise_gates(b, s // 2 - 4)
                    if s in (1, 3) and last:
                        add_projected(b - 1, 2 + s // 2)
                    if s in (9, 11):
                        add_projected(b, s // 2 - 4)
                    if s == 4 and (last or ahead):
                        if last:
                            dve.wait_ge(proj_added, 1 + Q * b)
                        statistics(call, b + 1, b - 1)
                        aggregate(call)
                    if s == 5 and (last or ahead):
                        guess_root(call)
                        refine(call, 0)
                        refine(call, 1)
                    if s == 6 and (last or ahead):
                        refine(call, 2)
                        shift_mean(call)

            def attention1():
                call = LnCall(LN1, False, True)
                statistics(call, 0, 0)
                normalisers(call)
                turn_keys(0)
                attention1_sequence(0, last=False)
                combine(0, 1)
                with dve.Fori(1, BG) as b:
                    attention1_sequence(b)
                attention1_sequence(BG)
                choose(1, 0)
                place(1, 0)
                weigh(1, 0)
                with dve.Fori(BG + 1, B - 1) as b:
                    attention1_sequence(b)
                attention1_sequence(B - 1, ahead=False)
                for s in range(4):
                    if s % 2 == 0:
                        normalise_gates(B - 1, 2 + s // 2)
                    else:
                        add_projected(B - 1, 2 + s // 2)
                call = LnCall(LN1 + B + 1, True, False)
                dve.wait_ge(proj_added, 1 + Q * B)
                statistics(call, 0, B - 1)
                normalisers(call)
                evac_logits1(B - 1)
                choose(1, 1)
                place(1, 1)
                weigh(1, 1)

            def bias1(e, mg, t):
                dve.wait_ge(up_psum, mg + 1)
                dve.wait_ge(hid_ready, mg - 1)
                nc.vector.tensor_tensor(act_out[:, t % 2, :], bG[t % 2][:, :],
                                        b1[:, bass.ds(e, 1), :].rearrange("p a n -> p (a n)"), ALU.add).then_inc(bias_added, 1)

            def evac_y1(e, m, mg, t):
                dve.wait_ge(y_psum, mg + 1)
                nc.vector.tensor_tensor(ysb[:, bass.ds(m, 1), :].rearrange("p a c -> p (a c)"), bY[t % 2][:, 0:C],
                                        b2[:, bass.ds(e, 1), :].rearrange("p a n -> p (a n)"), ALU.add).then_inc(y_ready, 1)

            def experts1(g):
                m0, nch = tile0(1, g), NT[1] // CH
                dve.wait_ge(y_stored, 16 * chunk0(1, g))
                dve.wait_ge(ffn1_loaded, 16 * 4)

                def chunk(c, first=False, last=False):
                    e = experts_of(mybir.EngineType.DVE, 1, g, c, first)
                    for t in range(CH):
                        m = c * CH + t
                        bias1(e[t], m + m0, t)
                        if not (first and t < 2):
                            evac_y1(e[t - 2], m - 2, m + m0 - 2, t)
                    return e

                chunk(0, first=True)
                with dve.Fori(1, nch - 1) as c:
                    chunk(c)
                e = chunk(nch - 1, last=True)
                for t in (2, 3):
                    m = nch * CH - CH + t
                    evac_y1(e[t], m, m + m0, t)

            nc.vector.memset(vbd[:], 0.0).then_inc(att1_zeroed, 1)
            nc.vector.memset(attbd[:], 0.0).then_inc(att1_zeroed, 1)
            dve.wait_ge(att1_zeroed, 2)
            for n in range(2):
                nc.vector.memset(vbd[n * KC:(n + 1) * KC, :, :, n, 2 * D:VW], 1.0).then_inc(att1_preset, 1)
                nc.vector.memset(attbd[n * L:(n + 1) * L, :, 2 * D + n:2 * D + n + 1], 1.0).then_inc(att1_preset, 1)
            attention0()
            for g in range(GROUPS):
                experts0(g)
            dve.wait_ge(att1_loaded, 16 * 7)
            nc.vector.tensor_tensor(latbd[:, :, :], lat[:, :].unsqueeze(1).to_broadcast([P, H, L]),
                                    cst("headmask").unsqueeze(2).to_broadcast([P, H, L]), ALU.mult).then_inc(latbd_ready, 1)
            combine(0, 0)
            attention1()
            for g in range(GROUPS):
                experts1(g)
            for g in range(GROUPS):
                combine(1, g)

        @block.tensor
        def _(pe):
            pe.wait_ge(const_cast, 5)
            pe.wait_ge(attw_loaded, 16 * 4)

            def t1(m):
                pe.wait_ge(xn_ready, m + 1)
                for i in range(Q):
                    ins = nc.tensor.transpose(bX[:, i * P:(i + 1) * P], xn[:, i, :], ident)
                ins.then_inc(xnT_psum, 1)

            def project_q(b):
                pe.wait_ge(xnT_ready, b + 1)
                after(pe, v_ready, 1 + b)
                nc.tensor.matmul(bQV[:, :], qkvw[:, 0, :], xnT[:, :], start=True, stop=True).then_inc(q_psum, 1)

            def project_k(b):
                nc.tensor.matmul(bK[:, :], qkvw[:, 1, :], xnT[:, :], start=True, stop=True).then_inc(k_psum, 1)

            def project_v(b):
                pe.wait_ge(q_ready, b + 1)
                for i in range(Q):
                    ins = nc.tensor.matmul(bQV[:, i * P:(i + 1) * P], xnT[:, i * P:(i + 1) * P], qkvw[:, 2, :],
                                           start=True, stop=True)
                ins.then_inc(v_psum, 1)

            def scores(b, i):
                if i == 0:
                    pe.wait_ge(k_ready, 1 + b + 1)
                after(pe, exp_done, 1 + Q * b + i - 1)
                nc.tensor.matmul(bS[i % 2][:, i * P:(i + 1) * P], ident_bf, causal_bf, start=True, stop=False,
                                 skip_group_check=True)
                nc.tensor.matmul(bS[i % 2][:, 0:(i + 1) * P], qT[:, i * P:(i + 1) * P], kT[:, 0:(i + 1) * P],
                                 start=False, stop=True, skip_group_check=True).then_inc(s_psum, 1)

            def pt(b, i):
                pe.wait_ge(exp_done, 1 + Q * b + i + 1)
                after(pe, pt_ready, 1 + Q * b + i)
                for j in range(i + 1):
                    ins = nc.tensor.transpose(bPT[:, j * P:(j + 1) * P], prob[:, i % 2, j * P:(j + 1) * P], ident)
                ins.then_inc(pt_psum, 1)

            def pv(b, i):
                pe.wait_ge(pt_ready, 1 + Q * b + i + 1)
                if i == 0:
                    pe.wait_ge(v_ready, 1 + b + 1)
                after(pe, attn_added, 1 + Q * b + i - 1)
                for j in range(i + 1):
                    ins = nc.tensor.matmul(bO[i % 2][:, 0:C], probT[:, i % 2, j * P:(j + 1) * P],
                                           v[:, j * C:(j + 1) * C],
                                           start=(j == 0), stop=(j == i))
                ins.then_inc(o_psum, 1)

            def t2(m):
                pe.wait_ge(rows_ready, m + 1)
                for i in range(Q):
                    ins = nc.tensor.transpose(bX[:, i * P:(i + 1) * P], xn2[:, i, :], ident)
                ins.then_inc(x2T_psum, 1)

            def route_logits(m, router, E):
                pe.wait_ge(x2T_ready, m + 1)
                for i in range(Q):
                    ins = nc.tensor.matmul(bX[:, i * E:(i + 1) * E], x2T[:, i * P:(i + 1) * P], router[:, :],
                                           start=True, stop=True)
                ins.then_inc(lg_psum, 1)

            def sequence0(b, last=True, ahead=True):
                scores(b, 0)
                scores(b, 1)
                pt(b, 0)
                scores(b, 2)
                pt(b, 1)
                pv(b, 0)
                scores(b, 3)
                pt(b, 2)
                pv(b, 1)
                if ahead:
                    after(pe, lg_ready, 1 + b - 1)
                    t1(b + 1)
                pt(b, 3)
                pv(b, 2)
                if last:
                    if ahead:
                        pe.wait_ge(xnT_ready, b + 2)
                    else:
                        pe.wait_ge(lg_ready, 1 + b - 1)
                    t2(b - 1)
                if ahead:
                    project_q(b + 1)
                pv(b, 3)
                if ahead:
                    project_k(b + 1)
                    project_v(b + 1)
                if last:
                    route_logits(b - 1, wr, E0)

            def attention0():
                t1(0)
                project_q(0)
                project_k(0)
                project_v(0)
                sequence0(0, last=False)
                with pe.Fori(1, BG) as b:
                    sequence0(b)
                sequence0(BG)
                rank(0, 0)
                with pe.Fori(BG + 1, B - 1) as b:
                    sequence0(b)
                sequence0(B - 1, ahead=False)
                pe.wait_ge(lg_ready, 1 + B - 1)
                t2(B - 1)
                route_logits(B - 1, wr, E0)
                rank(0, 1)

            def rank(n, g):
                E = (E0, E1)[n]
                pe.wait_ge(chosen, GROUPS * n + g + 1)
                nc.tensor.matmul(bRank[:, 0:TG * E], before_bf, rt_selbf[:, :, 0:E], start=True, stop=False,
                                 skip_group_check=True)
                for t in range(TG):
                    ins = nc.tensor.matmul(bRank[:, (t + 1) * E:(TG + 1) * E], ones_bf,
                                           rt_selbf[:, t, 0:E].unsqueeze(1).to_broadcast([P, TG - t, E]),
                                           start=False, stop=(t == TG - 1), skip_group_check=True)
                ins.then_inc(rank_psum, 1)

            def xs_transpose(c):
                pe.wait_ge(xs_loaded, 16 * c + 16)
                after(pe, xsT_ready, c)
                for t in range(CH):
                    ins = nc.tensor.transpose(bX[:, t * P:(t + 1) * P], xs[:, t, :], ident)
                ins.then_inc(xs_psum, 1)

            def up0(e, mg, t, chunk):
                if t == 0:
                    pe.wait_ge(xsT_ready, chunk + 1)
                after(pe, hid_ready, mg - 1)
                for bk, half in ((bG, 0), (bU, 1)):
                    ins = nc.tensor.matmul(bk[t % 2][:, 0:I0], xsT[:, t * P:(t + 1) * P],
                                           wgu[:, bass.ds(e, 1), half * I0:(half + 1) * I0].rearrange("p a n -> p (a n)"),
                                           start=True, stop=True)
                ins.then_inc(up_psum, 1)

            def turn0(mg, t):
                pe.wait_ge(hid_ready, mg + 1)
                after(pe, hidT_ready, mg)
                for j in range(HC0):
                    w = min(P, I0 - j * P)
                    ins = nc.tensor.transpose(bHT[0:w, j * P:(j + 1) * P], hid[:, t % 2, j * P:j * P + w], ident)
                ins.then_inc(hidT_psum, 1)

            def down0(e, mg, t):
                pe.wait_ge(hidT_ready, mg + 1)
                after(pe, y_ready, mg - 1)
                for j in range(HC0):
                    w = min(P, I0 - j * P)
                    ins = nc.tensor.matmul(bY[t % 2][:, 0:C], hidT[0:w, t % 2, j * P:(j + 1) * P],
                                           wd[0:w, bass.ds(e, 1), j, :].rearrange("p a n -> p (a n)"),
                                           start=(j == 0), stop=(j == HC0 - 1))
                ins.then_inc(y_psum, 1)

            def experts0(g):
                m0, c0, nch = tile0(0, g), chunk0(0, g), NT[0] // CH
                pe.wait_ge(ffn0_loaded, 16 * 3)
                pe.wait_ge(routed, g + 1)

                def chunk(c, first=False, last=False):
                    e = experts_of(mybir.EngineType.PE, 0, g, c, first)
                    for t in range(CH):
                        m = c * CH + t
                        up0(e[t], m + m0, t, c + c0)
                        if t == 3 and not last:
                            xs_transpose(c + c0 + 1)
                        if not (first and t < 1):
                            turn0(m + m0 - 1, t - 1)
                        if not (first and t < 2):
                            down0(e[t - 2], m + m0 - 2, t)
                    return e

                xs_transpose(c0)
                chunk(0, first=True)
                with pe.Fori(1, nch - 1) as c:
                    chunk(c)
                e = chunk(nch - 1, last=True)
                end = nch * CH
                turn0(end - 1 + m0, 3)
                down0(e[2], end - 2 + m0, 2)
                down0(e[3], end - 1 + m0, 3)

            def keys(b):
                pe.wait_ge(xkT_ready, b + 1)
                pe.wait_ge(xnT_ready, B + b + 1)
                for n in range(2):
                    ins = nc.tensor.matmul(bX[:, n * Q * KC:(n + 1) * Q * KC], wk1[:, n, :], xkT, start=True, stop=True)
                ins.then_inc(key_psum, 1)

            def values(b):
                pe.wait_ge(key_turned, b + 1)
                for n in range(2):
                    ins = nc.tensor.matmul(bX[:, n * C:(n + 1) * C], xkT[:, n * P:(n + 1) * P], wv1[:, :], start=True, stop=True)
                ins.then_inc(val_psum, 1)

            def produce(b, u):
                n = UNITS * b + u
                bk = bU1[u % 3]
                after(pe, unit_sub, 1 + n - 2)
                if u < 4:
                    pe.wait_ge(kT1_ready, b + 1)
                    nc.tensor.matmul(bk[:, :].rearrange("p (s k) -> p s k", s=8), ident_bf,
                                     latmask_bf.unsqueeze(1).to_broadcast([P, 8, KC]), start=True, stop=False,
                                     skip_group_check=True)
                    for h in range(2):
                        ins = nc.tensor.matmul(bk[:, h * Q * KC:(h + 1) * Q * KC],
                                               latbd[:, 4 * u + 2 * h:4 * u + 2 * h + 2, :].rearrange("p h l -> p (h l)"),
                                               kT1[:, :], start=False, stop=True, skip_group_check=True)
                else:
                    t, half = (u - 4) // 2, u % 2
                    if u == 4:
                        pe.wait_ge(xT1_ready, 16 * (b + 1))
                    ins = nc.tensor.matmul(bk[:, :], xT1[:, t * P:(t + 1) * P], wg1[:, half * 512:(half + 1) * 512],
                                           start=True, stop=True)
                ins.then_inc(unit_psum, 1)

            def turn_unit(b, u):
                n = UNITS * b + u
                pe.wait_ge(unit_exp, n + 1)
                after(pe, exT_ready, 1 + n - 1)
                for j in range(4):
                    ins = nc.tensor.transpose(bT1[u % 2][:, j * P:(j + 1) * P], ex[:, u % 3, j * P:(j + 1) * P], ident)
                ins.then_inc(exT_psum, 1)

            def use_unit(b, u):
                n = UNITS * b + u
                pe.wait_ge(exT_ready, 1 + n + 1)
                if u < 4:
                    if u >= 2:
                        pe.wait_ge(att_step, 3 * (Q * b + u - 2) + 2)
                    elif u == 0:
                        after(pe, mixed_ready, 1 + Q * b)
                    else:
                        after(pe, proj_added, 1 + Q * b)
                    if u == 0:
                        pe.wait_ge(val_ready, 2 * b + 2)
                    for j in range(4):
                        ins = nc.tensor.matmul(bO1[u % 2][:, j * 2 * VW:(j + 1) * 2 * VW], exT[:, u % 2, j * P:(j + 1) * P],
                                               vbd[:, j % 2, 2 * u + j // 2, :, :].rearrange("p n v -> p (n v)"),
                                               start=True, stop=True)
                else:
                    t = (u - 4) // 2
                    if t == 0:
                        pe.wait_ge(att_step, 3 * (Q * b + Q))
                    else:
                        pe.wait_ge(mixed_ready, 1 + Q * b + t)
                    for j in range(4):
                        h = 4 * (u % 2) + j
                        ins = nc.tensor.matmul(bO1[0][:, h * GW:(h + 1) * GW], exT[:, u % 2, j * P:(j + 1) * P],
                                               attbd[:, h, :], start=True, stop=True)
                ins.then_inc(unit_used, 1)

            def turn_mixed(b, t):
                pe.wait_ge(mixed_ready, 1 + Q * b + t + 1)
                if t == 0:
                    pe.wait_ge(att_step, 3 * (Q * b + Q))
                else:
                    pe.wait_ge(proj_added, 1 + Q * b + t)
                nc.tensor.transpose(bO1[1][:, 0:P], mixed[:, :, :, :].rearrange("p h k d -> p (h k d)"),
                                    ident).then_inc(mixedT_psum, 1)

            def project(b, t):
                pe.wait_ge(mixedT_ready, Q * b + t + 1)
                nc.tensor.matmul(bO1[1][:, 0:C], mixedT[:, :], wp1[:, :], start=True, stop=True).then_inc(proj_psum, 1)

            def attention1_sequence(b, last=True, ahead=True):
                for s in range(UNITS):
                    produce(b, s)
                    if s in (1, 3) and last:
                        turn_mixed(b - 1, 2 + s // 2)
                    if s in (9, 11):
                        turn_mixed(b, s // 2 - 4)
                    if last or s >= 2:
                        turn_unit(*unit(b, s - 2))
                    if last or s >= 3:
                        use_unit(*unit(b, s - 3))
                    if s in (1, 3) and last:
                        project(b - 1, 2 + s // 2)
                    if s in (9, 11):
                        project(b, s // 2 - 4)
                    if s == 7 and last:
                        pe.wait_ge(val_ready, 2 * b + 2)
                        t2(B + b - 1)
                    if s == 8 and last:
                        route_logits(B + b - 1, wr1, E1)
                    if s == 9 and ahead:
                        if last:
                            pe.wait_ge(lg_ready, 1 + B + b)
                        else:
                            pe.wait_ge(val_ready, 2 * b + 2)
                        t1(B + b + 1)
                    if s == 10 and ahead:
                        keys(b + 1)
                    if s == 11 and ahead:
                        values(b + 1)

            def attention1():
                pe.wait_ge(att1_loaded, 16 * 7)
                pe.wait_ge(latbd_ready, 1)
                pe.wait_ge(att1_preset, 4)
                t1(B)
                keys(0)
                values(0)
                attention1_sequence(0, last=False)
                with pe.Fori(1, BG) as b:
                    attention1_sequence(b)
                attention1_sequence(BG)
                rank(1, 0)
                with pe.Fori(BG + 1, B - 1) as b:
                    attention1_sequence(b)
                attention1_sequence(B - 1, ahead=False)
                for s in range(4):
                    if s % 2:
                        turn_mixed(B - 1, 2 + s // 2)
                    if s < 2:
                        turn_unit(B - 1, UNITS - 2 + s)
                    if s < 3:
                        use_unit(B - 1, UNITS - 3 + s)
                    if s % 2:
                        project(B - 1, 2 + s // 2)
                pe.wait_ge(lg_ready, 1 + 2 * B - 1)
                t2(2 * B - 1)
                route_logits(2 * B - 1, wr1, E1)
                rank(1, 1)

            def up1(e, mg, t, chunk):
                if t == 0:
                    pe.wait_ge(xsT_ready, chunk + 1)
                after(pe, bias_added, mg - tile0(1, 0) - 1)
                nc.tensor.matmul(bG[t % 2][:, :], xsT[:, t * P:(t + 1) * P],
                                 w1[:, bass.ds(e, 1), :].rearrange("p a n -> p (a n)"),
                                 start=True, stop=True).then_inc(up_psum, 1)

            def turn1(mg, t):
                pe.wait_ge(hid_ready, mg + 1)
                pe.wait_ge(hidT_ready, mg)
                for j in range(HC1):
                    ins = nc.tensor.transpose(bHT[:, j * P:(j + 1) * P], hid[:, t % 2, j * P:(j + 1) * P], ident)
                ins.then_inc(hidT_psum, 1)

            def down1(e, mg, t):
                pe.wait_ge(hidT_ready, mg + 1)
                pe.wait_ge(y_ready, mg - 1)
                for j in range(HC1):
                    ins = nc.tensor.matmul(bY[t % 2][:, 0:C], hidT[:, t % 2, j * P:(j + 1) * P],
                                           w2[:, bass.ds(e, 1), j, :].rearrange("p a n -> p (a n)"),
                                           start=(j == 0), stop=(j == HC1 - 1))
                ins.then_inc(y_psum, 1)

            def experts1(g):
                m0, c0, nch = tile0(1, g), chunk0(1, g), NT[1] // CH
                pe.wait_ge(ffn1_loaded, 16 * 4)
                pe.wait_ge(routed, GROUPS + g + 1)

                def chunk(c, first=False, last=False):
                    e = experts_of(mybir.EngineType.PE, 1, g, c, first)
                    for t in range(CH):
                        m = c * CH + t
                        up1(e[t], m + m0, t, c + c0)
                        if t == 3 and not last:
                            xs_transpose(c + c0 + 1)
                        if not (first and t < 1):
                            turn1(m + m0 - 1, t - 1)
                        if not (first and t < 2):
                            down1(e[t - 2], m + m0 - 2, t)
                    return e

                xs_transpose(c0)
                chunk(0, first=True)
                with pe.Fori(1, nch - 1) as c:
                    chunk(c)
                e = chunk(nch - 1, last=True)
                end = nch * CH
                turn1(end - 1 + m0, 3)
                down1(e[2], end - 2 + m0, 2)
                down1(e[3], end - 1 + m0, 3)

            attention0()
            for g in range(GROUPS):
                experts0(g)
            attention1()
            for g in range(GROUPS):
                experts1(g)


def _consts():
    import numpy as np
    c = np.zeros((P, NCONST), np.float32)
    p = np.arange(P)

    def put(name, value):
        c[:, COLS[name][0]:COLS[name][1]] = value

    put("ident", np.eye(P))
    inv = (1.0 / 10000.0 ** (np.arange(0, D, 2, dtype=np.float32) / D)).astype(np.float32)
    pos = (np.arange(Q)[:, None] * P + np.arange(KC)[None, :]).reshape(-1).astype(np.float32)
    ang = (pos[None, :] * inv[(p % D) // 2][:, None]).astype(np.float32)
    put("cos", np.cos(ang))
    put("sin", np.sin(ang) * np.where(p % 2 == 0, -1.0, 1.0)[:, None])
    put("headmask", (p[:, None] // D) == np.arange(H)[None, :])
    put("iota_e", np.arange(16)[None, :])
    put("iota_j", np.arange(ST)[None, :])
    e = np.arange(E0)
    put("below", (e[None, :] < e[:, None]).reshape(1, -1))
    put("ones", 1.0)
    put("before", p[:, None] < p[None, :])
    put("causal", np.where(p[None, :] <= p[:, None], 0.0, NEG))
    put("latmask", np.where(np.arange(KC)[None, :] <= (p % L)[:, None], 0.0, NEG))
    put("pairones", (p[:, None] // L) == np.arange(2)[None, :])
    return c


def kernel(**inputs):
    import numpy as np
    import concourse.bacc as bacc
    from concourse.bass_utils import run_bass_kernel_spmd

    i = {n: np.asarray(v) for n, v in inputs.items()}
    swap = np.arange(C) ^ 1
    arrays = {
        "const": _consts(),
        "L0_attn_x": i["L0_attn_x"],
        "qkvw": np.stack([i["L0_attn_Qw"], i["L0_attn_Kw"], i["L0_attn_Vw"]], axis=1),
        "qkb": np.stack([i["L0_attn_Qb"], i["L0_attn_Kb"]], axis=1),
        "L0_attn_Vb": i["L0_attn_Vb"],
        "L0_ffn_Wr": i["L0_ffn_Wr"],
        "wk1": np.stack([i["L1_attn_W_k"].T, i["L1_attn_W_k"].T[:, swap]], axis=1),
        "wv1": i["L1_attn_W_v"].T,
        "wg1": i["L1_attn_W_g"].T,
        "wp1": i["L1_attn_W_p"].T,
        "lat": i["L1_attn_latent_queries"][0].transpose(1, 2, 0).reshape(C, L),
        "L1_ffn_Wg": i["L1_ffn_Wg"],
        "L1_ffn_bg": i["L1_ffn_bg"],
        "w1": i["L1_ffn_W1"].transpose(1, 0, 2),
        "w2": i["L1_ffn_W2"].reshape(E1, HC1, P, C).transpose(2, 0, 1, 3),
        "L1_ffn_b1": i["L1_ffn_b1"],
        "L1_ffn_b2": i["L1_ffn_b2"],
        "wgu": np.concatenate([i["L0_ffn_Wg"], i["L0_ffn_Wu"]], axis=2).transpose(1, 0, 2),
        "wd_a": i["L0_ffn_Wd"][:, :2 * P].reshape(E0, 2, P, C).transpose(2, 0, 1, 3),
        "wd_b": i["L0_ffn_Wd"][:, 2 * P:].transpose(1, 0, 2),
    }
    arrays = {n: np.ascontiguousarray(v) for n, v in arrays.items()}
    nc = bacc.Bacc("TRN2", target_bir_lowering=False, num_devices=1)
    a = {n: nc.dram_tensor("in_" + n, v.shape, mybir.dt.from_np(v.dtype), kind="ExternalInput").ap()
         for n, v in arrays.items()}
    out = nc.dram_tensor("out", (B, T, C), F32, kind="ExternalOutput").ap()
    build(nc, a, out)
    got = run_bass_kernel_spmd(nc, [{"in_" + n: v for n, v in arrays.items()}], core_ids=[0])
    return got.results[0]["out"]
```

```python
from contextlib import ExitStack

import concourse.bass as bass
from concourse import mybir

F32 = mybir.dt.float32
BF16 = mybir.dt.bfloat16
I32 = mybir.dt.int32
U32 = mybir.dt.uint32
ALU = mybir.AluOpType
ACT = mybir.ActivationFunctionType
X = mybir.AxisListType.X

P = 128
B, T, C = 8, 512, 128
TILES = B * T // P
Q = T // P
GROUPS = 2
BG = B // GROUPS
TG = BG * Q
EPS = 1e-5
NEG = -1e30
SCALE0 = float(C) ** -0.5

E0, I0, K0 = 9, 352, 2
E1, I1, K1 = 8, 512, 1
HC0, HC1 = -(-I0 // P), I1 // P
CH = 4


def slot_tiles(experts, k):
    rows = k * TG * P
    most = (rows - experts) // P + experts
    return -(-most // CH) * CH


ST0, ST1 = slot_tiles(E0, K0), slot_tiles(E1, K1)
ST = max(ST0, ST1)

H, L = 16, 64
D = C // H
HP = H // 2
KC = 64
SCALE1 = float(D) ** -0.5
VW = 2 * D + 1
GW = 2 * D + 2

COLS, _at = {}, 0
for _name, _n in (("ident", P), ("cos", Q * KC), ("sin", Q * KC), ("headmask", H), ("iota_e", 16),
                  ("iota_j", ST), ("below", 81), ("ones", P), ("before", P), ("causal", P),
                  ("latmask", KC), ("pairones", 2)):
    COLS[_name] = (_at, _at + _n)
    _at += _n
NCONST = _at


NEWTON = 3
LN_STEPS = 3 * NEWTON + 3


def after(engine, semaphore, n):
    if not (isinstance(n, int) and n < 1):
        engine.wait_ge(semaphore, n)


def build(nc, a, out):
    ctx = ExitStack()
    with ctx:
        def sb(name, shape, dt=F32):
            return ctx.enter_context(nc.sbuf_tensor(name, shape, dt))

        def ps(name, shape, dt=F32):
            return ctx.enter_context(nc.psum_tensor(name, shape, dt))

        def sem(name):
            return ctx.enter_context(nc.semaphore(name))

        x = sb("x", [P, TILES, C])
        rows = sb("rows", [P, TILES, C])
        const = sb("const", [P, NCONST])

        def cst(name):
            return const[:, COLS[name][0]:COLS[name][1]]

        ident = cst("ident")
        cbf = sb("cbf", [P, 4 * P + KC], BF16)
        ident_bf, ones_bf, before_bf, causal_bf = (cbf[:, n * P:(n + 1) * P] for n in range(4))
        latmask_bf = cbf[:, 4 * P:4 * P + KC]
        qkvw = sb("qkvw", [P, 3, C])
        qkb = sb("qkb", [P, 2])
        vb = sb("vb", [P, C])
        work = sb("work", [P, 8 * T])
        xnT, qT, kT, v = (work[:, n * T:(n + 1) * T] for n in range(4))
        xn2 = sb("xn2", [P, Q, C])
        scratch = sb("scratch", [P, 1])
        primed = sb("primed", [P, 1])
        xn = sb("xn", [P, Q, C])
        bn = sb("bn", [P, 2 * Q, 6])
        mv = sb("mv", [P, 2 * Q, 2])
        var, root, square, shift = (sb(n, [P, 2 * Q]) for n in ("var", "root", "square", "shift"))
        prob = work[:, 4 * T:6 * T].rearrange("p (n t) -> p n t", n=2)
        probT = work[:, 6 * T:8 * T].rearrange("p (n t) -> p n t", n=2)
        mx = sb("mx", [P, Q])
        nmx = sb("nmx", [P, Q])
        rsum = sb("rsum", [P, Q])
        rinv = sb("rinv", [P, Q])
        x2T = sb("x2T", [P, T])
        wr = sb("wr", [P, E0])
        logits = sb("logits", [P, TILES, E0])
        wr1 = sb("wr1", [P, E1])
        br1 = sb("br1", [P, E1])
        logits1 = sb("logits1", [P, TILES, E1])
        wk1 = sb("wk1", [P, 2, C])
        wv1 = sb("wv1", [P, C])
        wg1 = sb("wg1", [P, H * L])
        wp1 = sb("wp1", [P, C])
        lat = sb("lat", [P, L])
        latbd = sb("latbd", [P, H, L])
        xT1 = work[:, 5 * 512:6 * 512]
        xTn = sb("xTn", [P, T])
        xkT = work[:, 7 * 512:7 * 512 + Q * KC]
        turned = work[:, 6 * 512:7 * 512].rearrange("p (n k) -> p n k", n=2)
        kT1 = sb("kT1", [P, Q * KC])
        vbd = sb("vbd", [P, 2, HP, 2, VW])
        ex = work[:, 0:3 * 512].rearrange("p (n t) -> p n t", n=3)
        exT = work[:, 3 * 512:5 * 512].rearrange("p (n t) -> p n t", n=2)
        umax = sb("umax", [P, 3, 8])
        chunk_inv = sb("chunk_inv", [P, 2, Q])
        chunk_out = sb("chunk_out", [P, 2, Q, 2 * D])
        attbd = sb("attbd", [P, HP, GW])
        gate_inv = sb("gate_inv", [P, HP, 2])
        mixed = sb("mixed", [P, HP, 2, D])
        mixedT = sb("mixedT", [P, P])

        below = cst("below").rearrange("p (e f) -> p e f", e=E0)
        rt_ge = sb("rt_ge", [P, TG, E0])
        rt_cand = sb("rt_cand", [P, TG, E0])
        rt_second = sb("rt_second", [P, TG, E0])
        rt_sel = sb("rt_sel", [P, K0, TG, E0])
        rt_selbf = sb("rt_selbf", [P, TG, E0], BF16)
        rt_pos = sb("rt_pos", [P, TG, E0])
        rt_prod = sb("rt_prod", [P, TG, E0])
        rt_max = sb("rt_max", [P, 3, TG])
        rt_gap = sb("rt_gap", [P, TG, E0])
        rt_den = sb("rt_den", [P, TG])
        rt_tiles = sb("rt_tiles", [P, E0], I32)
        rt_base = sb("rt_base", [P, E0])
        rt_end = sb("rt_end", [P, E0])
        rt_below = sb("rt_below", [P, E0, E0])
        rt_past = sb("rt_past", [P, ST, E0])
        rt_tile_e = sb("rt_tile_e", [P, ST])
        rt_posf = sb("rt_posf", [P, K0 * TG])
        rt_int = sb("rt_int", [P, 4, K0 * TG], I32)
        slot = [[sb(f"slot{n}{g}", [P, k, TG], U32) for g in range(GROUPS)] for n, k in ((0, K0), (1, K1))]
        weight = [[sb(f"weight{n}{g}", [P, k, TG]) for g in range(GROUPS)] for n, k in ((0, K0), (1, K1))]
        tile_e = [[sb(f"tile_e{n}{g}", [P, ST], I32) for g in range(GROUPS)] for n in (0, 1)]
        expert_w = sb("expert_w", [P, E0 * (2 * I0 + HC0 * C)])
        wgu = expert_w[:, 0:E0 * 2 * I0].rearrange("p (e n) -> p e n", e=E0)
        wd = expert_w[:, E0 * 2 * I0:].rearrange("p (e j c) -> p e j c", e=E0, j=HC0)
        w1 = expert_w[:, 0:E1 * I1].rearrange("p (e n) -> p e n", e=E1)
        w2 = expert_w[:, E1 * I1:2 * E1 * I1].rearrange("p (e j c) -> p e j c", e=E1, j=HC1)
        b1 = sb("b1", [P, E1, I1])
        b2 = sb("b2", [P, E1, C])
        zeros = sb("zeros", [P, CH * C])
        xs = sb("xs", [P, CH, C])
        xsT = sb("xsT", [P, CH * P])
        act_out = sb("act_out", [P, 2, 512])
        hid = sb("hid", [P, 2, 512])
        hidT = sb("hidT", [P, 2, 512])
        ysb = sb("ysb", [P, ST, C])
        fetched = sb("fetched", [P, TILES, C])
        back = [rows, fetched]

        xs_dram = [nc.dram_tensor(f"xs_dram{g}", (ST * P, C), F32, kind="Internal").ap() for g in range(GROUPS)]
        ys_dram = [nc.dram_tensor(f"ys_dram{g}", (ST * P, C), F32, kind="Internal").ap() for g in range(GROUPS)]
        xs_chunk = [t.rearrange("(c p t) h -> p c (t h)", p=P, t=CH) for t in xs_dram]
        ys_chunk = [t.rearrange("(c p t) h -> p c (t h)", p=P, t=CH) for t in ys_dram]

        bank = [ps(f"bank{n}", [P, 512]) for n in range(8)]
        bX, bQV, bK, bPT = bank[0], bank[1], bank[2], bank[5]
        bO = [bank[6], bank[7]]
        bS = [bank[3], bank[4]]
        bRank = [[bank[2], bank[0]], [bank[0], bank[0]]]
        bLast = bank[7]
        bU1, bT1, bO1 = [bank[1], bank[2], bank[3]], [bank[4], bank[5]], [bank[6], bank[7]]
        bG, bU, bHT, bY = [bank[1], bank[2]], [bank[3], bank[4]], bank[5], [bank[6], bank[7]]

        x_loaded = sem("x_loaded")
        const_loaded = sem("const_loaded")
        attw_loaded = sem("attw_loaded")
        const_cast = sem("const_cast")
        ln_stats, ln_step = sem("ln_stats"), sem("ln_step")
        xn_ready = sem("xn_ready")
        xnT_psum, xnT_ready = sem("xnT_psum"), sem("xnT_ready")
        q_psum, q_ready = sem("q_psum"), sem("q_ready")
        k_psum, k_ready = sem("k_psum"), sem("k_ready")
        v_psum, v_ready = sem("v_psum"), sem("v_ready")
        s_psum = sem("s_psum")
        max_step = sem("max_step")
        exp_done = sem("exp_done")
        pt_psum, pt_ready = sem("pt_psum"), sem("pt_ready")
        o_psum = sem("o_psum")
        rinv_done = sem("rinv_done")
        attn_added = sem("attn_added")
        rows_ready = sem("rows_ready")
        rows_kept = sem("rows_kept")
        x2T_psum, x2T_ready = sem("x2T_psum"), sem("x2T_ready")
        lg_psum, lg_ready = sem("lg_psum"), sem("lg_ready")
        out_stored = sem("out_stored")
        route_step = sem("route_step")
        chosen = sem("chosen")
        rank_psum, rank_read = sem("rank_psum"), sem("rank_read")
        gap_ready, gap_exp = sem("gap_ready"), sem("gap_exp")
        routed = sem("routed")
        zeros_ready = sem("zeros_ready")
        zero_filled = [sem(f"zero_filled{g}") for g in range(GROUPS)]
        ffn0_loaded = sem("ffn0_loaded")
        scattered = [sem(f"scattered{g}") for g in range(GROUPS)]
        fetched_back = [sem(f"fetched_back{g}") for g in range(GROUPS)]
        fetched_last = [sem(f"fetched_last{q}") for q in range(BG)]
        xs_loaded, xs_psum, xsT_ready = sem("xs_loaded"), sem("xs_psum"), sem("xsT_ready")
        up_psum = sem("up_psum")
        silu_done, hid_ready = sem("silu_done"), sem("hid_ready")
        hidT_psum, hidT_ready = sem("hidT_psum"), sem("hidT_ready")
        y_psum, y_ready, y_stored = sem("y_psum"), sem("y_ready"), sem("y_stored")
        join_step = sem("join_step")
        weighed, x_joined, combined = sem("weighed"), sem("x_joined"), sem("combined")
        att1_loaded, ffn1_loaded = sem("att1_loaded"), sem("ffn1_loaded")
        att1_zeroed, att1_preset, latbd_ready = sem("att1_zeroed"), sem("att1_preset"), sem("latbd_ready")
        key_psum, key_turned, kT1_ready = sem("key_psum"), sem("key_turned"), sem("kT1_ready")
        val_psum, val_ready = sem("val_psum"), sem("val_ready")
        unit_psum, unit_max, unit_sub, unit_exp = (sem("unit_" + n) for n in ("psum", "max", "sub", "exp"))
        exT_psum, exT_ready, unit_used = sem("exT_psum"), sem("exT_ready"), sem("unit_used")
        att_step = sem("att_step")
        gate_inverted, mixed_ready = sem("gate_inverted"), sem("mixed_ready")
        mixedT_psum, mixedT_ready = sem("mixedT_psum"), sem("mixedT_ready")
        proj_psum, proj_added = sem("proj_psum"), sem("proj_added")
        bias_added = sem("bias_added")
        xkT_ready = sem("xkT_ready")
        xT1_ready = sem("xT1_ready")

        credited = [xnT_psum, lg_psum, x2T_psum, rows_kept, o_psum, pt_psum, exp_done,
                    pt_ready, attn_added, v_ready, k_ready, lg_ready, unit_used, exT_psum,
                    exT_ready, unit_sub, mixedT_psum, proj_psum, proj_added, mixed_ready]

        x_dram = a["L0_attn_x"].rearrange("b (i p) c -> p b i c", p=P)
        out_dram = out.rearrange("b (i p) c -> p b i c", p=P)
        xb = x[:, :, :].rearrange("p (b i) c -> p b i c", b=B)
        rowsb = rows[:, :, :].rearrange("p (b i) c -> p b i c", b=B)
        logitsb = logits[:, :, :].rearrange("p (b i) e -> p b i e", b=B)

        logits1b = logits1[:, :, :].rearrange("p (b i) e -> p b i e", b=B)

        def quad(b):
            return xb[:, bass.ds(b, 1), :, :].rearrange("p a i c -> p (a i) c")

        UNITS = 12

        def unit(b, u):
            return (b, u) if u >= 0 else (b - 1, u + UNITS)

        NT, K_OF = [ST0, ST1], [K0, K1]

        def tile0(n, g):
            return GROUPS * ST0 * n + NT[n] * g

        def chunk0(n, g):
            return tile0(n, g) // CH

        def experts_of(engine, n, g, c, first):
            lead = 0 if first else 2
            table = tile_e[n][g][0:1, bass.ds(c * CH - lead, CH + lead)]
            _, values = nc.values_load_multi_w_load_instructions(
                table, engines=[engine], min_val=0, max_val=(E0, E1)[n] - 1,
                skip_runtime_bounds_check_because="routing clamps the table to the experts")
            return {t - lead: v for t, v in enumerate(values)}

        def ln_call(n, last, ahead):
            return n, 0 if ahead else Q, 2 * Q if last else Q

        LN1 = B + 2

        block = ctx.enter_context(nc.Block())

        @block.sync
        def _(sp):
            sp.dma_start(quad(0), x_dram[:, 0, :, :]).then_inc(x_loaded, 16)
            for s in credited:
                sp.sem_inc(s, 1)
            with sp.Fori(1, B) as b:
                sp.wait_ge(x_loaded, 16 * b)
                sp.dma_start(quad(b), x_dram[:, bass.ds(b, 1), :, :].rearrange("p a i c -> p (a i) c")
                             ).then_inc(x_loaded, 16)
            sp.wait_ge(zeros_ready, 1)
            def fill(g, c):
                sp.dma_start(xs_chunk[g][:, bass.ds(c, 1), :].rearrange("p a h -> p (a h)"),
                             zeros[:, :]).then_inc(zero_filled[g], 16)

            def load_expert0(e):
                ds = bass.ds(e, 1)
                sp.dma_start(wgu[:, ds, :].rearrange("p a n -> p (a n)"),
                             a["wgu"][:, ds, :].rearrange("p a n -> p (a n)")).then_inc(ffn0_loaded, 16)
                sp.dma_start(wd[:, ds, 0:2, :].rearrange("p a j c -> p (a j c)"),
                             a["wd_a"][:, ds, :, :].rearrange("p a j c -> p (a j c)")).then_inc(ffn0_loaded, 16)
                sp.dma_start(wd[0:I0 - 2 * P, ds, 2, :].rearrange("p a c -> p (a c)"),
                             a["wd_b"][:, ds, :].rearrange("p a c -> p (a c)")).then_inc(ffn0_loaded, 16)

            def load_attention1():
                for dst, name in ((wk1, "wk1"), (wv1, "wv1"), (wg1, "wg1"), (wp1, "wp1"), (lat, "lat"),
                                  (wr1, "L1_ffn_Wg")):
                    sp.dma_start(dst[:], a[name]).then_inc(att1_loaded, 16)
                sp.dma_start(br1[:, :], a["L1_ffn_bg"].partition_broadcast(P)).then_inc(att1_loaded, 16)

            def keep_rows(n, b):
                sp.wait_ge(rows_ready, b + B * n + 1)
                sp.dma_start(rowsb[:, bass.ds(b, 1), :, :].rearrange("p a i c -> p (a i) c"),
                             xn2[:, :, :]).then_inc(rows_kept, 16)

            def pass_on(b):
                sp.wait_ge(unit_psum, UNITS * b)
                sp.dma_start(xT1, xTn[:, :]).then_inc(xT1_ready, 16)

            def load_expert1(e):
                sp.dma_start(w1[:, bass.ds(e, 1), :].rearrange("p a n -> p (a n)"),
                             a["w1"][:, bass.ds(e, 1), :].rearrange("p a n -> p (a n)")).then_inc(ffn1_loaded, 16)
                sp.dma_start(w2[:, bass.ds(e, 1), :, :].rearrange("p a j c -> p (a j c)"),
                             a["w2"][:, bass.ds(e, 1), :, :].rearrange("p a j c -> p (a j c)")).then_inc(ffn1_loaded, 16)

            def load_biases1():
                sp.dma_start(b1[:, :, :], a["L1_ffn_b1"].partition_broadcast(P)).then_inc(ffn1_loaded, 16)
                sp.dma_start(b2[:, :, :], a["L1_ffn_b2"].partition_broadcast(P)).then_inc(ffn1_loaded, 16)

            def load_first(n, g):
                sp.wait_ge(scattered[g], 16 * (K0 * TG + (K1 * TG if n else 0)))
                c0 = chunk0(n, g)
                after(sp, xs_psum, c0)
                sp.dma_start(xs[:, :, :].rearrange("p t h -> p (t h)"), xs_chunk[g][:, 0, :]).then_inc(xs_loaded, 16)

            def load_rest(n, g):
                c0 = chunk0(n, g)
                with sp.Fori(1, NT[n] // CH) as c:
                    sp.wait_ge(xs_psum, c + c0)
                    sp.dma_start(xs[:, :, :].rearrange("p t h -> p (t h)"),
                                 xs_chunk[g][:, bass.ds(c, 1), :].rearrange("p a h -> p (a h)")).then_inc(xs_loaded, 16)

            def load_rows(n):
                load_first(n, 0)
                keep_rows(n, B - 1)
                load_rest(n, 0)
                for g in range(1, GROUPS):
                    load_first(n, g)
                    if n == 0 and g == GROUPS - 1:
                        load_attention1()
                    load_rest(n, g)


            for c in range(ST // CH):
                fill(0, c)
            for c in range(B - 1, ST // CH):
                fill(1, c)
            for e in range(B - 1, E0):
                load_expert0(e)
            with sp.Fori(0, B - 1) as b:
                keep_rows(0, b)
                load_expert0(b)
                fill(1, b)
            load_rows(0)
            sp.wait_ge(xnT_ready, B + 1)
            sp.dma_start(xT1, xTn[:, :]).then_inc(xT1_ready, 16)
            sp.wait_ge(x_joined, BG)
            sp.wait_ge(y_psum, GROUPS * ST0)
            for e in range(B - 1, E1):
                load_expert1(e)
            load_biases1()
            with sp.Fori(0, B - 1) as b:
                pass_on(b + 1)
                keep_rows(1, b)
                load_expert1(b)
            load_rows(1)
            sp.wait_ge(combined, 1)
            sp.dma_start(out_dram[:, 0:BG, :, :], xb[:, 0:BG, :, :]).then_inc(out_stored, 16)
            for q in range(BG):
                sp.wait_ge(combined, 1 + q + 1)
                sp.dma_start(out_dram[:, BG + q, :, :], xb[:, BG + q, :, :]).then_inc(out_stored, 16)
            sp.wait_ge(out_stored, 16 * (1 + BG))

        @block.gpsimd
        def _(pool):
            nc.gpsimd.memset(zeros[:, :], 0.0).then_inc(zeros_ready, 1)

            def scatter(n, g):
                pool.wait_ge(routed, GROUPS * n + g + 1)
                pool.wait_ge(rows_kept, 1 + 16 * (B * n + BG * (g + 1)))
                if n == 0:
                    pool.wait_ge(zero_filled[g], 16 * (ST // CH))
                for t in range(TG):
                    for k in range(K_OF[n]):
                        nc.gpsimd.indirect_dma_start(
                            out=xs_dram[g][:, :],
                            out_offset=bass.IndirectOffsetOnAxis(ap=slot[n][g][:, k, t:t + 1], axis=0),
                            in_=rows[:, TG * g + t, :], in_offset=None).then_inc(scattered[g], 16)

            def fetch(n, g):
                pool.wait_ge(y_stored, 16 * (chunk0(n, g) + NT[n] // CH))
                if g == 0:
                    for h in range(GROUPS):
                        pool.wait_ge(scattered[h], 16 * (K0 * TG + (K1 * TG if n else 0)))
                for t in range(TG):
                    for k in range(K_OF[n]):
                        nc.gpsimd.indirect_dma_start(
                            out=back[g][:, k * TG + t, :], out_offset=None, in_=ys_dram[g][:, :],
                            in_offset=bass.IndirectOffsetOnAxis(ap=slot[n][g][:, k, t:t + 1], axis=0),
                        ).then_inc(fetched_last[t // Q] if (n, g) == (1, GROUPS - 1) else fetched_back[g], 16)

            def join(g):
                pool.wait_ge(fetched_back[g], 16 * K0 * TG)
                pool.wait_ge(weighed, g + 1)
                step = 0
                for q in range(BG):
                    for k in range(K0):
                        got = back[g][:, k * TG + q * Q:k * TG + (q + 1) * Q, :]
                        nc.gpsimd.tensor_tensor(got, got, weight[0][g][:, k, q * Q:(q + 1) * Q].unsqueeze(2)
                                                .to_broadcast([P, Q, C]), ALU.mult).then_inc(join_step, 1)
                        step += 1
                        pool.wait_ge(join_step, step)
                        xt = x[:, TG * g + q * Q:TG * g + (q + 1) * Q, :]
                        ins = nc.gpsimd.tensor_tensor(xt, xt, got, ALU.add)
                        if k < K0 - 1:
                            ins.then_inc(join_step, 1)
                            step += 1
                        else:
                            ins.then_inc(x_joined, 1)

            for g in range(GROUPS):
                scatter(0, g)
            for g in range(GROUPS):
                fetch(0, g)
            join(1)
            for g in range(GROUPS):
                scatter(1, g)
            for g in range(GROUPS):
                fetch(1, g)

        @block.scalar
        def _(act):
            act.dma_start(const[:, :], a["const"]).then_inc(const_loaded, 16)
            act.dma_start(qkvw[:, :, :], a["qkvw"]).then_inc(attw_loaded, 16)
            act.dma_start(qkb[:, :], a["qkb"]).then_inc(attw_loaded, 16)
            act.dma_start(vb[:, :], a["L0_attn_Vb"].partition_broadcast(P)).then_inc(attw_loaded, 16)
            act.dma_start(wr[:, :], a["L0_ffn_Wr"]).then_inc(attw_loaded, 16)

            act.wait_ge(const_loaded, 16)
            nc.scalar.activation(primed[:, :], cst("ones")[:, 0:1], ACT.Exp)

            def normalise(n, b, dst, first):
                act.wait_ge(ln_step, LN_STEPS * (n + 1))
                for i in range(Q):
                    xt = xb[:, bass.ds(b, 1), i, :].rearrange("p a c -> p (a c)")
                    j = first + i
                    ins = nc.scalar.activation(dst[:, i, :], xt, ACT.Identity, bias=shift[:, j:j + 1],
                                               scale=root[:, j:j + 1])
                return ins

            def normalise_next(n, b, m):
                after(act, xnT_psum, 1 + m)
                normalise(n, b, xn, 0).then_inc(xn_ready, 1)

            def normalise_last(n, b, m):
                after(act, x2T_psum, 1 + m)
                after(act, rows_kept, 1 + 16 * m)
                normalise(n, b, xn2, Q).then_inc(rows_ready, 1)

            def evac_xnT(b):
                act.wait_ge(xnT_psum, 1 + b + 1)
                nc.scalar.activation(xnT[:, :], bX[:, :], ACT.Copy).then_inc(xnT_ready, 1)

            def evac_q(b):
                act.wait_ge(q_psum, b + 1)
                nc.scalar.activation(qT[:, :], bQV[:, :], ACT.Identity, bias=qkb[:, 0:1]).then_inc(q_ready, 1)

            def evac_k(b):
                act.wait_ge(k_psum, b + 1)
                nc.scalar.activation(kT[:, :], bK[:, :], ACT.Identity, bias=qkb[:, 1:2]).then_inc(k_ready, 1)

            def exp_scores(b, i):
                act.wait_ge(max_step, 2 * (Q * b + i + 1))
                after(act, pt_psum, 1 + Q * b + i - 1)
                nc.scalar.activation(prob[:, i % 2, 0:(i + 1) * P], bS[i % 2][:, 0:(i + 1) * P], ACT.Exp,
                                     bias=nmx[:, i:i + 1], scale=SCALE0,
                                     accum_out=rsum[:, i:i + 1]).then_inc(exp_done, 1)

            def evac_x2T(b, bk=bX):
                act.wait_ge(x2T_psum, 1 + b + 1)
                after(act, lg_psum, 1 + b)
                nc.scalar.activation(x2T[:, :], bk[:, :], ACT.Copy).then_inc(x2T_ready, 1)

            def sequence0(b, last=True, ahead=True, route=False):
                exp_scores(b, 0)
                exp_scores(b, 1)
                exp_scores(b, 2)
                if ahead:
                    normalise_next(b + 1, b + 1, b + 1)
                exp_scores(b, 3)
                if ahead:
                    evac_xnT(b + 1)
                if last:
                    normalise_last(b + 1, b - 1, b - 1)
                if ahead:
                    evac_q(b + 1)
                if last:
                    evac_x2T(b - 1)
                if ahead:
                    evac_k(b + 1)
                if route:
                    route_exp(0, 0)

            def attention0():
                act.wait_ge(attw_loaded, 16 * 4)
                normalise_next(0, 0, 0)
                evac_xnT(0)
                evac_q(0)
                evac_k(0)
                sequence0(0, last=False)
                with act.Fori(1, BG) as b:
                    sequence0(b)
                sequence0(BG)
                sequence0(BG + 1, route=True)
                with act.Fori(BG + 2, B - 1) as b:
                    sequence0(b)
                sequence0(B - 1, ahead=False)

            def route_exp(n, g):
                act.wait_ge(gap_ready, GROUPS * n + g + 1)
                gap = rt_gap[:, :, 0:1] if n == 0 else rt_gap[:, :, 0:E1]
                nc.scalar.activation(gap, gap, ACT.Exp).then_inc(gap_exp, 1)

            def evac_xs(c):
                act.wait_ge(xs_psum, c + 1)
                after(act, up_psum, CH * c)
                nc.scalar.activation(xsT[:, :], bX[:, :], ACT.Copy).then_inc(xsT_ready, 1)

            def silu0(m, t):
                act.wait_ge(up_psum, m + 1)
                after(act, hid_ready, m - 1)
                nc.scalar.activation(act_out[:, t % 2, 0:I0], bG[t % 2][:, 0:I0], ACT.Silu).then_inc(silu_done, 1)

            def evac_y(m, ml, t):
                act.wait_ge(y_psum, m + 1)
                nc.scalar.activation(ysb[:, bass.ds(ml, 1), :].rearrange("p a c -> p (a c)"), bY[t % 2][:, 0:C],
                                     ACT.Copy).then_inc(y_ready, 1)

            def store_y(n, g, c):
                act.wait_ge(y_ready, CH * (c + 1) + tile0(n, g))
                act.dma_start(ys_chunk[g][:, bass.ds(c, 1), :].rearrange("p a h -> p (a h)"),
                              ysb[:, bass.ds(c * CH, CH), :].rearrange("p t h -> p (t h)")).then_inc(y_stored, 16)

            def experts0(g):
                m0, c0, nch = tile0(0, g), chunk0(0, g), NT[0] // CH

                def chunk(c, first=False, last=False):
                    for t in range(CH):
                        m = c * CH + t
                        silu0(m + m0, t)
                        if first and g == 0 and t == 1:
                            normalise_last(B + 1, B - 1, B - 1)
                        if first and g == 0 and t == 2:
                            evac_x2T(B - 1, bLast)
                        if t == 3 and not (last and g == GROUPS - 1):
                            evac_xs(c + c0 + 1)
                        if not (first and t < 2):
                            evac_y(m + m0 - 2, m - 2, t)
                        if t == 1 and not first:
                            store_y(0, g, c - 1)
                        if t == 2 and last and g == GROUPS - 1:
                            normalise_next(LN1, 0, B)

                if g == 0:
                    evac_xs(c0)
                after(act, y_stored, 16 * c0)
                chunk(0, first=True)
                with act.Fori(1, nch - 1) as c:
                    chunk(c)
                chunk(nch - 1, last=True)
                if g == GROUPS - 1:
                    evac_xTn(0)
                for t in (2, 3):
                    m = (nch - 1) * CH + t
                    evac_y(m + m0, m, t)
                store_y(0, g, nch - 1)

            def exp_unit(b, u):
                n = UNITS * b + u
                act.wait_ge(unit_sub, 1 + n + 1)
                nc.scalar.activation(ex[:, u % 3, :], ex[:, u % 3, :], ACT.Exp, scale=SCALE1).then_inc(unit_exp, 1)

            def evac_exT(b, u):
                n = UNITS * b + u
                act.wait_ge(exT_psum, 1 + n + 1)
                after(act, unit_used, 1 + n - 1)
                nc.scalar.activation(exT[:, u % 2, :], bT1[u % 2][:, :], ACT.Copy).then_inc(exT_ready, 1)

            def evac_mixedT(b, t):
                act.wait_ge(mixedT_psum, 1 + Q * b + t + 1)
                after(act, proj_psum, 1 + Q * b + t)
                nc.scalar.activation(mixedT[:, :], bO1[1][:, 0:P], ACT.Copy).then_inc(mixedT_ready, 1)

            def evac_xTn(b):
                act.wait_ge(xnT_psum, 1 + B + b + 1)
                nc.scalar.activation(xkT.rearrange("p (n c) -> p n c", n=Q),
                                     bX[:, :].rearrange("p (n c) -> p n c", n=Q)[:, :, 0:KC],
                                     ACT.Copy).then_inc(xkT_ready, 1)
                after(act, xT1_ready, 16 * b)
                nc.scalar.activation(xTn[:, :], bX[:, :], ACT.Copy).then_inc(xnT_ready, 1)

            def evac_values(b):
                act.wait_ge(val_psum, b + 1)
                for n in range(2):
                    r = slice(n * KC, (n + 1) * KC)
                    nc.scalar.activation(vbd[r, :, :, n, 0:2 * D],
                                         bX[r, 0:2 * C].rearrange("p (u h d) -> p u h d", u=2, h=HP),
                                         ACT.Copy).then_inc(val_ready, 1)

            def attention1_sequence(b, last=True, ahead=True, route=False):
                for s in range(UNITS):
                    if s in (1, 3) and last:
                        evac_mixedT(b - 1, 2 + s // 2)
                    if s in (9, 11):
                        evac_mixedT(b, s // 2 - 4)
                    if s == 11 and last:
                        evac_x2T(B + b - 1)
                    if last or s >= 2:
                        evac_exT(*unit(b, s - 2))
                    if s == 10 and ahead:
                        evac_values(b + 1)
                    exp_unit(b, s)
                    if s == 7 and ahead:
                        normalise_next(LN1 + b + 1, b + 1, B + b + 1)
                    if s == 8 and ahead:
                        evac_xTn(b + 1)
                    if s == 7 and route:
                        route_exp(1, 0)
                    if s == 9 and last:
                        normalise_last(LN1 + b + 1, b - 1, B + b - 1)

            def attention1():
                evac_values(0)
                route_exp(0, 1)
                attention1_sequence(0, last=False)
                with act.Fori(1, BG) as b:
                    attention1_sequence(b)
                attention1_sequence(BG)
                attention1_sequence(BG + 1, route=True)
                with act.Fori(BG + 2, B - 1) as b:
                    attention1_sequence(b)
                attention1_sequence(B - 1, ahead=False)
                for s in range(4):
                    if s % 2:
                        evac_mixedT(B - 1, 2 + s // 2)
                    if s < 2:
                        evac_exT(B - 1, UNITS - 2 + s)

            def silu1(m, t):
                act.wait_ge(bias_added, m - tile0(1, 0) + 1)
                act.wait_ge(hidT_psum, m - 1)
                nc.scalar.activation(hid[:, t % 2, :], act_out[:, t % 2, :], ACT.Silu).then_inc(hid_ready, 1)

            def evac_hidT1(m, t):
                act.wait_ge(hidT_psum, m + 1)
                act.wait_ge(y_psum, m - 1)
                nc.scalar.activation(hidT[:, t % 2, :], bHT[:, :], ACT.Copy).then_inc(hidT_ready, 1)

            def experts1(g):
                m0, c0, nch = tile0(1, g), chunk0(1, g), NT[1] // CH

                def chunk(c, first=False, last=False):
                    for t in range(CH):
                        m = c * CH + t
                        if t == 3 and not last:
                            evac_xs(c + c0 + 1)
                        if not (first and t < 1):
                            evac_hidT1(m + m0 - 1, t - 1)
                        silu1(m + m0, t)
                        if first and g == 0 and t == 1:
                            normalise_last(LN1 + B + 1, B - 1, 2 * B - 1)
                        if first and g == 0 and t == 2:
                            evac_x2T(2 * B - 1, bLast)
                        if t == 2 and not first:
                            store_y(1, g, c - 1)

                evac_xs(c0)
                chunk(0, first=True)
                with act.Fori(1, nch - 1) as c:
                    chunk(c)
                chunk(nch - 1, last=True)
                evac_hidT1(nch * CH - 1 + m0, 3)
                store_y(1, g, nch - 1)

            attention0()
            for g in range(GROUPS):
                experts0(g)
            attention1()
            for g in range(GROUPS):
                experts1(g)
            route_exp(1, 1)

        @block.vector
        def _(dve):
            def take_wait():
                nc.vector.memset(scratch[:, :], 0.0)

            def statistics(call, tiles, b):
                n, lo, hi = call
                for j in tiles:
                    if lo <= j < hi:
                        src = quad(b if j < Q else b - 2)
                        ins = nc.vector.bn_stats(bn[:, j, :], src[:, j % Q, :])
                if hi - 1 in tiles:
                    ins.then_inc(ln_stats, 1)

            def aggregate(call, tiles):
                n, lo, hi = call
                if lo in tiles:
                    dve.wait_ge(ln_stats, 2 * n + 1)
                    take_wait()
                for j in tiles:
                    if lo <= j < hi:
                        ins = nc.vector.bn_aggr(mv[:, j, :], bn[:, j, :])
                if hi - 1 in tiles:
                    ins.then_inc(ln_stats, 1)

            def normaliser(call, steps):
                n, lo, hi = call
                r, q, v = root[:, lo:hi], square[:, lo:hi], var[:, lo:hi]
                for k in steps:
                    if k == 0:
                        dve.wait_ge(ln_stats, 2 * n + 2)
                        ins = nc.vector.tensor_scalar(v, mv[:, lo:hi, 1], EPS, None, ALU.add)
                    else:
                        dve.wait_ge(ln_step, LN_STEPS * n + k)
                        if k == 1:
                            ins = nc.vector.tensor_scalar(r.bitcast(I32), v.bitcast(I32), -0.5, float(0x5F3759DF),
                                                          ALU.mult, ALU.add)
                        elif k == LN_STEPS - 1:
                            ins = nc.vector.scalar_tensor_tensor(out=shift[:, lo:hi], in0=mv[:, lo:hi, 0], scalar=-1.0,
                                                                 in1=r, op0=ALU.mult, op1=ALU.mult)
                        elif k % 3 == 2:
                            ins = nc.vector.tensor_tensor(q, r, r, ALU.mult)
                        elif k % 3 == 0:
                            ins = nc.vector.scalar_tensor_tensor(out=q, in0=q, scalar=-0.5, in1=v, op0=ALU.mult,
                                                                 op1=ALU.mult)
                        else:
                            ins = nc.vector.scalar_tensor_tensor(out=r, in0=q, scalar=1.5, in1=r, op0=ALU.add,
                                                                 op1=ALU.mult)
                    ins.then_inc(ln_step, 1)

            def normalisers(call, b):
                statistics(call, range(2 * Q), b)
                aggregate(call, range(2 * Q))
                normaliser(call, range(LN_STEPS))

            def presets():
                dve.wait_ge(const_loaded, 16)
                for n, name in enumerate(("ident", "ones", "before", "causal")):
                    nc.vector.tensor_copy(cbf[:, n * P:(n + 1) * P], cst(name)).then_inc(const_cast, 1)
                nc.vector.tensor_copy(latmask_bf, cst("latmask")).then_inc(const_cast, 1)
                nc.vector.memset(vbd[:], 0.0).then_inc(att1_zeroed, 1)
                nc.vector.memset(attbd[:], 0.0).then_inc(att1_zeroed, 1)
                dve.wait_ge(att1_zeroed, 2)
                for n in range(2):
                    nc.vector.memset(vbd[n * KC:(n + 1) * KC, :, :, n, 2 * D:VW], 1.0).then_inc(att1_preset, 1)
                    nc.vector.memset(attbd[n * L:(n + 1) * L, :, 2 * D + n:2 * D + n + 1], 1.0).then_inc(att1_preset, 1)

            def rowmax(b, i, between=None):
                dve.wait_ge(s_psum, Q * b + i + 1)
                nc.vector.tensor_reduce(mx[:, i:i + 1], bS[i % 2][:, 0:(i + 1) * P], X, ALU.max).then_inc(max_step, 1)
                if between:
                    normaliser(*between)
                dve.wait_ge(max_step, 2 * (Q * b + i) + 1)
                nc.vector.tensor_scalar(nmx[:, i:i + 1], mx[:, i:i + 1], -SCALE0, None, ALU.mult).then_inc(max_step, 1)

            def copy_pt(b, i):
                dve.wait_ge(pt_psum, 1 + Q * b + i + 1)
                after(dve, o_psum, 1 + Q * b + i - 1)
                nc.vector.tensor_copy(probT[:, i % 2, 0:(i + 1) * P], bPT[:, 0:(i + 1) * P]).then_inc(pt_ready, 1)

            def add_attn(b, i):
                dve.wait_ge(exp_done, 1 + Q * b + i + 1)
                nc.vector.reciprocal(rinv[:, i:i + 1], rsum[:, i:i + 1]).then_inc(rinv_done, 1)
                dve.wait_ge(rinv_done, Q * b + i + 1)
                dve.wait_ge(o_psum, 1 + Q * b + i + 1)
                xt = xb[:, bass.ds(b, 1), i, :].rearrange("p a c -> p (a c)")
                nc.vector.scalar_tensor_tensor(out=xt, in0=bO[i % 2][:, 0:C], scalar=rinv[:, i:i + 1],
                                               in1=xt, op0=ALU.mult, op1=ALU.add).then_inc(attn_added, 1)

            def evac_v(b):
                dve.wait_ge(v_psum, b + 1)
                nc.vector.tensor_tensor(v[:, :].rearrange("p (i c) -> p i c", i=Q),
                                        bQV[:, :].rearrange("p (i c) -> p i c", i=Q),
                                        vb[:, :].unsqueeze(1).to_broadcast([P, Q, C]), ALU.add).then_inc(v_ready, 1)

            def evac_logits0(b, bk=bX):
                dve.wait_ge(lg_psum, 1 + b + 1)
                nc.vector.tensor_copy(logitsb[:, bass.ds(b, 1), :, :].rearrange("p a i e -> p (a i) e"),
                                      bk[:, 0:Q * E0].rearrange("p (i e) -> p i e", i=Q)).then_inc(lg_ready, 1)

            def evac_logits1(b, bk=bX):
                dve.wait_ge(lg_psum, 1 + B + b + 1)
                nc.vector.tensor_tensor(logits1b[:, bass.ds(b, 1), :, :].rearrange("p a i e -> p (a i) e"),
                                        bk[:, 0:Q * E1].rearrange("p (i e) -> p i e", i=Q),
                                        br1[:, :].unsqueeze(1).to_broadcast([P, Q, E1]), ALU.add).then_inc(lg_ready, 1)

            def sequence0(b, last=True, ahead=True, further=True, route=False):
                norm = last or ahead
                call = ln_call(b + 1, last, ahead)
                if norm:
                    normaliser(call, range(3))
                if route:
                    choose_first(0, 0)
                rowmax(b, 0, (call, (3,)) if norm else None)
                if norm:
                    normaliser(call, (4,))
                if route:
                    choose_second(0, 0)
                    announce(0, 0)
                rowmax(b, 1, (call, (5,)) if norm else None)
                if norm:
                    normaliser(call, (6,))
                copy_pt(b, 0)
                if norm:
                    normaliser(call, (7,))
                rowmax(b, 2, (call, (8,)) if norm else None)
                if norm:
                    normaliser(call, (9,))
                if route:
                    place_experts(0, 0)
                copy_pt(b, 1)
                if norm:
                    normaliser(call, (10, 11))
                if route:
                    place_tokens(0, 0)
                    place_slots(0, 0)
                rowmax(b, 3)
                if route:
                    place_tiles(0, 0)
                add_attn(b, 0)
                copy_pt(b, 2)
                add_attn(b, 1)
                copy_pt(b, 3)
                add_attn(b, 2)
                call = ln_call(b + 2, True, further)
                if ahead and further:
                    dve.wait_ge(x_loaded, 16 * b + 48)
                    take_wait()
                    statistics(call, range(Q), b + 2)
                add_attn(b, 3)
                if ahead:
                    dve.wait_ge(attn_added, 1 + Q * (b + 1))
                    take_wait()
                    statistics(call, range(Q, 2 * Q), b + 2)
                    evac_v(b + 1)
                    aggregate(call, range(2 * Q))
                if last:
                    evac_logits0(b - 1)
                if route:
                    weigh(0, 0)

            def attention0():
                call = ln_call(0, False, True)
                dve.wait_ge(x_loaded, 16)
                normalisers(call, 0)
                presets()
                call = ln_call(1, False, True)
                dve.wait_ge(x_loaded, 32)
                statistics(call, range(2 * Q), 1)
                aggregate(call, range(2 * Q))
                dve.wait_ge(attw_loaded, 16 * 4)
                evac_v(0)
                sequence0(0, last=False)
                with dve.Fori(1, BG) as b:
                    sequence0(b)
                sequence0(BG)
                sequence0(BG + 1, route=True)
                sequence0(B - 2, further=False)
                sequence0(B - 1, ahead=False)

            steps = [0]

            def then(ins):
                steps[0] += 1
                ins.then_inc(route_step, 1)
                dve.wait_ge(route_step, steps[0])

            def first_max(src, sel, top, E):
                ge, cand = rt_ge[:, :, 0:E], rt_cand[:, :, 0:E]
                iota = cst("iota_e")[:, 0:E].unsqueeze(1).to_broadcast([P, TG, E])
                then(nc.vector.tensor_reduce(top, src, X, ALU.max))
                then(nc.vector.tensor_tensor(ge, src, top.unsqueeze(2).to_broadcast([P, TG, E]), ALU.is_ge))
                then(nc.vector.scalar_tensor_tensor(out=cand, in0=ge, scalar=-16.0, in1=iota, op0=ALU.mult, op1=ALU.add))
                then(nc.vector.tensor_reduce(rt_max[:, 2, :], cand, X, ALU.min))
                then(nc.vector.tensor_tensor(sel, cand, rt_max[:, 2, :].unsqueeze(2).to_broadcast([P, TG, E]),
                                             ALU.is_equal))

            def logits_of(n, g):
                return (logits, logits1)[n][:, TG * g:TG * (g + 1), :]

            def choose_first(n, g):
                dve.wait_ge(lg_ready, 1 + B * n + BG * (g + 1))
                first_max(logits_of(n, g), rt_sel[:, 0, :, 0:(E0, E1)[n]], rt_max[:, 0, :], (E0, E1)[n])

            def choose_second(n, g):
                if n == 0:
                    then(nc.vector.scalar_tensor_tensor(out=rt_second[:, :, :], in0=rt_sel[:, 0], scalar=NEG,
                                                        in1=logits_of(n, g), op0=ALU.mult, op1=ALU.add))
                    first_max(rt_second[:, :, :], rt_sel[:, 1], rt_max[:, 1, :], E0)

            def announce(n, g):
                E, lg = (E0, E1)[n], logits_of(n, g)
                sel = rt_sel[:, :, :, 0:E]
                if n == 0:
                    nc.vector.tensor_tensor(rt_gap[:, :, 0], rt_max[:, 1, :], rt_max[:, 0, :],
                                            ALU.subtract).then_inc(gap_ready, 1)
                    nc.vector.tensor_tensor(rt_selbf[:, :, 0:E], sel[:, 0], sel[:, 1], ALU.add).then_inc(chosen, 1)
                else:
                    nc.vector.tensor_tensor(rt_gap[:, :, 0:E], lg, rt_max[:, 0, :].unsqueeze(2).to_broadcast([P, TG, E]),
                                            ALU.subtract).then_inc(gap_ready, 1)
                    nc.vector.tensor_copy(rt_selbf[:, :, 0:E], sel[:, 0]).then_inc(chosen, 1)

            def place_experts(n, g):
                E = (E0, E1)[n]
                tiles, base, end = rt_tiles[:, 0:E], rt_base[:, 0:E], rt_end[:, 0:E]
                dve.wait_ge(rank_psum, GROUPS * n + g + 1)
                counts = bRank[n][g][:, 0:(TG + 1) * E].rearrange("p (t e) -> p t e", e=E)
                then(nc.vector.tensor_scalar(tiles, counts[:, TG, :], P - 1.0, None, ALU.add))
                then(nc.vector.tensor_scalar(tiles, tiles, 7, None, ALU.logical_shift_right))
                then(nc.vector.tensor_tensor(rt_below[:, 0:E, 0:E], below[:, 0:E, 0:E],
                                             tiles.unsqueeze(1).to_broadcast([P, E, E]), ALU.mult))
                then(nc.vector.tensor_reduce(base, rt_below[:, 0:E, 0:E], X, ALU.add))
                nc.vector.tensor_tensor(end, base, tiles, ALU.add)
                nc.vector.scalar_tensor_tensor(out=rt_pos[:, :, 0:E], in0=base.unsqueeze(1).to_broadcast([P, TG, E]),
                                               scalar=float(P), in1=counts[:, 0:TG, :], op0=ALU.mult,
                                               op1=ALU.add).then_inc(rank_read, 1)
                dve.wait_ge(rank_read, GROUPS * n + g + 1)

            def place_tokens(n, g):
                E, K = (E0, E1)[n], K_OF[n]
                for k in range(K):
                    then(nc.vector.tensor_tensor(rt_prod[:, :, 0:E], rt_sel[:, k, :, 0:E], rt_pos[:, :, 0:E], ALU.mult))
                    then(nc.vector.tensor_reduce(rt_posf[:, k * TG:(k + 1) * TG], rt_prod[:, :, 0:E], X, ALU.add))

            def place_slots(n, g):
                pos, hi, mid, lo = (rt_int[:, m, 0:K_OF[n] * TG] for m in range(4))
                then(nc.vector.tensor_copy(pos, rt_posf[:, 0:K_OF[n] * TG]))
                nc.vector.tensor_scalar(hi, pos, ~(CH * P - 1) & 0x7FFFFFFF, None, ALU.bitwise_and)
                nc.vector.tensor_scalar(mid, pos, P - 1, 2, ALU.bitwise_and, ALU.logical_shift_left)
                then(nc.vector.tensor_scalar(lo, pos, 7, CH - 1, ALU.logical_shift_right, ALU.bitwise_and))
                then(nc.vector.tensor_tensor(hi, hi, mid, ALU.bitwise_or))
                then(nc.vector.tensor_tensor(slot[n][g][:, :, :].rearrange("p k t -> p (k t)").bitcast(I32), hi, lo,
                                             ALU.bitwise_or))

            def place_tiles(n, g):
                E, N = (E0, E1)[n], NT[n]
                past = rt_past[:, 0:N, 0:E]
                then(nc.vector.tensor_tensor(past, cst("iota_j")[:, 0:N].unsqueeze(2).to_broadcast([P, N, E]),
                                             rt_end[:, 0:E].unsqueeze(1).to_broadcast([P, N, E]), ALU.is_ge))
                then(nc.vector.tensor_reduce(rt_tile_e[:, 0:N], past, X, ALU.add))
                nc.vector.tensor_scalar(tile_e[n][g][:, 0:N], rt_tile_e[:, 0:N], E - 1.0, None,
                                        ALU.min).then_inc(routed, 1)

            def weigh(n, g):
                w = weight[n][g]
                dve.wait_ge(gap_exp, GROUPS * n + g + 1)
                if n == 0:
                    then(nc.vector.tensor_scalar(rt_den[:, :], rt_gap[:, :, 0], 1.0, None, ALU.add))
                    then(nc.vector.reciprocal(w[:, 0, :], rt_den[:, :]))
                    ins = nc.vector.tensor_tensor(w[:, 1, :], rt_gap[:, :, 0], w[:, 0, :], ALU.mult)
                else:
                    then(nc.vector.tensor_reduce(rt_den[:, :], rt_gap[:, :, 0:E1], X, ALU.add))
                    ins = nc.vector.reciprocal(w[:, 0, :], rt_den[:, :])
                ins.then_inc(weighed, 1)
                dve.wait_ge(weighed, GROUPS * n + g + 1)

            def spread_latents():
                dve.wait_ge(att1_loaded, 16 * 7)
                nc.vector.tensor_tensor(latbd[:, :, :], lat[:, :].unsqueeze(1).to_broadcast([P, H, L]),
                                        cst("headmask").unsqueeze(2).to_broadcast([P, H, L]),
                                        ALU.mult).then_inc(latbd_ready, 1)

            def normalise_end(n, t):
                call = ln_call(B + 1 + LN1 * n, True, False)
                if t == 0:
                    dve.wait_ge(proj_added if n else attn_added, 1 + Q * B)
                    statistics(call, range(Q, 2 * Q), B + 1)
                    aggregate(call, range(Q, 2 * Q))
                    normaliser(call, range(LN_STEPS // 2))
                if t == 1:
                    normaliser(call, range(LN_STEPS // 2, LN_STEPS))

            def gate0(m, t):
                dve.wait_ge(silu_done, m + 1)
                after(dve, hidT_psum, m - 1)
                nc.vector.tensor_tensor(hid[:, t % 2, 0:I0], act_out[:, t % 2, 0:I0], bU[t % 2][:, 0:I0],
                                        ALU.mult).then_inc(hid_ready, 1)

            def evac_hidT0(m, t):
                dve.wait_ge(hidT_psum, m + 1)
                after(dve, y_psum, m - 1)
                nc.vector.tensor_copy(hidT[:, t % 2, 0:HC0 * P], bHT[:, 0:HC0 * P]).then_inc(hidT_ready, 1)

            def experts0(g):
                m0, nch = tile0(0, g), NT[0] // CH

                def chunk(c, first=False, choose=False, place=False, join=False, last=False):
                    for t in range(CH):
                        m = c * CH + t + m0
                        if first and g == 0:
                            normalise_end(0, t)
                        gate0(m, t)
                        if not (first and t < 1):
                            evac_hidT0(m - 1, t - 1)
                        if first and g == 0 and t == 3:
                            evac_logits0(B - 1, bLast)
                        if choose and t < 3:
                            (choose_first, choose_second, announce)[t](0, 1)
                        if place:
                            (place_experts, place_tokens, place_slots, place_tiles)[t](0, 1)
                        if join:
                            combine(0, 0, t // 2, range(TG // 2 * (t % 2), TG // 2 * (t % 2 + 1)))
                        if last:
                            call = ln_call(LN1, False, True)
                            if t == 0:
                                dve.wait_ge(x_joined, 1)
                                statistics(call, range(Q), 0)
                            if t == 1:
                                aggregate(call, range(Q))
                                normaliser(call, range(LN_STEPS // 2))
                            if t == 2:
                                normaliser(call, range(LN_STEPS // 2, LN_STEPS))

                chunk(0, first=True)
                if g == 0:
                    chunk(1, choose=True)
                    chunk(2, place=True)
                    with dve.Fori(3, nch) as c:
                        chunk(c)
                else:
                    with dve.Fori(1, nch - 2) as c:
                        chunk(c)
                    spread_latents()
                    chunk(nch - 2, join=True)
                    chunk(nch - 1, last=True)
                evac_hidT0(nch * CH - 1 + m0, 3)

            def combine(n, g, k, tiles):
                if k == 0 and 0 in tiles and (n, g) != (1, GROUPS - 1):
                    dve.wait_ge(fetched_back[g], 16 * (K0 * TG + (K1 * TG if n else 0)))
                for t in tiles:
                    xt = x[:, TG * g + t, :]
                    ins = nc.vector.scalar_tensor_tensor(out=xt, in0=back[g][:, k * TG + t, :],
                                                         scalar=weight[n][g][:, k, t:t + 1], in1=xt,
                                                         op0=ALU.mult, op1=ALU.add)
                    if n == 0 and k == K0 - 1 and t % Q == Q - 1:
                        ins.then_inc(x_joined, 1)
                if n == 0 and k < K0 - 1 and TG - 1 in tiles:
                    then(ins)
                if n == 1:
                    ins.then_inc(combined, 1)

            def turn_keys(b):
                dve.wait_ge(key_psum, b + 1)
                nc.vector.tensor_tensor(turned[:, :, :].rearrange("p a k -> p (a k)"), bX[:, :],
                                        const[:, COLS["cos"][0]:COLS["sin"][1]], ALU.mult).then_inc(key_turned, 1)
                dve.wait_ge(key_turned, b + 1)
                nc.vector.tensor_tensor(kT1[:, :], turned[:, 0, :], turned[:, 1, :], ALU.add).then_inc(kT1_ready, 1)

            def unit_maxima(b, u):
                n = UNITS * b + u
                dve.wait_ge(unit_psum, n + 1)
                unit = bU1[u % 3][:, :].rearrange("p (s k) -> p s k", s=8)
                nc.vector.tensor_reduce(umax[:, u % 3, :], unit, X, ALU.max).then_inc(unit_max, 1)

            def subtract_maxima(b, u):
                n = UNITS * b + u
                unit = bU1[u % 3][:, :].rearrange("p (s k) -> p s k", s=8)
                dve.wait_ge(unit_max, n + 1)
                after(dve, exT_psum, 1 + n - 2)
                nc.vector.tensor_tensor(ex[:, u % 3, :].rearrange("p (s k) -> p s k", s=8), unit,
                                        umax[:, u % 3, :].unsqueeze(2).to_broadcast([P, 8, KC]),
                                        ALU.subtract).then_inc(unit_sub, 1)

            def chunk_results(u):
                return bO1[u % 2][:, 0:2 * Q * VW].rearrange("p (h n v) -> p h n v", h=2, n=Q)

            def invert_chunks(b, u):
                dve.wait_ge(unit_used, 1 + UNITS * b + u + 1)
                nc.vector.reciprocal(chunk_inv[:, :, :], chunk_results(u)[:, :, :, 2 * D]).then_inc(att_step, 1)

            def scale_chunks(b, u):
                dve.wait_ge(att_step, 3 * (Q * b + u) + 1)
                nc.vector.tensor_tensor(chunk_out[:, :, :, :], chunk_results(u)[:, :, :, 0:2 * D],
                                        chunk_inv[:, :, :].unsqueeze(3).to_broadcast([P, 2, Q, 2 * D]),
                                        ALU.mult).then_inc(att_step, 1)

            def sum_chunks(b, u):
                dve.wait_ge(att_step, 3 * (Q * b + u) + 2)
                after(dve, unit_used, 1 + UNITS * b)
                for n in range(2):
                    r = slice(n * L, (n + 1) * L)
                    ins = nc.vector.tensor_reduce(attbd[r, 2 * u:2 * u + 2, n * D:(n + 1) * D],
                                                  chunk_out[r, :, :, n * D:(n + 1) * D].rearrange("p h n d -> p h d n"),
                                                  X, ALU.add)
                ins.then_inc(att_step, 1)

            def normalise_gates(b, t):
                dve.wait_ge(unit_used, 1 + UNITS * b + 4 + 2 * t + 2)
                got = bO1[0][:, 0:HP * GW].rearrange("p (h v) -> p h v", h=HP)
                nc.vector.reciprocal(gate_inv[:, :, :], got[:, :, 2 * D:GW]).then_inc(gate_inverted, 1)
                dve.wait_ge(gate_inverted, Q * b + t + 1)
                after(dve, mixedT_psum, 1 + Q * b + t)
                nc.vector.tensor_tensor(mixed[:, :, :, :], got[:, :, 0:2 * D].rearrange("p h (k d) -> p h k d", k=2),
                                        gate_inv[:, :, :].unsqueeze(3).to_broadcast([P, HP, 2, D]),
                                        ALU.mult).then_inc(mixed_ready, 1)

            def add_projected(b, t):
                dve.wait_ge(proj_psum, 1 + Q * b + t + 1)
                xt = xb[:, bass.ds(b, 1), t, :].rearrange("p a c -> p (a c)")
                nc.vector.tensor_tensor(xt, xt, bO1[1][:, 0:C], ALU.add).then_inc(proj_added, 1)

            def attention1_sequence(b, last=True, ahead=True, route=False):
                call = ln_call(LN1 + b + 1, last, ahead)
                norm = last or ahead
                for s in range(UNITS):
                    if s == 10 and ahead:
                        turn_keys(b + 1)
                    unit_maxima(b, s)
                    if s == 6 and norm:
                        normaliser(call, (0,))
                    if s == 7 and norm:
                        normaliser(call, (5,))
                    subtract_maxima(b, s)
                    if s == 6 and norm:
                        normaliser(call, (1,))
                    if s in (0, 2) and last:
                        normalise_gates(b - 1, 2 + s // 2)
                    if s in (1, 3) and last:
                        add_projected(b - 1, 2 + s // 2)
                    if s == 1 and ahead:
                        dve.wait_ge(x_joined, b + 2)
                        take_wait()
                    if s in (1, 2) and ahead:
                        statistics(call, (2 * s - 2, 2 * s - 1), b + 1)
                    if s == 4 and last:
                        dve.wait_ge(proj_added, 1 + Q * b)
                        take_wait()
                    if 3 <= s < 7:
                        invert_chunks(b, s - 3)
                        if s == 4 and last:
                            statistics(call, (4, 5), b + 1)
                        if s == 5 and norm:
                            aggregate(call, range(Q))
                        if s == 6 and norm:
                            normaliser(call, (2,))
                        scale_chunks(b, s - 3)
                        if s == 4 and last:
                            statistics(call, (6, 7), b + 1)
                        if s == 5 and norm:
                            aggregate(call, range(Q, 2 * Q))
                        if s == 6 and norm:
                            normaliser(call, (3,))
                        sum_chunks(b, s - 3)
                        if s == 6 and norm:
                            normaliser(call, (4,))
                    if s == 7 and norm:
                        normaliser(call, range(6, LN_STEPS))
                    if s in (8, 10):
                        normalise_gates(b, s // 2 - 4)
                    if s in (9, 11):
                        add_projected(b, s // 2 - 4)
                    if s == 11 and last:
                        evac_logits1(b - 1)
                    if route and s == 0:
                        choose_first(1, 0)
                    if route and s == 1:
                        announce(1, 0)
                    if route and s == 7:
                        place_experts(1, 0)
                    if route and s == 8:
                        place_tokens(1, 0)
                    if route and s == 9:
                        place_slots(1, 0)
                    if route and s == 10:
                        place_tiles(1, 0)
                    if route and s == 11:
                        weigh(1, 0)

            def attention1():
                turn_keys(0)
                weigh(0, 1)
                attention1_sequence(0, last=False)
                with dve.Fori(1, BG) as b:
                    attention1_sequence(b)
                attention1_sequence(BG)
                attention1_sequence(BG + 1, route=True)
                with dve.Fori(BG + 2, B - 1) as b:
                    attention1_sequence(b)
                attention1_sequence(B - 1, ahead=False)
                for s in range(4):
                    if s % 2 == 0:
                        normalise_gates(B - 1, 2 + s // 2)
                    else:
                        add_projected(B - 1, 2 + s // 2)

            def bias1(e, mg, t):
                dve.wait_ge(up_psum, mg + 1)
                dve.wait_ge(hid_ready, mg - 1)
                nc.vector.tensor_tensor(act_out[:, t % 2, :], bG[t % 2][:, :],
                                        b1[:, bass.ds(e, 1), :].rearrange("p a n -> p (a n)"), ALU.add).then_inc(bias_added, 1)

            def evac_y1(e, m, mg, t):
                dve.wait_ge(y_psum, mg + 1)
                nc.vector.tensor_tensor(ysb[:, bass.ds(m, 1), :].rearrange("p a c -> p (a c)"), bY[t % 2][:, 0:C],
                                        b2[:, bass.ds(e, 1), :].rearrange("p a n -> p (a n)"), ALU.add).then_inc(y_ready, 1)

            def experts1(g):
                m0, nch = tile0(1, g), NT[1] // CH
                dve.wait_ge(y_stored, 16 * chunk0(1, g))
                dve.wait_ge(ffn1_loaded, 16 * (2 + 2 * E1))

                def chunk(c, first=False, choose=False, place=False):
                    e = experts_of(mybir.EngineType.DVE, 1, g, c, first)
                    for t in range(CH):
                        m = c * CH + t
                        if first and g == 0:
                            normalise_end(1, t)
                        bias1(e[t], m + m0, t)
                        if first and g == 0 and t == 3:
                            evac_logits1(B - 1, bLast)
                        if not (first and t < 2):
                            evac_y1(e[t - 2], m - 2, m + m0 - 2, t)
                        if choose and t < 3:
                            (choose_first, choose_second, announce)[t](1, 1)
                        if place:
                            (place_experts, place_tokens, place_slots, place_tiles)[t](1, 1)
                    return e

                chunk(0, first=True)
                if g == 0:
                    chunk(1, choose=True)
                    chunk(2, place=True)
                with dve.Fori(1 if g else 3, nch - 1) as c:
                    chunk(c)
                e = chunk(nch - 1)
                for t in (2, 3):
                    m = nch * CH - CH + t
                    evac_y1(e[t], m, m + m0, t)

            attention0()
            experts0(0)
            experts0(1)
            attention1()
            for g in range(GROUPS):
                experts1(g)
            combine(1, 0, 0, range(TG))
            weigh(1, 1)
            for q in range(BG):
                dve.wait_ge(fetched_last[q], 16 * K1 * Q)
                combine(1, 1, 0, range(q * Q, (q + 1) * Q))

        @block.tensor
        def _(pe):
            pe.wait_ge(const_loaded, 16)
            pe.wait_ge(attw_loaded, 16 * 4)

            def t1(m):
                pe.wait_ge(xn_ready, m + 1)
                for i in range(Q):
                    ins = nc.tensor.transpose(bX[:, i * P:(i + 1) * P], xn[:, i, :], ident)
                ins.then_inc(xnT_psum, 1)

            def project_q(b):
                pe.wait_ge(xnT_ready, b + 1)
                after(pe, v_ready, 1 + b)
                nc.tensor.matmul(bQV[:, :], qkvw[:, 0, :], xnT[:, :], start=True, stop=True).then_inc(q_psum, 1)

            def project_k(b):
                nc.tensor.matmul(bK[:, :], qkvw[:, 1, :], xnT[:, :], start=True, stop=True).then_inc(k_psum, 1)

            def project_v(b):
                pe.wait_ge(q_ready, b + 1)
                for i in range(Q):
                    ins = nc.tensor.matmul(bQV[:, i * P:(i + 1) * P], xnT[:, i * P:(i + 1) * P], qkvw[:, 2, :],
                                           start=True, stop=True)
                ins.then_inc(v_psum, 1)

            def scores(b, i):
                if i == 0:
                    pe.wait_ge(k_ready, 1 + b + 1)
                after(pe, exp_done, 1 + Q * b + i - 1)
                nc.tensor.matmul(bS[i % 2][:, i * P:(i + 1) * P], ident_bf, causal_bf, start=True, stop=False,
                                 skip_group_check=True)
                nc.tensor.matmul(bS[i % 2][:, 0:(i + 1) * P], qT[:, i * P:(i + 1) * P], kT[:, 0:(i + 1) * P],
                                 start=False, stop=True, skip_group_check=True).then_inc(s_psum, 1)

            def pt(b, i):
                pe.wait_ge(exp_done, 1 + Q * b + i + 1)
                after(pe, pt_ready, 1 + Q * b + i)
                for j in range(i + 1):
                    ins = nc.tensor.transpose(bPT[:, j * P:(j + 1) * P], prob[:, i % 2, j * P:(j + 1) * P], ident)
                ins.then_inc(pt_psum, 1)

            def pv(b, i):
                pe.wait_ge(pt_ready, 1 + Q * b + i + 1)
                if i == 0:
                    pe.wait_ge(v_ready, 1 + b + 1)
                after(pe, attn_added, 1 + Q * b + i - 1)
                for j in range(i + 1):
                    ins = nc.tensor.matmul(bO[i % 2][:, 0:C], probT[:, i % 2, j * P:(j + 1) * P],
                                           v[:, j * C:(j + 1) * C],
                                           start=(j == 0), stop=(j == i))
                ins.then_inc(o_psum, 1)

            def t2(m, bk=bX):
                pe.wait_ge(rows_ready, m + 1)
                for i in range(Q):
                    ins = nc.tensor.transpose(bk[:, i * P:(i + 1) * P], xn2[:, i, :], ident)
                ins.then_inc(x2T_psum, 1)

            def route_logits(m, router, E, bk=bX):
                pe.wait_ge(x2T_ready, m + 1)
                for i in range(Q):
                    ins = nc.tensor.matmul(bk[:, i * E:(i + 1) * E], x2T[:, i * P:(i + 1) * P], router[:, :],
                                           start=True, stop=True)
                ins.then_inc(lg_psum, 1)

            def sequence0(b, last=True, ahead=True, route=False):
                scores(b, 0)
                scores(b, 1)
                pt(b, 0)
                scores(b, 2)
                if route:
                    rank(0, 0)
                pt(b, 1)
                pv(b, 0)
                scores(b, 3)
                pt(b, 2)
                pv(b, 1)
                if ahead:
                    after(pe, lg_ready, 1 + b - 1)
                    t1(b + 1)
                pt(b, 3)
                pv(b, 2)
                if ahead:
                    project_q(b + 1)
                pv(b, 3)
                if last:
                    if ahead:
                        pe.wait_ge(xnT_ready, b + 2)
                    else:
                        pe.wait_ge(lg_ready, 1 + b - 1)
                    t2(b - 1)
                if route:
                    pe.wait_ge(rank_read, 1)
                if ahead:
                    project_k(b + 1)
                    project_v(b + 1)
                if last:
                    route_logits(b - 1, wr, E0)

            def attention0():
                t1(0)
                project_q(0)
                project_k(0)
                project_v(0)
                pe.wait_ge(const_cast, 5)
                sequence0(0, last=False)
                with pe.Fori(1, BG) as b:
                    sequence0(b)
                sequence0(BG)
                sequence0(BG + 1, route=True)
                with pe.Fori(BG + 2, B - 1) as b:
                    sequence0(b)
                sequence0(B - 1, ahead=False)

            def rank(n, g):
                E = (E0, E1)[n]
                pe.wait_ge(chosen, GROUPS * n + g + 1)
                nc.tensor.matmul(bRank[n][g][:, 0:TG * E], before_bf, rt_selbf[:, :, 0:E], start=True, stop=False,
                                 skip_group_check=True)
                for t in range(TG):
                    ins = nc.tensor.matmul(bRank[n][g][:, (t + 1) * E:(TG + 1) * E], ones_bf,
                                           rt_selbf[:, t, 0:E].unsqueeze(1).to_broadcast([P, TG - t, E]),
                                           start=False, stop=(t == TG - 1), skip_group_check=True)
                ins.then_inc(rank_psum, 1)

            def xs_transpose(c):
                pe.wait_ge(xs_loaded, 16 * c + 16)
                after(pe, xsT_ready, c)
                for t in range(CH):
                    ins = nc.tensor.transpose(bX[:, t * P:(t + 1) * P], xs[:, t, :], ident)
                ins.then_inc(xs_psum, 1)

            def up0(e, mg, t, chunk):
                if t == 0:
                    pe.wait_ge(xsT_ready, chunk + 1)
                after(pe, hid_ready, mg - 1)
                for bk, half in ((bG, 0), (bU, 1)):
                    ins = nc.tensor.matmul(bk[t % 2][:, 0:I0], xsT[:, t * P:(t + 1) * P],
                                           wgu[:, bass.ds(e, 1), half * I0:(half + 1) * I0].rearrange("p a n -> p (a n)"),
                                           start=True, stop=True)
                ins.then_inc(up_psum, 1)

            def turn0(mg, t):
                pe.wait_ge(hid_ready, mg + 1)
                after(pe, hidT_ready, mg)
                for j in range(HC0):
                    w = min(P, I0 - j * P)
                    ins = nc.tensor.transpose(bHT[0:w, j * P:(j + 1) * P], hid[:, t % 2, j * P:j * P + w], ident)
                ins.then_inc(hidT_psum, 1)

            def down0(e, mg, t):
                pe.wait_ge(hidT_ready, mg + 1)
                after(pe, y_ready, mg - 1)
                for j in range(HC0):
                    w = min(P, I0 - j * P)
                    ins = nc.tensor.matmul(bY[t % 2][:, 0:C], hidT[0:w, t % 2, j * P:(j + 1) * P],
                                           wd[0:w, bass.ds(e, 1), j, :].rearrange("p a n -> p (a n)"),
                                           start=(j == 0), stop=(j == HC0 - 1))
                ins.then_inc(y_psum, 1)

            def experts0(g):
                m0, c0, nch = tile0(0, g), chunk0(0, g), NT[0] // CH
                pe.wait_ge(ffn0_loaded, 16 * 3 * E0)
                pe.wait_ge(lg_ready, 1 + B - 1)
                pe.wait_ge(routed, g + 1)

                def chunk(c, first=False, last=False, route=False):
                    e = experts_of(mybir.EngineType.PE, 0, g, c, first)
                    for t in range(CH):
                        m = c * CH + t
                        up0(e[t], m + m0, t, c + c0)
                        if first and g == 0 and t == 3:
                            route_logits(B - 1, wr, E0, bLast)
                        if t == 3 and route:
                            pe.wait_ge(rank_read, 2)
                        if t == 3 and not (last and g == GROUPS - 1):
                            xs_transpose(c + c0 + 1)
                        if not (first and t < 1):
                            turn0(m + m0 - 1, t - 1)
                        if not (first and t < 2):
                            if first and g == 0 and t == 3:
                                pe.wait_ge(lg_ready, 1 + B - 1 + 1)
                            down0(e[t - 2], m + m0 - 2, t)
                        if first and g == 0 and t == 2:
                            t2(B - 1, bLast)
                        if t == 0 and route:
                            pe.wait_ge(xsT_ready, c + c0 + 1)
                            rank(0, 1)
                        if t == 3 and last and g == GROUPS - 1:
                            pe.wait_ge(xsT_ready, c + c0 + 1)
                            t1(B)
                    return e

                if g == 0:
                    xs_transpose(c0)
                chunk(0, first=True)
                if g == 0:
                    chunk(1)
                    chunk(2, route=True)
                with pe.Fori(1 if g else 3, nch - 1) as c:
                    chunk(c)
                e = chunk(nch - 1, last=True)
                end = nch * CH
                turn0(end - 1 + m0, 3)
                if g == GROUPS - 1:
                    pe.wait_ge(att1_loaded, 16 * 7)
                    keys(0)
                down0(e[2], end - 2 + m0, 2)
                down0(e[3], end - 1 + m0, 3)

            def keys(b):
                pe.wait_ge(xkT_ready, b + 1)
                pe.wait_ge(xnT_ready, B + b + 1)
                for n in range(2):
                    ins = nc.tensor.matmul(bX[:, n * Q * KC:(n + 1) * Q * KC], wk1[:, n, :], xkT, start=True, stop=True)
                ins.then_inc(key_psum, 1)

            def values(b):
                pe.wait_ge(key_turned, b + 1)
                for n in range(2):
                    ins = nc.tensor.matmul(bX[:, n * C:(n + 1) * C], xkT[:, n * P:(n + 1) * P], wv1[:, :], start=True, stop=True)
                ins.then_inc(val_psum, 1)

            def produce(b, u):
                n = UNITS * b + u
                bk = bU1[u % 3]
                after(pe, unit_sub, 1 + n - 2)
                if u < 4:
                    pe.wait_ge(kT1_ready, b + 1)
                    nc.tensor.matmul(bk[:, :].rearrange("p (s k) -> p s k", s=8), ident_bf,
                                     latmask_bf.unsqueeze(1).to_broadcast([P, 8, KC]), start=True, stop=False,
                                     skip_group_check=True)
                    for h in range(2):
                        ins = nc.tensor.matmul(bk[:, h * Q * KC:(h + 1) * Q * KC],
                                               latbd[:, 4 * u + 2 * h:4 * u + 2 * h + 2, :].rearrange("p h l -> p (h l)"),
                                               kT1[:, :], start=False, stop=True, skip_group_check=True)
                else:
                    t, half = (u - 4) // 2, u % 2
                    if u == 4:
                        pe.wait_ge(xT1_ready, 16 * (b + 1))
                    ins = nc.tensor.matmul(bk[:, :], xT1[:, t * P:(t + 1) * P], wg1[:, half * 512:(half + 1) * 512],
                                           start=True, stop=True)
                ins.then_inc(unit_psum, 1)

            def turn_unit(b, u):
                n = UNITS * b + u
                pe.wait_ge(unit_exp, n + 1)
                after(pe, exT_ready, 1 + n - 1)
                for j in range(4):
                    ins = nc.tensor.transpose(bT1[u % 2][:, j * P:(j + 1) * P], ex[:, u % 3, j * P:(j + 1) * P], ident)
                ins.then_inc(exT_psum, 1)

            def use_unit(b, u):
                n = UNITS * b + u
                pe.wait_ge(exT_ready, 1 + n + 1)
                if u < 4:
                    if u >= 2:
                        pe.wait_ge(att_step, 3 * (Q * b + u - 2) + 2)
                    elif u == 0:
                        after(pe, mixed_ready, 1 + Q * b)
                    else:
                        after(pe, proj_added, 1 + Q * b)
                    if u == 0:
                        pe.wait_ge(val_ready, 2 * b + 2)
                    for j in range(4):
                        ins = nc.tensor.matmul(bO1[u % 2][:, j * 2 * VW:(j + 1) * 2 * VW], exT[:, u % 2, j * P:(j + 1) * P],
                                               vbd[:, j % 2, 2 * u + j // 2, :, :].rearrange("p n v -> p (n v)"),
                                               start=True, stop=True)
                else:
                    t = (u - 4) // 2
                    if t == 0:
                        pe.wait_ge(att_step, 3 * (Q * b + Q))
                    else:
                        pe.wait_ge(mixed_ready, 1 + Q * b + t)
                    for j in range(4):
                        h = 4 * (u % 2) + j
                        ins = nc.tensor.matmul(bO1[0][:, h * GW:(h + 1) * GW], exT[:, u % 2, j * P:(j + 1) * P],
                                               attbd[:, h, :], start=True, stop=True)
                ins.then_inc(unit_used, 1)

            def turn_mixed(b, t):
                pe.wait_ge(mixed_ready, 1 + Q * b + t + 1)
                if t == 0:
                    pe.wait_ge(att_step, 3 * (Q * b + Q))
                else:
                    pe.wait_ge(proj_added, 1 + Q * b + t)
                nc.tensor.transpose(bO1[1][:, 0:P], mixed[:, :, :, :].rearrange("p h k d -> p (h k d)"),
                                    ident).then_inc(mixedT_psum, 1)

            def project(b, t):
                pe.wait_ge(mixedT_ready, Q * b + t + 1)
                nc.tensor.matmul(bO1[1][:, 0:C], mixedT[:, :], wp1[:, :], start=True, stop=True).then_inc(proj_psum, 1)

            def attention1_sequence(b, last=True, ahead=True, route=False):
                for s in range(UNITS):
                    produce(b, s)
                    if s in (1, 3) and last:
                        turn_mixed(b - 1, 2 + s // 2)
                    if s in (9, 11):
                        turn_mixed(b, s // 2 - 4)
                    if last or s >= 2:
                        turn_unit(*unit(b, s - 2))
                    if s == 10 and ahead:
                        values(b + 1)
                    if s == 11 and last:
                        route_logits(B + b - 1, wr1, E1)
                    if last or s >= 3:
                        use_unit(*unit(b, s - 3))
                    if s in (1, 3) and last:
                        project(b - 1, 2 + s // 2)
                    if s in (9, 11):
                        project(b, s // 2 - 4)
                    if s == 3 and route:
                        pe.wait_ge(lg_ready, 1 + B + b - 1)
                        rank(1, 0)
                    if s == 8 and route:
                        pe.wait_ge(rank_read, GROUPS + 1)
                    if s == 8 and ahead:
                        pe.wait_ge(val_ready, 2 * b + 2)
                        if last:
                            pe.wait_ge(lg_ready, 1 + B + b - 1)
                        t1(B + b + 1)
                    if s == 9 and ahead:
                        keys(b + 1)
                    if s == 10 and last:
                        if ahead:
                            pe.wait_ge(val_ready, 2 * b + 4)
                        else:
                            pe.wait_ge(lg_ready, 1 + B + b - 1)
                        t2(B + b - 1)

            def attention1():
                pe.wait_ge(latbd_ready, 1)
                pe.wait_ge(att1_preset, 4)
                values(0)
                attention1_sequence(0, last=False)
                with pe.Fori(1, BG) as b:
                    attention1_sequence(b)
                attention1_sequence(BG)
                attention1_sequence(BG + 1, route=True)
                with pe.Fori(BG + 2, B - 1) as b:
                    attention1_sequence(b)
                attention1_sequence(B - 1, ahead=False)
                for s in range(4):
                    if s % 2:
                        turn_mixed(B - 1, 2 + s // 2)
                    if s < 2:
                        turn_unit(B - 1, UNITS - 2 + s)
                    if s < 3:
                        use_unit(B - 1, UNITS - 3 + s)
                    if s % 2:
                        project(B - 1, 2 + s // 2)

            def up1(e, mg, t, chunk):
                if t == 0:
                    pe.wait_ge(xsT_ready, chunk + 1)
                after(pe, bias_added, mg - tile0(1, 0) - 1)
                nc.tensor.matmul(bG[t % 2][:, :], xsT[:, t * P:(t + 1) * P],
                                 w1[:, bass.ds(e, 1), :].rearrange("p a n -> p (a n)"),
                                 start=True, stop=True).then_inc(up_psum, 1)

            def turn1(mg, t):
                pe.wait_ge(hid_ready, mg + 1)
                pe.wait_ge(hidT_ready, mg)
                for j in range(HC1):
                    ins = nc.tensor.transpose(bHT[:, j * P:(j + 1) * P], hid[:, t % 2, j * P:(j + 1) * P], ident)
                ins.then_inc(hidT_psum, 1)

            def down1(e, mg, t):
                pe.wait_ge(hidT_ready, mg + 1)
                pe.wait_ge(y_ready, mg - 1)
                for j in range(HC1):
                    ins = nc.tensor.matmul(bY[t % 2][:, 0:C], hidT[:, t % 2, j * P:(j + 1) * P],
                                           w2[:, bass.ds(e, 1), j, :].rearrange("p a n -> p (a n)"),
                                           start=(j == 0), stop=(j == HC1 - 1))
                ins.then_inc(y_psum, 1)

            def experts1(g):
                m0, c0, nch = tile0(1, g), chunk0(1, g), NT[1] // CH
                pe.wait_ge(ffn1_loaded, 16 * (2 + 2 * E1))
                pe.wait_ge(lg_ready, 1 + 2 * B - 1)
                pe.wait_ge(routed, GROUPS + g + 1)

                def chunk(c, first=False, last=False, route=False):
                    e = experts_of(mybir.EngineType.PE, 1, g, c, first)
                    for t in range(CH):
                        m = c * CH + t
                        up1(e[t], m + m0, t, c + c0)
                        if first and g == 0 and t == 3:
                            route_logits(2 * B - 1, wr1, E1, bLast)
                        if t == 3 and route:
                            pe.wait_ge(rank_read, GROUPS + 2)
                        if t == 3 and not last:
                            xs_transpose(c + c0 + 1)
                        if not (first and t < 1):
                            turn1(m + m0 - 1, t - 1)
                        if not (first and t < 2):
                            if first and g == 0 and t == 3:
                                pe.wait_ge(lg_ready, 1 + 2 * B - 1 + 1)
                            down1(e[t - 2], m + m0 - 2, t)
                        if first and g == 0 and t == 2:
                            t2(2 * B - 1, bLast)
                        if t == 0 and route:
                            pe.wait_ge(xsT_ready, c + c0 + 1)
                            rank(1, 1)
                    return e

                xs_transpose(c0)
                chunk(0, first=True)
                if g == 0:
                    chunk(1)
                    chunk(2, route=True)
                with pe.Fori(1 if g else 3, nch - 1) as c:
                    chunk(c)
                e = chunk(nch - 1, last=True)
                end = nch * CH
                turn1(end - 1 + m0, 3)
                down1(e[2], end - 2 + m0, 2)
                down1(e[3], end - 1 + m0, 3)

            attention0()
            for g in range(GROUPS):
                experts0(g)
            attention1()
            for g in range(GROUPS):
                experts1(g)


def _consts():
    import numpy as np
    c = np.zeros((P, NCONST), np.float32)
    p = np.arange(P)

    def put(name, value):
        c[:, COLS[name][0]:COLS[name][1]] = value

    put("ident", np.eye(P))
    inv = (1.0 / 10000.0 ** (np.arange(0, D, 2, dtype=np.float32) / D)).astype(np.float32)
    pos = (np.arange(Q)[:, None] * P + np.arange(KC)[None, :]).reshape(-1).astype(np.float32)
    ang = (pos[None, :] * inv[(p % D) // 2][:, None]).astype(np.float32)
    put("cos", np.cos(ang))
    put("sin", np.sin(ang) * np.where(p % 2 == 0, -1.0, 1.0)[:, None])
    put("headmask", (p[:, None] // D) == np.arange(H)[None, :])
    put("iota_e", np.arange(16)[None, :])
    put("iota_j", np.arange(ST)[None, :])
    e = np.arange(E0)
    put("below", (e[None, :] < e[:, None]).reshape(1, -1))
    put("ones", 1.0)
    put("before", p[:, None] < p[None, :])
    put("causal", np.where(p[None, :] <= p[:, None], 0.0, NEG))
    put("latmask", np.where(np.arange(KC)[None, :] <= (p % L)[:, None], 0.0, NEG))
    put("pairones", (p[:, None] // L) == np.arange(2)[None, :])
    return c


def kernel(**inputs):
    import numpy as np
    import concourse.bacc as bacc
    from concourse.bass_utils import run_bass_kernel_spmd

    i = {n: np.asarray(v) for n, v in inputs.items()}
    swap = np.arange(C) ^ 1
    arrays = {
        "const": _consts(),
        "L0_attn_x": i["L0_attn_x"],
        "qkvw": np.stack([i["L0_attn_Qw"], i["L0_attn_Kw"], i["L0_attn_Vw"]], axis=1),
        "qkb": np.stack([i["L0_attn_Qb"], i["L0_attn_Kb"]], axis=1),
        "L0_attn_Vb": i["L0_attn_Vb"],
        "L0_ffn_Wr": i["L0_ffn_Wr"],
        "wk1": np.stack([i["L1_attn_W_k"].T, i["L1_attn_W_k"].T[:, swap]], axis=1),
        "wv1": i["L1_attn_W_v"].T,
        "wg1": i["L1_attn_W_g"].T,
        "wp1": i["L1_attn_W_p"].T,
        "lat": i["L1_attn_latent_queries"][0].transpose(1, 2, 0).reshape(C, L),
        "L1_ffn_Wg": i["L1_ffn_Wg"],
        "L1_ffn_bg": i["L1_ffn_bg"],
        "w1": i["L1_ffn_W1"].transpose(1, 0, 2),
        "w2": i["L1_ffn_W2"].reshape(E1, HC1, P, C).transpose(2, 0, 1, 3),
        "L1_ffn_b1": i["L1_ffn_b1"],
        "L1_ffn_b2": i["L1_ffn_b2"],
        "wgu": np.concatenate([i["L0_ffn_Wg"], i["L0_ffn_Wu"]], axis=2).transpose(1, 0, 2),
        "wd_a": i["L0_ffn_Wd"][:, :2 * P].reshape(E0, 2, P, C).transpose(2, 0, 1, 3),
        "wd_b": i["L0_ffn_Wd"][:, 2 * P:].transpose(1, 0, 2),
    }
    arrays = {n: np.ascontiguousarray(v) for n, v in arrays.items()}
    nc = bacc.Bacc("TRN2", target_bir_lowering=False, num_devices=1)
    a = {n: nc.dram_tensor("in_" + n, v.shape, mybir.dt.from_np(v.dtype), kind="ExternalInput").ap()
         for n, v in arrays.items()}
    out = nc.dram_tensor("out", (B, T, C), F32, kind="ExternalOutput").ap()
    build(nc, a, out)
    got = run_bass_kernel_spmd(nc, [{"in_" + n: v for n, v in arrays.items()}], core_ids=[0])
    return got.results[0]["out"]
```
